# Optimizing a Trainium2 kernel written in Bass

```python
import numpy as np
import jax
import jax.numpy as jnp

def _softmax(x, axis=-1):
    return jax.nn.softmax(x, axis=axis)

def _gelu(x):
    return jax.nn.gelu(x, approximate=True)

def _silu(x):
    return jax.nn.silu(x)

def _sigmoid(x):
    return jax.nn.sigmoid(x)

def _layernorm(x, axis=-1, eps=1e-05):
    m = jnp.mean(x, axis=axis, keepdims=True)
    v = jnp.var(x, axis=axis, keepdims=True)
    return (x - m) / jnp.sqrt(v + eps)

def _scatter_add(tgt, idx, src, axis=0):
    return tgt.at[idx].add(src)

def _segment_sum(src, seg, n):
    return jax.ops.segment_sum(src, seg, n)
kernel_name = 'mk_flamingo_gated_d1_seqx_r4_fc8718'

def setup_inputs(seed: int=0):
    np.random.seed(seed)
    _w = jnp.asarray

    def _rec_inputs():
        import jax
        import jax.numpy as jnp
        _rk = jax.random.key(seed)
        x = 0.5 + 0.2887 * jax.random.normal(jax.random.fold_in(_rk, 1), (4, 512, 512), jnp.float32)
        _lenS = 512 - jax.random.randint(jax.random.fold_in(_rk, 7), (4,), 0, max(1, 512 // 4) + 1, jnp.int32)
        _lenS2 = 512 - jax.random.randint(jax.random.fold_in(_rk, 8), (4,), 0, max(1, 512 // 4) + 1, jnp.int32)
        _ctx_512P = jax.random.normal(jax.random.fold_in(_rk, 11), (4, 16, 128), jnp.float32)
        _ctx_512c = jax.random.dirichlet(jax.random.fold_in(_rk, 511), 0.3 * jnp.ones((16,), jnp.float32), (4, 512))
        _ctx_512t = jnp.einsum('bsk,bkd->bsd', _ctx_512c, _ctx_512P)
        _ctx_512t = _ctx_512t * jax.lax.rsqrt(jnp.mean(jnp.square(_ctx_512t)) + 1e-12) * 0.953939
        ctx_512 = -0.000392918 + 0.999932 * (_ctx_512t + 0.3 * jax.random.normal(jax.random.fold_in(_rk, 611), (4, 512, 128), jnp.float32))
        _g = jax.random.normal(jax.random.fold_in(_rk, 9001), (2, 1), jnp.float32)
        _g = jnp.sign(_g) * jnp.maximum(jnp.abs(_g), 1.0) + (_g == 0) * 1.0
        g_xattn = _g[0]
        g_ffn = _g[1]
        return (x, ctx_512, g_xattn, g_ffn)
    x, ctx_512, g_xattn, g_ffn = _rec_inputs()

    def _L0_xattn_setup():
        import jax, jax.numpy as jnp
        import numpy as np
        B, N, D = (16, 512, 128)
        H = 4
        TOP_K_RATIO = 0.3
        key = jax.random.key(seed)
        k1, k2, k3, k4 = jax.random.split(key, 4)
        h = jax.random.normal(k1, (B, N, D), dtype=jnp.float32)
        adj_raw = jax.random.uniform(k2, (B, N, N), dtype=jnp.float32)
        lim = 1.0 / np.sqrt(D)
        Wq = jax.random.uniform(k3, (D, D), minval=-lim, maxval=lim, dtype=jnp.float32)
        Wk = jax.random.uniform(k4, (D, D), minval=-lim, maxval=lim, dtype=jnp.float32)
        gamma_raw = jnp.float32(-0.85)
        return {'h': h, 'adj_raw': adj_raw, 'Wq': Wq, 'Wk': Wk, 'gamma_raw': gamma_raw}
    _L0_xattn_all = _L0_xattn_setup()
    _L0_xattn_in = {k: v for k, v in _L0_xattn_all.items() if k in ('Wq', 'Wk', 'gamma_raw')}
    del _L0_xattn_all

    def _L0_ffn_setup():
        import jax, jax.numpy as jnp
        import numpy as np
        TOPK = 2
        N_EXPERTS = 8
        ROUTE_SCALE = 1.0
        key = jax.random.key(seed)
        ks = jax.random.split(key, 7)
        B, T, C = (4, 512, 512)
        H = 352
        HS = 704
        E = N_EXPERTS
        s = 0.02
        return {'x': jax.random.normal(ks[0], (B, T, C), jnp.float32), 'gate_w': jax.random.normal(ks[1], (E, C), jnp.float32) * s, 'gate_bias': jnp.zeros((E,), jnp.float32), 'shared_gw': jax.random.normal(ks[2], (2 * HS, C), jnp.float32) * s, 'shared_dw': jax.random.normal(ks[3], (C, HS), jnp.float32) * s, 'up_w': jax.random.normal(ks[4], (E, 2 * H, C), jnp.float32) * s, 'down_w': jax.random.normal(ks[5], (E, C, H), jnp.float32) * s}
    _L0_ffn_all = _L0_ffn_setup()
    _L0_ffn_in = {k: v for k, v in _L0_ffn_all.items() if k in ('gate_w', 'gate_bias', 'shared_gw', 'shared_dw', 'up_w', 'down_w')}
    del _L0_ffn_all
    return {'x': x, 'ctx_512': ctx_512, 'g_xattn': g_xattn, 'g_ffn': g_ffn, 'L0_xattn_Wq': _L0_xattn_in['Wq'], 'L0_xattn_Wk': _L0_xattn_in['Wk'], 'L0_xattn_gamma_raw': _L0_xattn_in['gamma_raw'], 'L0_ffn_gate_w': _L0_ffn_in['gate_w'], 'L0_ffn_gate_bias': _L0_ffn_in['gate_bias'], 'L0_ffn_shared_gw': _L0_ffn_in['shared_gw'], 'L0_ffn_shared_dw': _L0_ffn_in['shared_dw'], 'L0_ffn_up_w': _L0_ffn_in['up_w'], 'L0_ffn_down_w': _L0_ffn_in['down_w']}

def reference(x, ctx_512, g_xattn, g_ffn, L0_xattn_Wq, L0_xattn_Wk, L0_xattn_gamma_raw, L0_ffn_gate_w, L0_ffn_gate_bias, L0_ffn_shared_gw, L0_ffn_shared_dw, L0_ffn_up_w, L0_ffn_down_w):
    import jax
    import jax.numpy as jnp

    def _L0_xattn_ref(h, adj_raw, Wq, Wk, gamma_raw):
        import jax, jax.numpy as jnp
        import numpy as np
        B, N, D = (16, 512, 128)
        H = 4
        TOP_K_RATIO = 0.3
        b, n, dm = h.shape
        d = dm // H
        Q = (h @ Wq.T).reshape(b, n, H, d).transpose(0, 2, 1, 3)
        K = (h @ Wk.T).reshape(b, n, H, d).transpose(0, 2, 1, 3)
        sim = jnp.einsum('bhnd,bhmd->bnm', Q, K) / (jnp.sqrt(jnp.float32(d)) * H)
        k = max(1, int(n * TOP_K_RATIO))
        topk_vals = jax.lax.top_k(sim, k)[0]
        threshold = topk_vals[:, :, -1:]
        sparse_mask = (sim >= threshold).astype(sim.dtype)
        A_learned = jax.nn.sigmoid(sim) * sparse_mask
        A_learned = (A_learned + jnp.swapaxes(A_learned, -1, -2)) * 0.5
        gamma = jax.nn.sigmoid(gamma_raw)
        return (1.0 - gamma) * adj_raw + gamma * A_learned

    def _L0_ffn_ref(x, gate_w, gate_bias, shared_gw, shared_dw, up_w, down_w):
        import jax, jax.numpy as jnp
        import numpy as np
        TOPK = 2
        N_EXPERTS = 8
        ROUTE_SCALE = 1.0
        B, T, C = x.shape
        xf = x.reshape(-1, C)
        yg = xf @ shared_gw.T
        y, g = jnp.split(yg, 2, axis=-1)
        shared = jax.nn.silu(g) * y @ shared_dw.T
        scores = jax.nn.sigmoid(xf @ gate_w.T)
        _, topk_idx = jax.lax.top_k(scores + gate_bias, TOPK)
        w = jnp.take_along_axis(scores, topk_idx, axis=-1)
        w = w / jnp.sum(w, axis=-1, keepdims=True) * ROUTE_SCALE
        out = jnp.zeros_like(xf)
        for e in range(N_EXPERTS):
            we = jnp.sum(jnp.where(topk_idx == e, w, 0.0), axis=-1)
            gu = xf @ up_w[e].T
            g_e, u_e = jnp.split(gu, 2, axis=-1)
            h = jax.nn.silu(g_e) * u_e
            out = out + h @ down_w[e].T * we[:, None]
        return (shared + out).reshape(B, T, C)
    x = x + jnp.tanh(g_xattn[0]) * _L0_xattn_ref(ctx_512, _layernorm(x, axis=-1), L0_xattn_Wq, L0_xattn_Wk, L0_xattn_gamma_raw)
    x = x + jnp.tanh(g_ffn[0]) * _L0_ffn_ref(_layernorm(x, axis=-1), L0_ffn_gate_w, L0_ffn_gate_bias, L0_ffn_shared_gw, L0_ffn_shared_dw, L0_ffn_up_w, L0_ffn_down_w)
    return x

_drawn_inputs = setup_inputs


def setup_inputs(seed=0):
    import zlib

    import numpy as np

    out = dict(_drawn_inputs(seed))
    spreads = {'L0_ffn_gate_bias': (0.0, 0.924)}
    factors = {'L0_ffn_gate_w': 21.315}
    for name, (base, spread) in spreads.items():
        noise = np.random.default_rng([zlib.crc32(name.encode()), seed]).standard_normal(out[name].shape)
        drawn = base * np.exp(spread * noise) if base else spread * noise
        out[name] = jnp.asarray(drawn.astype(out[name].dtype))
    for name, factor in factors.items():
        out[name] = (out[name] * factor).astype(out[name].dtype)
    return out
```

```python
import numpy as np

BATCHES, SEQ, C, D = 4, 512, 512, 128
P = 128
TOKENS = BATCHES * SEQ
TPB = SEQ // P
TILES = TOKENS // P
KC = C // P
EXPERTS, TOPK = 8, 2
H = 352
HALVES = 2
HP = 384
JC = HP // P
KEEP = int(SEQ * 0.3)
UP_W = KC * 2 * H
ITEM_W = UP_W + JC * C
ITEMS = HALVES + EXPERTS
EARLY = 7
CHUNKS = 4
CHUNK_W = ITEM_W // CHUNKS
SLOT_TILES = TOKENS * TOPK // P + EXPERTS - 1
SLOT_COLS = SLOT_TILES + 2
PAD_ROWS = P
ROUNDS = 5
X_SCALE, W_SCALE, H_SCALE = 16.0, 256.0, 16.0
UP_UNSCALE = 1.0 / (X_SCALE * W_SCALE)
DOWN_UNSCALE = 1.0 / (H_SCALE * W_SCALE)
SIM_SCALE = 1.0 / (float(np.sqrt(np.float32(D // 4))) * 4.0)
LN_EPS = 1e-5
BIG = 3.0e38
CREDIT = 32


def build(nc, x, ctx_t, wq_t, wk_t, gates, gate_wt, gate_bias, weights, out, xn_rows):
    import concourse.bass as bass
    from concourse import mybir
    from contextlib import ExitStack

    F32, F16, I32, U32 = mybir.dt.float32, mybir.dt.float16, mybir.dt.int32, mybir.dt.uint32
    ALU, ACT, AX = mybir.AluOpType, mybir.ActivationFunctionType, mybir.AxisListType
    ds = bass.ds

    x_tiles = x.rearrange("(g p) c -> p g c", p=P)
    out_tiles = out.rearrange("(g p) c -> p g c", p=P)
    xn_tiles = xn_rows.rearrange("(g p) c -> p g c", p=P)

    with ExitStack() as ctx:
        def sb(name, shape, dt=F32):
            return ctx.enter_context(nc.sbuf_tensor(name, shape, dt))

        def bank(name):
            return ctx.enter_context(nc.psum_tensor(name, [P, 512], F32))

        credited = []

        def sem(name, credit=True):
            s = ctx.enter_context(nc.semaphore(name))
            if credit:
                credited.append(s)
            return s

        w = sb("w", [P, ITEMS, 2, ITEM_W], F16)
        attn = w[:, EARLY:ITEMS, :, :].rearrange("p a b c -> p (a b c)").bitcast(F32)
        taken = [0]

        def attn_buf(words):
            taken[0] += words
            assert taken[0] <= (ITEMS - EARLY) * ITEM_W
            return attn[:, taken[0] - words:taken[0]]

        def attn_tiles():
            return attn_buf(TPB * SEQ).rearrange("p (i c) -> p i c", i=TPB)

        xb = attn_tiles()
        sim = attn_tiles()
        att = attn_tiles()
        xnr = attn_buf(TPB * C).bitcast(F16).rearrange("p (i c) -> p i c", i=TPB)
        ctx_b, q_t, k_t = attn_buf(SEQ), attn_buf(SEQ), attn_buf(SEQ)
        xn = attn_buf(2 * C).rearrange("p (i c) -> p i c", i=2)
        junk = attn_buf(TPB * SEQ // 2).bitcast(F16).rearrange("p (i c) -> p i c", i=TPB)
        masked = junk.rearrange("p i c -> p (i c)").bitcast(F32).rearrange("p (i c) -> p i c", i=2)

        stage = sb("stage", [P, 2, CHUNK_W])
        x_t = sb("x_t", [P, 2, 2 * KC, P], F16)
        sil = sb("sil", [P, 2, H])
        hid = sb("hid", [P, 2, HP])
        hid_t = sb("hid_t", [P, 2, 2, HP], F16)
        rows = sb("rows", [P, 2, C])
        xg = sb("xg", [P, 2, 2 * C], F16)
        ident, ident16 = sb("ident", [P, P]), sb("ident16", [P, P], F16)
        ones, tri = sb("ones", [P, P], F16), sb("tri", [P, P], F16)
        one1 = sb("one1", [P, 1])
        iota_col = sb("iota_col", [P, P])
        iota_p = sb("iota_p", [P, 1])
        iota_tile = iota_col[:, 0:SLOT_COLS]
        first = sb("first", [P, EXPERTS])
        gcol, cst = sb("gcol", [P, 3]), sb("cst", [P, 9])
        wq_s, wk_s = attn_buf(D), attn_buf(D)
        gw_f, gw = attn_buf(KC * EXPERTS).rearrange("p (k e) -> p k e", k=KC), sb("gw", [P, KC, 2, EXPERTS], F16)
        bias_b = sb("bias_b", [P, EXPERTS])
        half_pow = sb("half_pow", [P, 2, TPB])
        bn6 = attn_buf(3 * TPB * 6).rearrange("p (s i c) -> p s i c", s=3, i=TPB)
        mv = sb("mv", [P, 3, TPB, 2])
        pt = sb("pt", [P, 8, TPB])
        lo, hi, cur = (attn_buf(2 * TPB).rearrange("p (a i) -> p a i", a=2) for _ in range(3))
        below, above = sb("below", [P, TPB], U32), sb("above", [P, TPB], U32)
        tmp4 = sb("tmp4", [P, 6, TPB])
        top8, pick8 = (attn_buf(TPB * 8).rearrange("p (i c) -> p i c", i=TPB) for _ in range(2))
        thr = sb("thr", [P, TPB])
        missed, missed_i = sb("missed", [P, 1]), sb("missed_i", [1, 1], I32)
        lg = sb("lg", [P, TILES, 2, EXPERTS])
        r = [sb(f"r{n}", [P, TILES, EXPERTS], F16 if n == 2 else F32) for n in range(6)]

        rc = sb("rc", [P, 7, TILES])
        re8 = sb("re8", [P, 6, EXPERTS])
        ri8 = sb("ri8", [P, EXPERTS], I32)
        slot_i = sb("slot_i", [P, 3, TOPK, TILES], I32)
        slot_f = sb("slot_f", [P, 4, TOPK, TILES])
        idx = sb("idx", [P, SLOT_COLS], I32)
        idx_g, idx_s = sb("idx_g", [P, 2], I32), sb("idx_s", [P, 2], I32)
        w_slot = sb("w_slot", [P, SLOT_COLS])
        tile_e = sb("tile_e", [1, SLOT_COLS], I32)
        hot_col = xg.rearrange("p a c -> p (a c)")[:, 0:4 * 2 * P].bitcast(F32).rearrange("p (a c) -> p a c", a=4)
        hot_val = xg.rearrange("p a c -> p (a c)")[:, 4 * 2 * P:4 * 2 * P + 4 * 4 * SLOT_COLS].bitcast(F32)\
            .rearrange("p (a v c) -> p a v c", a=4, v=2)

        pa = [bank("pa0"), bank("pa1")]
        pg, pu = [bank("pg0"), bank("pg1")], [bank("pu0"), bank("pu1")]
        pt_bank = bank("pt_bank")
        py = bank("py")
        xt_ps = pt_bank[:, :].bitcast(F16).rearrange("p (a c) -> p a c", a=2 * KC)

        waits_apart = {}
        sp_tick, pool_tick = sem("sp_tick", False), sem("pool_tick", False)
        ready = sem("ready", False)
        const_ok = sem("const_ok", False)
        pool_c = sem("pool_c", False)
        small_ld = sem("small_ld", False)
        cst_act = sem("cst_act", False)
        cst_ok = sem("cst_ok", False)
        gw_ok = sem("gw_ok", False)
        gw_hi = sem("gw_hi", False)
        pad_st = sem("pad_st", False)
        w_ld = [sem("w_ld0"), sem("w_ld1")]
        w_hi, w_lo = sem("w_hi"), sem("w_lo")
        x_ld, ctx_ld = sem("x_ld"), sem("ctx_ld")
        qk_mm, qk_sb = sem("qk_mm"), sem("qk_sb")
        sim_mm, sim_sb, tanh_sb = sem("sim_mm"), sem("sim_sb"), sem("tanh_sb")
        stats_ok, guess_ok, base_ok, base_sb = sem("stats_ok"), sem("guess_ok"), sem("base_ok"), sem("base_sb")
        miss_ok, miss_mm = sem("miss_ok"), sem("miss_mm")
        a_made, at_mm, x1_made = sem("a_made"), sem("at_mm"), sem("x1_made")
        x1_st, ln_stats, ln_ok = sem("x1_st"), sem("ln_stats"), sem("ln_ok")
        xn_hi, xn_lo, xn_st = sem("xn_hi"), sem("xn_lo"), sem("xn_st")
        xt_mm, xt_sb = sem("xt_mm"), sem("xt_sb")
        up_mm, sil_sb, hid_sb = sem("up_mm"), sem("sil_sb"), sem("hid_sb")
        hid_mm, hhi_sb, hlo_sb = sem("hid_mm"), sem("hhi_sb"), sem("hlo_sb")
        down_mm, y_sb = sem("down_mm"), sem("y_sb")
        lg_sb = sem("lg_sb")
        x1_ld, sh_st = [sem("x1_ld0"), sem("x1_ld1")], sem("sh_st")
        pool_ch = sem("pool_ch", False)
        dve_ch = sem("dve_ch", False)
        fb_ch = sem("fb_ch", False)
        exp_ok, route_mm, route_ok = sem("exp_ok", False), sem("route_mm", False), sem("route_ok", False)
        z_ok = sem("z_ok", False)
        hot_ok, hot_mm, table_ok = sem("hot_ok", False), sem("hot_mm", False), sem("table_ok", False)
        g_ld = [sem("g_ld0", False), sem("g_ld1", False)]
        idx_c = sem("idx_c", False)
        y_add = sem("y_add", False)
        rows_free = sem("rows_free")

        def after(eng, s, n):
            eng.wait_ge(s, n + CREDIT)
            if waits_apart.get(eng) is not None:
                eng.sem_inc(waits_apart[eng], 1)

        class Order:

            def __init__(self, eng, s):
                self.eng, self.s, self.n = eng, s, 0

            def mark(self, ins):
                self.n += 1
                ins.then_inc(self.s, 1)

            def wait(self):
                self.eng.wait_ge(self.s, self.n)

            def then(self, ins):
                self.mark(ins)
                self.wait()

            def clear(self):
                if self.n:
                    self.wait()
                self.eng.sem_clear(self.s)
                self.n = 0

        block = ctx.enter_context(nc.Block())

        @block.sync
        def _(sp):
            waits_apart[sp] = sp_tick
            sp.wait_ge(ready, 1)

            def load_item(item):
                for n in range(CHUNKS):
                    after(sp, w_lo, item * CHUNKS + n - 1)
                    sp.dma_start(stage[:, n % 2, :], weights[ds(item, 1), :, n * CHUNK_W:(n + 1) * CHUNK_W]
                                 .rearrange("a p c -> (a p) c")).then_inc(w_ld[n % 2], 16)

            sp.dma_start(gcol[:], gates.rearrange("(a n) -> a n", a=1).partition_broadcast(P)
                         .rearrange("p a n -> p (a n)")).then_inc(small_ld, 16)
            sp.dma_start(wq_s, wq_t).then_inc(small_ld, 16)
            sp.dma_start(wk_s, wk_t).then_inc(small_ld, 16)
            sp.dma_start(gw_f, gate_wt).then_inc(small_ld, 16)
            sp.dma_start(bias_b[:], gate_bias.rearrange("(a n) -> a n", a=1).partition_broadcast(P)
                         .rearrange("p a n -> p (a n)")).then_inc(small_ld, 16)
            sp.wait_ge(const_ok, 1)
            sp.dma_start(out_tiles[:, TILES, :], rows[:, 0, :]).then_inc(pad_st, 16)
            sp.dma_start(xn_tiles[:, TILES, :], rows[:, 0, :].bitcast(F16)).then_inc(pad_st, 16)
            with sp.Fori(0, HALVES) as item:
                load_item(item)
            sp.wait_ge(pad_st, 32)
            with sp.Fori(0, BATCHES) as b:
                tile0 = sp.snap(b * TPB)
                after(sp, x1_st, b * TPB * 16)
                after(sp, xn_hi, b * TPB)
                after(sp, xn_lo, b * TPB)
                sp.dma_start(xb, x_tiles[:, ds(tile0, TPB), :]).then_inc(x_ld, 16)
                after(sp, qk_mm, b * 2)
                sp.dma_start(ctx_b, ctx_t[:, ds(b * SEQ, SEQ)]).then_inc(ctx_ld, 16)
                for i in range(TPB):
                    after(sp, x1_made, b * TPB + i + 1)
                    sp.dma_start(out_tiles[:, ds(tile0 + i, 1), :], xb[:, i:i + 1, :]).then_inc(x1_st, 16)
                for i in range(TPB):
                    after(sp, xn_lo, b * TPB + i + 1)
                    after(sp, xn_hi, b * TPB + i + 1)
                    sp.dma_start(xn_tiles[:, ds(tile0 + i, 1), :], xnr[:, i:i + 1, :]).then_inc(xn_st, 16)
                load_item(b + HALVES)
                after(sp, x1_st, (b + 1) * TPB * 16)
                for i in range(TPB):
                    after(sp, sh_st, (b * TPB + i - 1) * 16)
                    sp.dma_start(rows[:, i % 2:i % 2 + 1, :], out_tiles[:, ds(tile0 + i, 1), :]).then_inc(x1_ld[i % 2], 16)
                    if i:
                        after(sp, y_sb, b * TPB + i)
                        sp.dma_start(out_tiles[:, ds(tile0 + i - 1, 1), :],
                                     rows[:, (i - 1) % 2:(i - 1) % 2 + 1, :]).then_inc(sh_st, 16)
                after(sp, y_sb, b * TPB + TPB)
                sp.dma_start(out_tiles[:, ds(tile0 + TPB - 1, 1), :],
                             rows[:, (TPB - 1) % 2:(TPB - 1) % 2 + 1, :]).then_inc(sh_st, 16)
            load_item(EARLY - 1)
            after(sp, xn_st, TILES * 16)
            after(sp, xt_mm, TILES)
            with sp.Fori(EARLY, ITEMS) as item:
                load_item(item)
            sp.wait_ge(pad_st, 32)
            after(sp, x1_st, TILES * 16)
            after(sp, sh_st, TILES * 16)
            after(sp, rows_free, SLOT_TILES)

        @block.gpsimd
        def _(pool):
            waits_apart[pool] = pool_tick
            for s in credited:
                pool.sem_inc(s, CREDIT)
            pool.sem_inc(ready, 1)
            c = Order(pool, pool_c)
            pool.memset(rows[:, 0, :], 0.0).then_inc(const_ok, 1)
            c.mark(pool.memset(ident[:], 0.0))
            c.mark(pool.memset(ident16[:], 0.0))
            c.mark(pool.memset(ones[:], 1.0))
            c.mark(pool.memset(tri[:], 0.0))
            c.mark(pool.memset(hid[:, :, H:HP], 0.0))
            c.mark(pool.memset(half_pow[:, 0, :], 0.5))
            c.mark(pool.memset(half_pow[:, 1, :], -0.5))
            c.mark(pool.iota(iota_col[:], pattern=[[1, P]], base=0, channel_multiplier=0, allow_small_or_imprecise_dtypes=True))
            c.mark(pool.memset(one1[:], 1.0))
            c.mark(pool.iota(iota_p[:], pattern=[[1, 1]], base=0, channel_multiplier=1, allow_small_or_imprecise_dtypes=True))
            c.mark(pool.iota(first[:], pattern=[[-1, EXPERTS]], base=EXPERTS, channel_multiplier=0, allow_small_or_imprecise_dtypes=True))
            c.wait()
            for m in (ident, ident16):
                c.mark(pool.affine_select(out=m[:], in_=m[:], compare_op=ALU.not_equal, fill=1.0, base=0,
                                          pattern=[[-1, P]], channel_multiplier=1))
            c.mark(pool.affine_select(out=tri[:], in_=tri[:], compare_op=ALU.is_ge, fill=1.0, base=0,
                                      pattern=[[-1, P]], channel_multiplier=1))
            c.wait()
            pool.sem_inc(const_ok, 1)

            pool.wait_ge(cst_ok, 1)
            with pool.Fori(0, BATCHES) as b:
                o = Order(pool, pool_ch)
                o.clear()
                after(pool, stats_ok, b + 1)
                after(pool, base_sb, b * TPB)
                sd, var_e, rstd, step = pt[:, 0, :], pt[:, 1, :], pt[:, 2, :], pt[:, 3, :]
                mean_s, var_s = mv[:, 0, :, 0], mv[:, 0, :, 1]
                mean_x, var_x = mv[:, 1, :, 0], mv[:, 1, :, 1]
                o.mark(pool.tensor_tensor(sd, var_s, half_pow[:, 0, :], ALU.pow))
                o.then(pool.tensor_scalar(var_e, var_x, LN_EPS, None, ALU.add))
                o.mark(pool.tensor_tensor(rstd, var_e, half_pow[:, 1, :], ALU.pow))
                for dst, z in ((cur, 0.5077), (lo, -0.2), (hi, 1.2)):
                    o.then(pool.tensor_scalar(step, sd, z, None, ALU.mult))
                    o.then(pool.tensor_tensor(dst[:, 0, :], step, mean_s, ALU.add))
                o.mark(pool.memset(lo[:, 1, :], 290.0))
                o.then(pool.memset(hi[:, 1, :], 60.0))
                pool.sem_inc(guess_ok, 1)
                gain, shift = pt[:, 4, :], pt[:, 5, :]
                o.then(pool.tensor_scalar(step, rstd, cst[:, 3:4], None, ALU.mult))
                o.mark(pool.tensor_scalar(gain, step, 1.0, None, ALU.add))
                o.then(pool.tensor_tensor(shift, step, mean_x, ALU.mult))
                o.then(pool.tensor_scalar(shift, shift, -1.0, None, ALU.mult))
                pool.sem_inc(base_ok, 1)
                after(pool, ln_stats, b + 1)
                after(pool, xn_hi, b * TPB)
                gain2, shift2 = pt[:, 6, :], pt[:, 7, :]
                mean_2, var_2 = mv[:, 2, :, 0], mv[:, 2, :, 1]
                o.then(pool.tensor_scalar(var_e, var_2, LN_EPS, None, ALU.add))
                o.then(pool.tensor_tensor(rstd, var_e, half_pow[:, 1, :], ALU.pow))
                o.then(pool.tensor_scalar(gain2, rstd, X_SCALE, None, ALU.mult))
                o.then(pool.tensor_tensor(shift2, gain2, mean_2, ALU.mult))
                o.then(pool.tensor_scalar(shift2, shift2, -1.0, None, ALU.mult))
                pool.sem_inc(ln_ok, 1)

            pool.wait_ge(table_ok, 1)
            pool.wait_ge(pad_st, 32)
            after(pool, xn_st, TILES * 16)
            after(pool, sh_st, TILES * 16)

            def gather(t, p):
                pool.sem_clear(idx_c)
                pool.tensor_copy(idx_g[:, p:p + 1], idx[:, ds(t, 1)]).then_inc(idx_c, 1)
                pool.wait_ge(idx_c, 1)
                pool.indirect_dma_start(out=xg[:, p, :], out_offset=None, in_=xn_rows,
                                        in_offset=bass.IndirectOffsetOnAxis(ap=idx_g[:, p:p + 1], axis=0)).then_inc(g_ld[p], 16)

            def add_rows(t, p):
                after(pool, y_sb, TILES + t + 1)
                pool.sem_clear(idx_c)
                pool.tensor_copy(idx_s[:, p:p + 1], idx[:, ds(t, 1)]).then_inc(idx_c, 1)
                pool.wait_ge(idx_c, 1)
                pool.indirect_dma_start(out=out, out_offset=bass.IndirectOffsetOnAxis(ap=idx_s[:, p:p + 1], axis=0),
                                        in_=rows[:, p, :], in_offset=None, compute_op=ALU.add).then_inc(y_add, 16)

            def rows_added(t):
                pool.wait_ge(y_add, (t + 1) * 16)
                pool.sem_inc(rows_free, 1)

            def pool_tile(t, p, before):
                after(pool, xt_mm, TILES + t + 2)
                gather(t + 3, 1 - p)
                if before is not None:
                    rows_added(before)
                add_rows(t, p)

            gather(0, 0)
            gather(1, 1)
            after(pool, xt_mm, TILES + 1)
            gather(2, 0)
            pool_tile(0, 0, None)
            with pool.Fori(0, SLOT_TILES // 2 - 1) as i:
                pool_tile(i * 2 + 1, 1, i * 2)
                pool_tile(i * 2 + 2, 0, i * 2 + 1)
            t = SLOT_TILES - 2
            pool_tile(t, 1, t - 1)
            rows_added(t)
            add_rows(t + 1, 0)
            rows_added(t + 1)

        @block.scalar
        def _(act):
            act.wait_ge(ready, 1)
            act.wait_ge(small_ld, 16 * 5)
            act.activation(cst[:, 0:2], gcol[:, 0:2], ACT.Tanh).then_inc(cst_act, 1)
            act.activation(cst[:, 2:3], gcol[:, 2:3], ACT.Tanh, scale=0.5).then_inc(cst_act, 1)
            act.activation(gw[:, :, 0, :], gw_f, ACT.Copy, scale=W_SCALE).then_inc(gw_hi, 1)

            def high_halves(item):
                for n in range(CHUNKS):
                    after(act, w_ld[n % 2], (item * (CHUNKS // 2) + n // 2 + 1) * 16)
                    act.activation(w[:, ds(item, 1), 0, n * CHUNK_W:(n + 1) * CHUNK_W], stage[:, n % 2:n % 2 + 1, :],
                                   ACT.Copy, scale=W_SCALE).then_inc(w_hi, 1)

            def silu(q, p):
                after(act, up_mm, q + 1)
                after(act, hid_sb, q - 1)
                act.activation(sil[:, p, :], pg[p][:, 0:H], ACT.Silu, scale=UP_UNSCALE).then_inc(sil_sb, 1)

            def hidden_high(q, p):
                after(act, hid_mm, q + 1)
                after(act, down_mm, q - 1)
                act.activation(hid_t[:, p, 0, :], pt_bank[:, 0:HP], ACT.Copy).then_inc(hhi_sb, 1)

            with act.Fori(0, HALVES) as item:
                high_halves(item)
            with act.Fori(0, BATCHES) as b:
                after(act, sim_mm, b * TPB)
                for n, dst in enumerate((q_t, k_t)):
                    after(act, qk_mm, b * 2 + n + 1)
                    act.activation(dst, pa[n][:, :], ACT.Copy).then_inc(qk_sb, 1)
                after(act, a_made, b * TPB)
                after(act, at_mm, b * TPB)
                after(act, x1_made, b * TPB)
                for i in range(TPB):
                    after(act, sim_mm, b * TPB + i + 1)
                    act.activation(sim[:, i, :], pa[i % 2][:, :], ACT.Copy).then_inc(sim_sb, 1)
                    act.activation(att[:, i, :], pa[i % 2][:, :], ACT.Tanh, scale=0.5 * SIM_SCALE).then_inc(tanh_sb, 1)
                after(act, base_ok, b + 1)
                for i in range(TPB):
                    act.activation(xb[:, i, :], xb[:, i, :], ACT.Identity, bias=pt[:, 5, i:i + 1],
                                   scale=pt[:, 4, i:i + 1]).then_inc(base_sb, 1)
                after(act, ln_ok, b + 1)
                after(act, xn_st, b * TPB * 16)
                after(act, xt_mm, b * TPB)
                for i in range(TPB):
                    act.activation(xnr[:, i, 0:C], xb[:, i, :], ACT.Identity, bias=pt[:, 7, i:i + 1],
                                   scale=pt[:, 6, i:i + 1]).then_inc(xn_hi, 1)
                high_halves(b + HALVES)
                for m in range(TPB * HALVES):
                    q = b * (TPB * HALVES) + m
                    if m:
                        hidden_high(q - 1, (m - 1) % 2)
                    silu(q, m % 2)
                    if m % HALVES == 0:
                        act.activation(lg[:, ds(b * TPB + m // 2, 1), :, :], pg[0][:, H:H + 2 * EXPERTS], ACT.Copy).then_inc(lg_sb, 1)
                hidden_high((b + 1) * (TPB * HALVES) - 1, 1)
            high_halves(EARLY - 1)
            after(act, xn_st, TILES * 16)
            after(act, xt_mm, TILES)
            with act.Fori(EARLY, ITEMS) as item:
                high_halves(item)
            act.wait_ge(z_ok, 1)
            act.activation(r[1][:], r[0][:], ACT.Exp, scale=-UP_UNSCALE).then_inc(exp_ok, 1)

            Q0 = TILES * HALVES

            def expert_rows(t, p):
                after(act, down_mm, Q0 + t + 1)
                after(act, rows_free, t - 1)
                act.activation(rows[:, p, :], py[:, :], ACT.Copy, scale=w_slot[:, ds(t, 1)]).then_inc(y_sb, 1)

            act.wait_ge(table_ok, 1)
            silu(Q0, 0)
            with act.Fori(0, SLOT_TILES // 2) as i:
                for k in range(2):
                    t = i * 2 + k + 1
                    hidden_high(Q0 + t - 1, k)
                    silu(Q0 + t, 1 - k)
                    expert_rows(t - 1, k)
            hidden_high(Q0 + SLOT_TILES - 1, 0)
            expert_rows(SLOT_TILES - 1, 0)

        @block.tensor
        def _(pe):
            pe.wait_ge(ready, 1)
            pe.wait_ge(const_ok, 2)
            pe.wait_ge(small_ld, 16 * 5)
            pe.wait_ge(gw_ok, 1)

            def up(q, p, item, x_ready, ks, slot, logits):
                if 0 in ks:
                    after(pe, hid_sb, q - 1)
                    after(pe, xt_sb, x_ready)
                    if logits is not None:
                        after(pe, lg_sb, logits)
                for k in ks:
                    at = k * 2 * H
                    for part in range(2):
                        lhs = x_t[:, slot, part * KC + k, :]
                        for half in range(2 - part):
                            begin, end = (k, part, half) == (0, 0, 0), (k, part) == (KC - 1, 1)
                            pe.matmul(pg[p][:, 0:H], lhs, w[:, item, half, at:at + H], start=begin,
                                      stop=end, skip_group_check=True)
                            mm = pe.matmul(pu[p][:, 0:H], lhs, w[:, item, half, at + H:at + 2 * H], start=begin,
                                           stop=end, skip_group_check=True)
                        if logits is not None:
                            n = (2 - part) * EXPERTS
                            mm = pe.matmul(pg[p][:, H:H + n], lhs, gw[:, k, 0:2 - part, :].rearrange("p a e -> p (a e)"),
                                           start=False, stop=end, skip_group_check=True)
                if KC - 1 in ks:
                    mm.then_inc(up_mm, 1)

            def turn_hidden(q, p, xts):
                after(pe, hid_sb, q + 1)
                after(pe, xt_sb, xts)
                after(pe, hhi_sb, q)
                after(pe, hlo_sb, q)
                for j in range(JC):
                    mm = pe.transpose(pt_bank[:, j * P:(j + 1) * P], hid[:, p, j * P:(j + 1) * P], ident[:])
                mm.then_inc(hid_mm, 1)

            def down(q, p, item, begin, end, ys):
                after(pe, hhi_sb, q + 1)
                after(pe, hlo_sb, q + 1)
                if begin:
                    after(pe, y_sb, ys)
                for j in range(JC):
                    at = UP_W + j * C
                    for part in range(2):
                        for half in range(2 - part):
                            mm = pe.matmul(py[:, :], hid_t[:, p, part, j * P:(j + 1) * P], w[:, item, half, at:at + C],
                                           start=begin and (j, part, half) == (0, 0, 0),
                                           stop=end and (j, part) == (JC - 1, 1))
                mm.then_inc(down_mm, 1)

            def turn_rows(src, q):
                after(pe, hhi_sb, q)
                after(pe, hlo_sb, q)
                for n in range(2 * KC):
                    mm = pe.transpose(xt_ps[:, n, :], src[:, n * P:(n + 1) * P], ident16[:])
                mm.then_inc(xt_mm, 1)

            with pe.Fori(0, BATCHES) as b:
                after(pe, ctx_ld, (b + 1) * 16)
                after(pe, x1_made, b * TPB)
                pe.matmul(pa[0][:, :], wq_s, ctx_b, start=True, stop=True).then_inc(qk_mm, 1)
                pe.matmul(pa[1][:, :], wk_s, ctx_b, start=True, stop=True).then_inc(qk_mm, 1)
                after(pe, qk_sb, (b + 1) * 2)
                for i in range(TPB):
                    if i >= 2:
                        after(pe, tanh_sb, b * TPB + i - 1)
                        after(pe, sim_sb, b * TPB + i - 1)
                    pe.matmul(pa[i % 2][:, :], q_t[:, i * P:(i + 1) * P], k_t, start=True, stop=True).then_inc(sim_mm, 1)
                after(pe, miss_ok, b + 1)
                after(pe, tanh_sb, (b + 1) * TPB)
                pe.matmul(pa[0][0:1, 0:1], missed[:], one1[:], start=True, stop=True).then_inc(miss_mm, 1)
                after(pe, a_made, (b + 1) * TPB)
                for i in range(TPB):
                    if i >= 2:
                        after(pe, x1_made, b * TPB + i - 1)
                    for j in range(TPB):
                        mm = pe.transpose(pa[i % 2][:, j * P:(j + 1) * P], att[:, j, i * P:(i + 1) * P], ident[:])
                    mm.then_inc(at_mm, 1)

                after(pe, w_lo, HALVES * CHUNKS)
                after(pe, w_hi, HALVES * CHUNKS)
                q0 = b * (TPB * HALVES)
                t0 = b * TPB
                after(pe, xn_hi, t0 + 1)
                after(pe, xn_lo, t0 + 1)
                turn_rows(xnr[:, 0, :], q0)
                for m in range(TPB * HALVES):
                    q, i, h = q0 + m, m // HALVES, m % HALVES
                    up(q, m % 2, h, t0 + i + 1, range(0, KC // 2), i % 2, (t0 + i) if h == 0 else None)
                    if m:
                        turn_hidden(q - 1, (m - 1) % 2, t0 + i + 1 + (h == 1 and i + 1 < TPB))
                    up(q, m % 2, h, None, range(KC // 2, KC), i % 2, (t0 + i) if h == 0 else None)
                    if m:
                        down(q - 1, (m - 1) % 2, 1 - h, h == 1, h == 0, t0 + (m - 1) // HALVES)
                    if h == 0 and i + 1 < TPB:
                        after(pe, xn_hi, t0 + i + 2)
                        after(pe, xn_lo, t0 + i + 2)
                        turn_rows(xnr[:, i + 1, :], q)
                q_last = q0 + TPB * HALVES - 1
                turn_hidden(q_last, 1, t0 + TPB)
                down(q_last, 1, 1, False, True, t0 + TPB - 1)

            pe.wait_ge(route_ok, 1)
            sel = r[2][:].rearrange("p t e -> p (t e)")
            pe.matmul(pa[0][:, 0:P], tri[:], sel, start=True, stop=True).then_inc(route_mm, 1)
            pe.matmul(pa[1][:, 0:P], ones[:], sel, start=True, stop=True).then_inc(route_mm, 1)
            pe.wait_ge(route_ok, 2)
            for n in range(TOPK * TILES):
                pe.wait_ge(hot_ok, n + 1)
                pe.matmul(pa[0][:, 0:2 * SLOT_COLS], hot_col[:, n % 4, :],
                          hot_val[:, n % 4, :, :].rearrange("p v c -> p (v c)"),
                          start=(n == 0), stop=(n == TOPK * TILES - 1)).then_inc(hot_mm, 1)

            pe.wait_ge(table_ok, 1)
            after(pe, w_lo, ITEMS * CHUNKS)
            after(pe, w_hi, ITEMS * CHUNKS)
            Q0 = TILES * HALVES

            def turn_gathered(t, p, n, q):
                pe.wait_ge(g_ld[p], (n + 1) * 16)
                turn_rows(xg[:, p, :], q)

            def item_of(t):
                return pe.value_load(tile_e[0:1, ds(t, 1)], min_val=HALVES, max_val=ITEMS - 1)

            turn_gathered(0, 0, 0, Q0)
            turn_gathered_wait = TILES + 1
            after(pe, xt_sb, turn_gathered_wait)
            turn_gathered(1, 1, 0, Q0)
            e = item_of(0)
            up(Q0, 0, ds(e, 1), TILES + 1, range(KC), 0, None)
            after(pe, xt_sb, TILES + 2)
            turn_gathered(2, 0, 1, Q0)
            with pe.Fori(0, SLOT_TILES // 2) as i:
                for k in range(2):
                    t = i * 2 + k + 1
                    e_now, e_before = item_of(t), item_of(t - 1)
                    up(Q0 + t, 1 - k, ds(e_now, 1), TILES + t + 1, range(0, KC // 2), 1 - k, None)
                    turn_hidden(Q0 + t - 1, k, TILES + t + 2)
                    up(Q0 + t, 1 - k, ds(e_now, 1), None, range(KC // 2, KC), 1 - k, None)
                    down(Q0 + t - 1, k, ds(e_before, 1), True, True, TILES + t - 1)
                    turn_gathered(t + 2, 1 - k, i + 1 + k, Q0 + t)
            t = SLOT_TILES
            e = item_of(t - 1)
            turn_hidden(Q0 + t - 1, 0, TILES + t + 2)
            down(Q0 + t - 1, 0, ds(e, 1), True, True, TILES + t - 1)

        @block.vector
        def _(dve):
            dve.wait_ge(ready, 1)
            o = Order(dve, dve_ch)

            dve.wait_ge(cst_act, 2)
            o.then(dve.tensor_scalar(cst[:, 5:6], cst[:, 2:3], 0.5, 0.5, ALU.mult, ALU.add))
            o.mark(dve.tensor_scalar(cst[:, 6:7], cst[:, 5:6], -1.0, 1.0, ALU.mult, ALU.add))
            o.then(dve.tensor_tensor(cst[:, 7:8], cst[:, 5:6], cst[:, 0:1], ALU.mult))
            o.mark(dve.tensor_tensor(cst[:, 3:4], cst[:, 6:7], cst[:, 0:1], ALU.mult))
            o.mark(dve.tensor_scalar(cst[:, 4:5], cst[:, 7:8], 0.25, None, ALU.mult))
            o.then(dve.tensor_scalar(cst[:, 8:9], cst[:, 1:2], DOWN_UNSCALE, None, ALU.mult))
            dve.wait_ge(gw_hi, 1)
            dve.scalar_tensor_tensor(out=gw[:, :, 1, :], in0=gw_f, scalar=W_SCALE, in1=gw[:, :, 0, :],
                                     op0=ALU.mult, op1=ALU.subtract).then_inc(gw_ok, 1)
            dve.sem_inc(cst_ok, 1)
            dve.wait_ge(const_ok, 2)
            unscaled_tanh_ffn = cst[:, 8:9]
            quarter_gamma = cst[:, 4:5]

            def low_halves(item):
                for n in range(CHUNKS):
                    after(dve, w_hi, item * CHUNKS + n + 1)
                    dve.scalar_tensor_tensor(out=w[:, ds(item, 1), 1, n * CHUNK_W:(n + 1) * CHUNK_W],
                                             in0=stage[:, n % 2:n % 2 + 1, :], scalar=W_SCALE,
                                             in1=w[:, ds(item, 1), 0, n * CHUNK_W:(n + 1) * CHUNK_W],
                                             op0=ALU.mult, op1=ALU.subtract).then_inc(w_lo, 1)

            def hidden(q, p):
                after(dve, up_mm, q + 1)
                after(dve, sil_sb, q + 1)
                after(dve, hid_mm, q - 1)
                dve.scalar_tensor_tensor(out=hid[:, p, 0:H], in0=pu[p][:, 0:H], scalar=UP_UNSCALE * H_SCALE,
                                         in1=sil[:, p, :], op0=ALU.mult, op1=ALU.mult).then_inc(hid_sb, 1)

            def hidden_low(q, p):
                after(dve, hhi_sb, q + 1)
                dve.tensor_tensor(hid_t[:, p, 1, :], pt_bank[:, 0:HP], hid_t[:, p, 0, :], ALU.subtract).then_inc(hlo_sb, 1)

            def rows_turned(g, p, uses):
                after(dve, xt_mm, g + 1)
                after(dve, up_mm, uses)
                dve.tensor_copy(x_t[:, p, :, :], xt_ps).then_inc(xt_sb, 1)

            with dve.Fori(0, HALVES) as item:
                low_halves(item)
            with dve.Fori(0, BATCHES) as b:
                o.clear()
                for i in range(TPB):
                    after(dve, sim_sb, b * TPB + i + 1)
                    o.mark(dve.bn_stats(bn6[:, 0, i, :], sim[:, i, :]))
                after(dve, x_ld, (b + 1) * 16)
                for i in range(TPB):
                    o.mark(dve.bn_stats(bn6[:, 1, i, :], xb[:, i, :]))
                o.wait()
                for s in range(2):
                    for i in range(TPB):
                        o.mark(dve.bn_aggr(mv[:, s, i, :], bn6[:, s, i, :]))
                o.wait()
                dve.sem_inc(stats_ok, 1)
                after(dve, tanh_sb, (b + 1) * TPB)
                for i in range(TPB):
                    o.mark(dve.tensor_scalar(att[:, i, :], att[:, i, :], 1.0, None, ALU.add))

                after(dve, guess_ok, b + 1)
                for n in range(ROUNDS):
                    for i in range(TPB):
                        o.mark(dve.tensor_scalar(junk[:, i, :], sim[:, i, :], cur[:, 0, i:i + 1], 0.0, ALU.is_ge, ALU.add,
                                                 accum_out=cur[:, 1, i:i + 1]))
                    o.wait()
                    o.mark(dve.tensor_scalar(above[:], cur[:, 1, :], float(KEEP), None, ALU.is_ge))
                    o.then(dve.tensor_scalar(below[:], cur[:, 1, :], float(KEEP), None, ALU.is_lt))
                    o.mark(dve.copy_predicated(lo[:, 0, :], above[:], cur[:, 0, :]))
                    o.mark(dve.copy_predicated(lo[:, 1, :], above[:], cur[:, 1, :]))
                    o.mark(dve.copy_predicated(hi[:, 0, :], below[:], cur[:, 0, :]))
                    o.then(dve.copy_predicated(hi[:, 1, :], below[:], cur[:, 1, :]))
                    if n < ROUNDS - 1:
                        gap, frac, width = tmp4[:, 0, :], tmp4[:, 1, :], tmp4[:, 2, :]
                        o.mark(dve.tensor_tensor(gap, lo[:, 1, :], hi[:, 1, :], ALU.subtract))
                        o.then(dve.tensor_tensor(width, hi[:, 0, :], lo[:, 0, :], ALU.subtract))
                        o.then(dve.reciprocal(gap, gap))
                        o.then(dve.scalar_tensor_tensor(out=frac, in0=lo[:, 1, :], scalar=KEEP - 4.0, in1=gap,
                                                        op0=ALU.subtract, op1=ALU.mult))
                        o.then(dve.tensor_scalar(frac, frac, 0.02, 0.98, ALU.max, ALU.min))
                        o.then(dve.tensor_tensor(frac, frac, width, ALU.mult))
                        o.then(dve.tensor_tensor(cur[:, 0, :], frac, lo[:, 0, :], ALU.add))
                rank, miss = tmp4[:, 3, :], tmp4[:, 4, :]
                o.mark(dve.tensor_scalar(rank, hi[:, 1, :], -1.0, KEEP - 1.0, ALU.mult, ALU.add))
                o.mark(dve.tensor_scalar(miss, hi[:, 1, :], KEEP - 8.0, 0.0, ALU.is_lt, ALU.add, accum_out=missed[:]))
                o.wait()
                dve.sem_inc(miss_ok, 1)
                for i in range(TPB):
                    o.then(dve.tensor_scalar(masked[:, i % 2, :], sim[:, i, :], hi[:, 0, i:i + 1], -BIG, ALU.is_ge, ALU.mult))
                    o.then(dve.tensor_tensor(masked[:, i % 2, :], masked[:, i % 2, :], sim[:, i, :], ALU.add))
                    o.then(dve.max(top8[:, i, :], masked[:, i % 2, :]))
                    o.then(dve.scalar_tensor_tensor(out=pick8[:, i, :], in0=iota_col[:, 0:8], scalar=rank[:, i:i + 1],
                                                    in1=top8[:, i, :], op0=ALU.is_equal, op1=ALU.mult,
                                                    accum_out=thr[:, i:i + 1]))
                after(dve, miss_mm, b + 1)
                o.then(dve.tensor_copy(missed_i[:], pa[0][0:1, 0:1]))
                any_missed = dve.value_load(missed_i[0:1, 0:1], min_val=0, max_val=P * TPB)
                with dve.If(any_missed > 0):
                    f = Order(dve, fb_ch)
                    f.clear()
                    for i in range(TPB):
                        f.then(dve.tensor_copy(masked[:, 0, :], sim[:, i, :]))
                        with dve.Fori(0, (KEEP - 1) // 8):
                            dve.sem_clear(fb_ch)
                            dve.max(top8[:, i, :], masked[:, 0, :]).then_inc(fb_ch, 1)
                            dve.wait_ge(fb_ch, 1)
                            dve.match_replace(out=masked[:, 0, :], in_to_replace=top8[:, i, :], in_values=masked[:, 0, :],
                                              imm_value=-BIG).then_inc(fb_ch, 1)
                            dve.wait_ge(fb_ch, 2)
                        f.n = 0
                        dve.sem_clear(fb_ch)
                        f.then(dve.max(top8[:, i, :], masked[:, 0, :]))
                        f.then(dve.tensor_copy(thr[:, i:i + 1], top8[:, i, (KEEP - 1) % 8:(KEEP - 1) % 8 + 1]))
                for i in range(TPB):
                    dve.scalar_tensor_tensor(out=att[:, i, :], in0=sim[:, i, :], scalar=thr[:, i:i + 1], in1=att[:, i, :],
                                             op0=ALU.is_ge, op1=ALU.mult).then_inc(a_made, 1)
                after(dve, a_made, (b + 1) * TPB)
                for i in range(TPB):
                    after(dve, base_sb, b * TPB + i + 1)
                    o.mark(dve.scalar_tensor_tensor(out=xb[:, i, :], in0=att[:, i, :], scalar=quarter_gamma, in1=xb[:, i, :],
                                                    op0=ALU.mult, op1=ALU.add))
                o.wait()
                for i in range(TPB):
                    after(dve, at_mm, b * TPB + i + 1)
                    dve.scalar_tensor_tensor(out=xb[:, i, :], in0=pa[i % 2][:, :], scalar=quarter_gamma, in1=xb[:, i, :],
                                             op0=ALU.mult, op1=ALU.add).then_inc(x1_made, 1)
                for i in range(TPB):
                    after(dve, x1_made, b * TPB + i + 1)
                    o.mark(dve.bn_stats(bn6[:, 2, i, :], xb[:, i, :]))
                o.wait()
                for i in range(TPB):
                    o.mark(dve.bn_aggr(mv[:, 2, i, :], bn6[:, 2, i, :]))
                o.wait()
                dve.sem_inc(ln_stats, 1)
                after(dve, ln_ok, b + 1)
                for i in range(TPB):
                    o.then(dve.tensor_scalar(xn[:, i % 2, :], xb[:, i, :], pt[:, 6, i:i + 1], pt[:, 7, i:i + 1], ALU.mult, ALU.add))
                    after(dve, xn_hi, b * TPB + i + 1)
                    dve.tensor_tensor(xnr[:, i, C:2 * C], xn[:, i % 2, :], xnr[:, i, 0:C], ALU.subtract).then_inc(xn_lo, 1)
                after(dve, xn_lo, (b + 1) * TPB)
                low_halves(b + HALVES)

                q0, t0 = b * (TPB * HALVES), b * TPB

                def shared_rows(i):
                    after(dve, down_mm, q0 + 2 * i + 2)
                    after(dve, x1_ld[i % 2], (b * (TPB // 2) + i // 2 + 1) * 16)
                    dve.scalar_tensor_tensor(out=rows[:, i % 2, :], in0=py[:, :], scalar=unscaled_tanh_ffn,
                                             in1=rows[:, i % 2, :], op0=ALU.mult, op1=ALU.add).then_inc(y_sb, 1)

                rows_turned(t0, 0, q0)
                for m in range(TPB * HALVES):
                    q, i, h = q0 + m, m // HALVES, m % HALVES
                    if m:
                        hidden_low(q - 1, (m - 1) % 2)
                    hidden(q, m % 2)
                    if h == 0 and i:
                        shared_rows(i - 1)
                    if h == 0 and i + 1 < TPB:
                        rows_turned(t0 + i + 1, (i + 1) % 2, q)
                hidden_low(q0 + TPB * HALVES - 1, 1)
                shared_rows(TPB - 1)
            low_halves(EARLY - 1)
            with dve.Fori(EARLY, ITEMS) as item:
                low_halves(item)

            o.clear()

            def bc(col):
                return col.unsqueeze(2).to_broadcast([P, TILES, EXPERTS])

            def over_tiles(row):
                return row.unsqueeze(1).to_broadcast([P, TILES, EXPERTS])

            after(dve, lg_sb, TILES)
            o.then(dve.tensor_tensor(r[0][:], lg[:, :, 0, :], lg[:, :, 1, :], ALU.add))
            dve.sem_inc(z_ok, 1)
            dve.wait_ge(exp_ok, 1)
            s, cand, sel, hot1, hot2 = r[1][:], r[3][:], r[2][:], r[4][:], r[5][:]
            o.then(dve.tensor_scalar(s, s, 1.0, None, ALU.add))
            o.then(dve.reciprocal(s, s))
            o.then(dve.tensor_tensor(cand, s, over_tiles(bias_b[:]), ALU.add))

            def best(hot, col):
                o.then(dve.tensor_reduce(rc[:, col, :], cand, AX.X, ALU.max))
                o.then(dve.tensor_tensor(hot, cand, bc(rc[:, col, :]), ALU.is_equal))
                o.then(dve.tensor_tensor(hot, hot, over_tiles(first[:]), ALU.mult))
                o.then(dve.tensor_reduce(rc[:, col, :], hot, AX.X, ALU.max))
                o.then(dve.tensor_tensor(hot, over_tiles(first[:]), bc(rc[:, col, :]), ALU.is_equal))

            best(hot1, 1)
            o.then(dve.scalar_tensor_tensor(out=cand, in0=hot1, scalar=-BIG, in1=cand, op0=ALU.mult, op1=ALU.add))
            best(hot2, 2)
            dve.tensor_tensor(sel, hot1, hot2, ALU.add).then_inc(route_ok, 1)
            z = r[0][:]
            for k, hot in enumerate((hot1, hot2)):
                o.then(dve.tensor_tensor(z, s, hot, ALU.mult))
                o.then(dve.tensor_reduce(rc[:, 3 + k, :], z, AX.X, ALU.add))
            o.then(dve.tensor_tensor(rc[:, 5, :], rc[:, 3, :], rc[:, 4, :], ALU.add))
            o.then(dve.reciprocal(rc[:, 5, :], rc[:, 5, :]))
            gate = slot_f[:, 0, :, :]
            for k in range(TOPK):
                o.then(dve.tensor_tensor(gate[:, k, :], rc[:, 3 + k, :], rc[:, 5, :], ALU.mult))
            dve.wait_ge(route_mm, 2)
            total = r[1][:]
            o.then(dve.tensor_copy(total, pa[1][:, 0:P].rearrange("p (t e) -> p t e", t=TILES)))
            o.then(dve.tensor_copy(cand, total))
            a, c2 = cand, z
            step = 1
            while step < TILES:
                o.mark(dve.tensor_copy(c2[:, 0:step, :], a[:, 0:step, :]))
                o.then(dve.tensor_tensor(c2[:, step:, :], a[:, step:, :], a[:, :TILES - step, :], ALU.add))
                a, c2 = c2, a
                step *= 2
            o.then(dve.tensor_scalar(re8[:, 0, :], a[:, TILES - 1, :], float(P - 1), None, ALU.add))
            o.then(dve.tensor_copy(ri8[:], re8[:, 0, :]))
            o.then(dve.tensor_scalar(ri8[:], ri8[:], P.bit_length() - 1, None, ALU.logical_shift_right))
            o.then(dve.tensor_copy(re8[:, 0, :], ri8[:]))
            o.then(dve.tensor_copy(re8[:, 3, :], re8[:, 0, :]))
            ea, eb = re8[:, 3, :], re8[:, 1, :]
            step = 1
            while step < EXPERTS:
                o.mark(dve.tensor_copy(eb[:, 0:step], ea[:, 0:step]))
                o.then(dve.tensor_tensor(eb[:, step:], ea[:, step:], ea[:, :EXPERTS - step], ALU.add))
                ea, eb = eb, ea
                step *= 2
            ends = ea
            o.then(dve.tensor_tensor(re8[:, 2, :], ends, re8[:, 0, :], ALU.subtract))
            o.then(dve.tensor_scalar(re8[:, 2, :], re8[:, 2, :], float(P), None, ALU.mult))
            o.then(dve.tensor_tensor(a, a, total, ALU.subtract))
            o.then(dve.tensor_tensor(a, a, pa[0][:, 0:P].rearrange("p (t e) -> p t e", t=TILES), ALU.add))
            o.then(dve.tensor_tensor(a, a, over_tiles(re8[:, 2, :]), ALU.add))
            for k, hot in enumerate((hot1, hot2)):
                o.then(dve.tensor_tensor(total, a, hot, ALU.mult))
                o.then(dve.tensor_reduce(slot_f[:, 1, k, :], total, AX.X, ALU.add))
            o.then(dve.tensor_copy(slot_i[:, 0, :, :], slot_f[:, 1, :, :]))
            o.mark(dve.tensor_scalar(slot_i[:, 1, :, :], slot_i[:, 0, :, :], P.bit_length() - 1, None, ALU.logical_shift_right))
            o.then(dve.tensor_scalar(slot_i[:, 2, :, :], slot_i[:, 0, :, :], P - 1, None, ALU.bitwise_and))
            o.mark(dve.tensor_copy(slot_f[:, 1, :, :], slot_i[:, 1, :, :]))
            o.then(dve.tensor_copy(slot_f[:, 2, :, :], slot_i[:, 2, :, :]))
            o.then(dve.tensor_scalar(rc[:, 6, :], iota_tile[:, 0:TILES], float(P), iota_p[:, 0:1], ALU.mult, ALU.add))
            for k in range(TOPK):
                o.then(dve.scalar_tensor_tensor(out=slot_f[:, 3, k, :], in0=rc[:, 6, :], scalar=-float(TOKENS),
                                                in1=slot_f[:, 2, k, :], op0=ALU.add, op1=ALU.subtract))
            tcount = rc[0:1, 0:3, :].rearrange("p a b -> p (a b)")[:, 0:SLOT_COLS]
            o.then(dve.tensor_scalar(tcount, iota_col[0:1, 0:SLOT_COLS], 0.0, float(HALVES), ALU.mult, ALU.add))
            for n in range(EXPERTS - 1):
                o.then(dve.scalar_tensor_tensor(out=tcount, in0=iota_col[0:1, 0:SLOT_COLS], scalar=ends[0:1, n:n + 1], in1=tcount,
                                                op0=ALU.is_ge, op1=ALU.add))
            o.then(dve.tensor_copy(tile_e[:], tcount))
            dve.sem_inc(route_ok, 1)
            for n in range(TOPK * TILES):
                k, g = n // TILES, n % TILES
                if n >= 4:
                    dve.wait_ge(hot_mm, n - 3)
                o.mark(dve.tensor_scalar(hot_col[:, n % 4, :], iota_col[:], slot_f[:, 2, k, g:g + 1], None, ALU.is_equal))
                o.mark(dve.tensor_scalar(hot_val[:, n % 4, 0, :], iota_tile, slot_f[:, 1, k, g:g + 1],
                                         slot_f[:, 3, k, g:g + 1], ALU.is_equal, ALU.mult))
                o.then(dve.tensor_scalar(hot_val[:, n % 4, 1, :], iota_tile, slot_f[:, 1, k, g:g + 1],
                                         gate[:, k, g:g + 1], ALU.is_equal, ALU.mult))
                dve.sem_inc(hot_ok, 1)
                dve.wait_ge(hot_ok, n + 1)
            dve.wait_ge(hot_mm, TOPK * TILES)
            o.mark(dve.tensor_scalar(idx[:], pa[0][:, 0:SLOT_COLS], iota_p[:, 0:1], float(TOKENS), ALU.add, ALU.add))
            o.then(dve.tensor_scalar(w_slot[:], pa[0][:, SLOT_COLS:2 * SLOT_COLS], unscaled_tanh_ffn, None, ALU.mult))
            dve.sem_inc(table_ok, 1)

            Q0 = TILES * HALVES
            rows_turned(TILES, 0, Q0)
            rows_turned(TILES + 1, 1, Q0)
            hidden(Q0, 0)
            rows_turned(TILES + 2, 0, Q0 + 1)
            with dve.Fori(0, SLOT_TILES // 2) as i:
                for k in range(2):
                    t = i * 2 + k + 1
                    hidden_low(Q0 + t - 1, k)
                    hidden(Q0 + t, 1 - k)
                    rows_turned(TILES + t + 2, 1 - k, Q0 + t + 1)
            hidden_low(Q0 + SLOT_TILES - 1, 0)


def kernel(x, ctx_512, g_xattn, g_ffn, L0_xattn_Wq, L0_xattn_Wk, L0_xattn_gamma_raw, L0_ffn_gate_w, L0_ffn_gate_bias,
           L0_ffn_shared_gw, L0_ffn_shared_dw, L0_ffn_up_w, L0_ffn_down_w):
    import concourse.bacc as bacc
    from concourse import mybir
    from concourse.bass_utils import run_bass_kernel_spmd

    def chunks(m):
        m = np.asarray(m)
        return m.reshape(-1, P, m.shape[1]).transpose(1, 0, 2).reshape(P, -1)

    def item(gate, value, down):
        up = np.concatenate([np.asarray(gate).T, np.asarray(value).T], axis=1)
        dn = np.zeros((HP, C), np.float32)
        dn[:H] = np.asarray(down).T
        return np.concatenate([chunks(up), chunks(dn)], axis=1)

    gw, dw = np.asarray(L0_ffn_shared_gw), np.asarray(L0_ffn_shared_dw)
    up_w, down_w = np.asarray(L0_ffn_up_w), np.asarray(L0_ffn_down_w)
    S = HALVES * H
    items = [item(gw[S + h * H:S + (h + 1) * H], gw[h * H:(h + 1) * H], dw[:, h * H:(h + 1) * H]) for h in range(HALVES)]
    items += [item(up_w[e, :H], up_w[e, H:], down_w[e]) for e in range(EXPERTS)]
    arrays = {
        "x": np.asarray(x).reshape(TOKENS, C),
        "ctx_t": np.asarray(ctx_512).reshape(TOKENS, D).T,
        "wq_t": np.asarray(L0_xattn_Wq).T,
        "wk_t": np.asarray(L0_xattn_Wk).T,
        "gates": np.concatenate([np.asarray(g_xattn).reshape(1), np.asarray(g_ffn).reshape(1),
                                 np.asarray(L0_xattn_gamma_raw).reshape(1)]),
        "gate_wt": np.asarray(L0_ffn_gate_w).T.reshape(KC, P, EXPERTS).transpose(1, 0, 2),
        "gate_bias": np.asarray(L0_ffn_gate_bias),
        "weights": np.stack(items),
    }
    nc = bacc.Bacc("TRN2", target_bir_lowering=False, num_devices=1)
    named, args = {}, []
    for name, a in arrays.items():
        a = np.ascontiguousarray(a)
        named[f"in_{name}"] = a
        args.append(nc.dram_tensor(f"in_{name}", a.shape, mybir.dt.from_np(a.dtype), kind="ExternalInput").ap())
    out = nc.dram_tensor("out", (TOKENS + PAD_ROWS, C), mybir.dt.float32, kind="ExternalOutput").ap()
    xn_rows = nc.dram_tensor("xn_rows", (TOKENS + PAD_ROWS, 2 * C), mybir.dt.float16, kind="Internal").ap()
    build(nc, *args, out, xn_rows)
    res = run_bass_kernel_spmd(nc, [named], core_ids=[0])
    return res.results[0]["out"][:TOKENS].reshape(BATCHES, SEQ, C)
```

```python
import numpy as np

BATCHES, SEQ, C, D = 4, 512, 512, 128
P = 128
TOKENS = BATCHES * SEQ
TPB = SEQ // P
TILES = TOKENS // P
KC = C // P
EXPERTS, TOPK = 8, 2
H = 352
HALVES = 2
HP = 384
JC = HP // P
PIECES = [(h, j * P, min(P, H - j * P)) for h in range(HALVES) for j in range(JC)]
UPS = len(PIECES)
SLOTS_STEP = TOPK * TILES // (UPS - 2)
BEFORE = 3
PER_STEP = 4
KEEP = int(SEQ * 0.3)
UP_W = KC * 2 * H
ITEM_W = UP_W + JC * C
ITEMS = HALVES + EXPERTS
EARLY = 7
CHUNKS = 8
RING = 4
CHUNK_W = ITEM_W // CHUNKS
SLOT_TILES = TOKENS * TOPK // P + EXPERTS - 1
SLOT_COLS = SLOT_TILES + 2
PAD_ROWS = P
SMALL = 3
ROUNDS = 5
X_SCALE, W_SCALE, H_SCALE = 16.0, 256.0, 16.0
UP_UNSCALE = 1.0 / (X_SCALE * W_SCALE)
DOWN_UNSCALE = 1.0 / (H_SCALE * W_SCALE)
SIM_SCALE = 1.0 / (float(np.sqrt(np.float32(D // 4))) * 4.0)
LN_EPS = 1e-5
BIG = 3.0e38
CREDIT = 32


def build(nc, x, ctx_t, wq_t, wk_t, gates, gate_wt, gate_bias, weights, out, xn_rows):
    import concourse.bass as bass
    from concourse import mybir
    from contextlib import ExitStack

    F32, F16, I32, U32 = mybir.dt.float32, mybir.dt.float16, mybir.dt.int32, mybir.dt.uint32
    ALU, ACT, AX = mybir.AluOpType, mybir.ActivationFunctionType, mybir.AxisListType
    ds = bass.ds

    x_tiles = x.rearrange("(g p) c -> p g c", p=P)
    out_tiles = out.rearrange("(g p) c -> p g c", p=P)
    xn_tiles = xn_rows.rearrange("(g p) c -> p g c", p=P)

    with ExitStack() as ctx:
        def sb(name, shape, dt=F32):
            return ctx.enter_context(nc.sbuf_tensor(name, shape, dt))

        def bank(name):
            return ctx.enter_context(nc.psum_tensor(name, [P, 512], F32))

        credited = []

        def sem(name, credit=True):
            s = ctx.enter_context(nc.semaphore(name))
            if credit:
                credited.append(s)
            return s

        w = sb("w", [P, ITEMS, 2, ITEM_W], F16)
        attn = w[:, EARLY:ITEMS, :, :].rearrange("p a b c -> p (a b c)").bitcast(F32)
        taken = [0]

        def attn_buf(words):
            taken[0] += words
            assert taken[0] <= (ITEMS - EARLY) * ITEM_W
            return attn[:, taken[0] - words:taken[0]]

        def attn_tiles():
            return attn_buf(TPB * SEQ).rearrange("p (i c) -> p i c", i=TPB)

        xb = attn_tiles()
        sim = attn_tiles()
        wq_s, wk_s = attn_buf(D), attn_buf(D)
        att = attn_tiles()
        xnr = attn_buf(TPB * C).bitcast(F16).rearrange("p (i c) -> p i c", i=TPB)
        taken[0] = (ITEMS - 1 - EARLY) * ITEM_W
        hot = attn_buf(2 * SEQ + TPB * SEQ // 2)
        q_t, k_t = hot[:, 0:SEQ], hot[:, SEQ:2 * SEQ]
        ctx_b = q_t
        junk = hot[:, 2 * SEQ:].bitcast(F16).rearrange("p (i c) -> p i c", i=TPB)
        masked = junk.rearrange("p i c -> p (i c)").bitcast(F32).rearrange("p (i c) -> p i c", i=2)
        xn = masked
        x_tb = attn_buf(KC * SEQ).bitcast(F16).rearrange("p (a c) -> p a c", a=2 * KC)

        stage = sb("stage", [P, RING, CHUNK_W])
        work = sb("work", [P, 2 * KC * P + 2 * HP + 2 * HP + 2 * C + 2 * H])
        used = [0]

        def work_buf(words):
            used[0] += words
            return work[:, used[0] - words:used[0]]

        hid_tb = work_buf(UPS * SEQ).bitcast(F16).rearrange("p (u a c) -> p u a c", u=UPS, a=2)
        hb = work_buf(2 * SEQ).rearrange("p (a c) -> p a c", a=2)
        used[0] = 0
        x_t = work_buf(2 * KC * P).bitcast(F16).rearrange("p (s a c) -> p s a c", s=2, a=2 * KC)
        hid = work_buf(2 * HP).rearrange("p (a c) -> p a c", a=2)
        hid_t = work_buf(2 * HP).bitcast(F16).rearrange("p (s a c) -> p s a c", s=2, a=2)
        sil = work_buf(2 * H).rearrange("p (a c) -> p a c", a=2)
        assert used[0] >= UPS * SEQ
        xg = work_buf(2 * C).bitcast(F16).rearrange("p (a c) -> p a c", a=2)
        rows = sb("rows", [P, 2, C])
        ident, ident16 = sb("ident", [P, P]), sb("ident16", [P, P], F16)
        ones, tri = sb("ones", [P, P], F16), sb("tri", [P, P], F16)
        one1 = sb("one1", [P, 1])
        iota_col = sb("iota_col", [P, P])
        iota_p = sb("iota_p", [P, 1])
        iota_tile = iota_col[:, 0:SLOT_COLS]
        first = sb("first", [P, EXPERTS])
        warm = sb("warm", [P, 1])
        gcol, cst = sb("gcol", [P, 3]), sb("cst", [P, 9])
        gw_f, gw = attn_buf(KC * EXPERTS).rearrange("p (k e) -> p k e", k=KC), sb("gw", [P, KC, 2, EXPERTS], F16)
        bias_b = sb("bias_b", [P, EXPERTS])
        half_pow = sb("half_pow", [P, 2, TPB])
        bn6 = attn_buf(3 * TPB * 6).rearrange("p (s i c) -> p s i c", s=3, i=TPB)
        mv = sb("mv", [P, 3, TPB, 2])
        pt = sb("pt", [P, 8, TPB])
        lo, hi, cur = (attn_buf(2 * TPB).rearrange("p (a i) -> p a i", a=2) for _ in range(3))
        below, above = sb("below", [P, TPB], U32), sb("above", [P, TPB], U32)
        tmp4 = sb("tmp4", [P, 6, TPB])
        top8, pick8 = (attn_buf(TPB * 8).rearrange("p (i c) -> p i c", i=TPB) for _ in range(2))
        thr = sb("thr", [P, TPB])
        acc = sb("acc", [P, TPB // 2])
        missed, missed_i = sb("missed", [P, 1]), sb("missed_i", [1, 1], I32)
        lg = sb("lg", [P, TILES, 2, EXPERTS])
        r = [sb(f"r{n}", [P, TILES, EXPERTS], F16 if n == 2 else F32) for n in range(6)]

        rc = sb("rc", [P, 7, TILES])
        re8 = sb("re8", [P, 6, EXPERTS])
        ri8 = sb("ri8", [P, EXPERTS], I32)
        slot_i = sb("slot_i", [P, 3, TOPK, TILES], I32)
        slot_f = sb("slot_f", [P, 4, TOPK, TILES])
        idx = sb("idx", [P, SLOT_COLS], I32)
        idx_g, idx_s = sb("idx_g", [P, 2], I32), sb("idx_s", [P, 2], I32)
        w_slot = sb("w_slot", [P, SLOT_COLS])
        tile_e = sb("tile_e", [1, SLOT_COLS], I32)
        hot_col = hot[:, 0:SLOTS_STEP * P].rearrange("p (a c) -> p a c", a=SLOTS_STEP)
        hot_val = hot[:, SLOTS_STEP * P:SLOTS_STEP * (P + 2 * SLOT_COLS)].rearrange("p (a v c) -> p a v c", a=SLOTS_STEP, v=2)

        pa = [bank("pa0"), bank("pa1")]
        pg, pu = [bank("pg0"), bank("pg1")], [bank("pu0"), bank("pu1")]
        pt_bank = bank("pt_bank")
        py = bank("py")
        xt_banks = [b_[:, :].bitcast(F16).rearrange("p (a c) -> p a c", a=2 * KC) for b_ in (pt_bank, pg[0])]
        score_banks = [pu[1], pg[1], pa[0], pa[1]]
        turn_banks = [pa[0], pa[1], pt_bank, pg[0]]
        y_banks = [py, pu[0]]
        xt_ps = pt_bank[:, :].bitcast(F16).rearrange("p (a c) -> p a c", a=2 * KC)

        waits_apart = {}
        sp_tick, pool_tick = sem("sp_tick", False), sem("pool_tick", False)
        ready = sem("ready", False)
        const_ok = sem("const_ok", False)
        pool_c = sem("pool_c", False)
        small_ld = sem("small_ld", False)
        cst_act = sem("cst_act", False)
        cst_ok = sem("cst_ok", False)
        gw_ok = sem("gw_ok", False)
        gw_hi = sem("gw_hi", False)
        pad_st = sem("pad_st", False)
        w_ld = [sem(f"w_ld{n}") for n in range(RING)]
        w_hi, w_lo = sem("w_hi"), sem("w_lo")
        w_scaled = sem("w_scaled")
        x_ld, ctx_ld = sem("x_ld"), sem("ctx_ld")
        qk_mm, qk_sb = sem("qk_mm"), sem("qk_sb")
        lg_mm = sem("lg_mm")
        sim_mm, sim_sb, tanh_sb = sem("sim_mm"), sem("sim_sb"), sem("tanh_sb")
        sig_sb, xn_sb, xa_made = sem("sig_sb"), sem("xn_sb"), sem("xa_made")
        stats_ok, x_stats_ok, guess_ok, base_ok, base_sb = sem("stats_ok"), sem("x_stats_ok"), sem("guess_ok"), sem("base_ok"), sem("base_sb")
        cur_ok, cnt_sb = sem("cur_ok", False), sem("cnt_sb")
        miss_ok, miss_mm = sem("miss_ok"), sem("miss_mm")
        a_made, at_mm, x1_made = sem("a_made"), sem("at_mm"), sem("x1_made")
        x1_st, ln_stats, ln_ok = sem("x1_st"), sem("ln_stats"), sem("ln_ok")
        xn_hi, xn_lo, xn_st = sem("xn_hi"), sem("xn_lo"), sem("xn_st")
        xt_mm, xt_sb = sem("xt_mm"), sem("xt_sb")
        up_mm, sil_sb, hid_sb = sem("up_mm"), sem("sil_sb"), sem("hid_sb")
        hid_mm, hhi_sb, hlo_sb = sem("hid_mm"), sem("hhi_sb"), sem("hlo_sb")
        down_mm, y_sb = sem("down_mm"), sem("y_sb")
        lg_sb = sem("lg_sb")
        x1_ld, sh_st = [sem("x1_ld0"), sem("x1_ld1")], sem("sh_st")
        pool_ch = sem("pool_ch", False)
        dve_ch = sem("dve_ch", False)
        fb_ch = sem("fb_ch", False)
        exp_ok, route_mm, route_ok = sem("exp_ok", False), sem("route_mm", False), sem("route_ok", False)
        z_ok = sem("z_ok", False)
        warm_ok = sem("warm_ok", False)
        wqk_ld = sem("wqk_ld", False)
        hid_pad = sem("hid_pad", False)
        hot_ok, hot_mm, table_ok = sem("hot_ok", False), sem("hot_mm", False), sem("table_ok", False)
        g_ld = [sem("g_ld0", False), sem("g_ld1", False)]
        idx_c = sem("idx_c", False)
        y_add = sem("y_add", False)
        rows_free = sem("rows_free")

        def after(eng, s, n):
            eng.wait_ge(s, n + CREDIT)
            if waits_apart.get(eng) is not None:
                eng.sem_inc(waits_apart[eng], 1)

        Q0 = BATCHES * UPS

        class Order:

            def __init__(self, eng, s):
                self.eng, self.s, self.n = eng, s, 0

            def mark(self, ins):
                self.n += 1
                ins.then_inc(self.s, 1)
                return self.n

            def wait(self, n=None):
                self.eng.wait_ge(self.s, self.n if n is None else n)

            def then(self, ins):
                self.mark(ins)
                self.wait()

            def clear(self):
                if self.n:
                    self.wait()
                self.eng.sem_clear(self.s)
                self.n = 0

        block = ctx.enter_context(nc.Block())

        @block.sync
        def _(sp):
            waits_apart[sp] = sp_tick
            sp.wait_ge(ready, 1)

            def load_piece(item, n):
                after(sp, w_lo, item * CHUNKS + n - RING + 1)
                sp.dma_start(stage[:, n % RING, :], weights[ds(item, 1), :, n * CHUNK_W:(n + 1) * CHUNK_W]
                             .rearrange("a p c -> (a p) c")).then_inc(w_ld[n % RING], 16)

            def load_item(item):
                for n in range(CHUNKS):
                    load_piece(item, n)

            def load_context(b, tile0):
                after(sp, sim_mm, tile0)
                sp.dma_start(ctx_b, ctx_t[:, ds(b * SEQ, SEQ)]).then_inc(ctx_ld, 16)

            def load_x(tile0):
                after(sp, x1_st, tile0 * 16)
                after(sp, xn_sb, tile0)
                sp.dma_start(xb, x_tiles[:, ds(tile0, TPB), :]).then_inc(x_ld, 16)

            def store_attended(tile0):
                for i in range(TPB):
                    after(sp, x1_made, tile0 + i + 1)
                    sp.dma_start(out_tiles[:, ds(tile0 + i, 1), :], xb[:, i:i + 1, :]).then_inc(x1_st, 16)
                for i in range(TPB):
                    after(sp, xn_lo, tile0 + i + 1)
                    after(sp, xn_hi, tile0 + i + 1)
                    sp.dma_start(xn_tiles[:, ds(tile0 + i, 1), :], xnr[:, i:i + 1, :]).then_inc(xn_st, 16)

            def reload(tile0, i):
                after(sp, x1_st, (tile0 + TPB) * 16)
                after(sp, sh_st, (tile0 + i - 1) * 16)
                sp.dma_start(rows[:, i % 2:i % 2 + 1, :], out_tiles[:, ds(tile0 + i, 1), :]).then_inc(x1_ld[i % 2], 16)

            def store_shared(tile0, i):
                after(sp, y_sb, tile0 + i + 1)
                sp.dma_start(out_tiles[:, ds(tile0 + i, 1), :], rows[:, i % 2:i % 2 + 1, :]).then_inc(sh_st, 16)

            load_context(0, 0)
            sp.dma_start(wq_s, wq_t).then_inc(wqk_ld, 16)
            sp.dma_start(wk_s, wk_t).then_inc(wqk_ld, 16)
            load_x(0)
            sp.dma_start(gcol[:], gates.rearrange("(a n) -> a n", a=1).partition_broadcast(P)
                         .rearrange("p a n -> p (a n)")).then_inc(small_ld, 16)
            sp.dma_start(gw_f, gate_wt).then_inc(small_ld, 16)
            sp.dma_start(bias_b[:], gate_bias.rearrange("(a n) -> a n", a=1).partition_broadcast(P)
                         .rearrange("p a n -> p (a n)")).then_inc(small_ld, 16)
            for n in range(RING):
                load_piece(0, n)
            sp.wait_ge(const_ok, 1)
            sp.wait_ge(warm_ok, 1)
            sp.dma_start(out_tiles[:, TILES, :], rows[:, 0, :]).then_inc(pad_st, 16)
            sp.dma_start(xn_tiles[:, TILES, :], rows[:, 0, :].bitcast(F16)).then_inc(pad_st, 16)
            for k in range(RING, BEFORE * CHUNKS):
                load_piece(k // CHUNKS, k % CHUNKS)
            sp.wait_ge(pad_st, 32)
            load_context(1, TPB)
            store_attended(0)
            load_x(TPB)

            def together(b, more):
                tile0, tile1, tile2 = (sp.snap((b + n) * TPB) if more else (b + n) * TPB for n in range(3))
                later = sp.snap(b + 2) if more else None
                item = sp.snap(b + BEFORE) if more else b + BEFORE
                for n in range(RING):
                    load_piece(item, n)
                reload(tile0, 0)
                reload(tile0, 1)
                if more:
                    load_context(later, tile2)
                for n in range(RING, CHUNKS):
                    load_piece(item, n)
                for i in range(TPB):
                    store_shared(tile0, i)
                    if i + 2 < TPB:
                        reload(tile0, i + 2)
                store_attended(tile1)
                if more:
                    load_x(tile2)

            with sp.Fori(0, BATCHES - 2) as b:
                together(b, True)
            together(BATCHES - 2, False)
            tile0 = TILES - TPB
            reload(tile0, 0)
            reload(tile0, 1)
            load_item(EARLY - 1)
            after(sp, x1_st, TILES * 16)
            after(sp, xn_st, TILES * 16)
            after(sp, xt_mm, TILES)
            load_item(EARLY)
            load_item(EARLY + 1)
            for n in range(RING):
                load_piece(ITEMS - 1, n)
            store_shared(tile0, 0)
            reload(tile0, 2)
            store_shared(tile0, 1)
            reload(tile0, 3)
            store_shared(tile0, 2)
            store_shared(tile0, 3)
            sp.wait_ge(pad_st, 32)
            after(sp, x1_st, TILES * 16)
            after(sp, sh_st, TILES * 16)
            after(sp, rows_free, SLOT_TILES)

        @block.gpsimd
        def _(pool):
            waits_apart[pool] = pool_tick
            for s in credited:
                pool.sem_inc(s, CREDIT)
            pool.sem_inc(ready, 1)
            c = Order(pool, pool_c)
            pool.memset(rows[:, 0, :], 0.0).then_inc(const_ok, 1)
            c.mark(pool.memset(ident[:], 0.0))
            c.mark(pool.memset(ident16[:], 0.0))
            c.mark(pool.memset(ones[:], 1.0))
            c.mark(pool.memset(tri[:], 0.0))
            c.mark(pool.memset(half_pow[:, 0, :], 0.5))
            c.mark(pool.memset(half_pow[:, 1, :], -0.5))
            c.mark(pool.iota(iota_col[:], pattern=[[1, P]], base=0, channel_multiplier=0, allow_small_or_imprecise_dtypes=True))
            c.mark(pool.memset(one1[:], 1.0))
            c.mark(pool.iota(iota_p[:], pattern=[[1, 1]], base=0, channel_multiplier=1, allow_small_or_imprecise_dtypes=True))
            c.mark(pool.iota(first[:], pattern=[[-1, EXPERTS]], base=EXPERTS, channel_multiplier=0, allow_small_or_imprecise_dtypes=True))
            c.wait()
            for m in (ident, ident16):
                c.mark(pool.affine_select(out=m[:], in_=m[:], compare_op=ALU.not_equal, fill=1.0, base=0,
                                          pattern=[[-1, P]], channel_multiplier=1))
            c.mark(pool.affine_select(out=tri[:], in_=tri[:], compare_op=ALU.is_ge, fill=1.0, base=0,
                                      pattern=[[-1, P]], channel_multiplier=1))
            c.wait()
            pool.sem_inc(const_ok, 1)

            pool.wait_ge(cst_ok, 1)
            sd, var_e, rstd, step = pt[:, 0, :], pt[:, 1, :], pt[:, 2, :], pt[:, 3, :]
            o = Order(pool, pool_ch)

            def guess(b):
                after(pool, stats_ok, b + 1)
                after(pool, cnt_sb, b * ROUNDS * (TPB // 2))
                mean_s, var_s = mv[:, 0, :, 0], mv[:, 0, :, 1]
                o.then(pool.tensor_tensor(sd, var_s, half_pow[:, 0, :], ALU.pow))
                for dst, z in ((cur, 0.5077), (lo, -0.2), (hi, 1.2)):
                    o.then(pool.tensor_scalar(step, sd, z, None, ALU.mult))
                    o.then(pool.tensor_tensor(dst[:, 0, :], step, mean_s, ALU.add))
                o.mark(pool.memset(lo[:, 1, :], 290.0))
                o.then(pool.memset(hi[:, 1, :], 60.0))
                pool.sem_inc(guess_ok, 1)

            def base_scalars(b):
                after(pool, x_stats_ok, b + 1)
                after(pool, base_sb, b * TPB)
                mean_x, var_x = mv[:, 1, :, 0], mv[:, 1, :, 1]
                o.then(pool.tensor_scalar(var_e, var_x, LN_EPS, None, ALU.add))
                o.then(pool.tensor_tensor(rstd, var_e, half_pow[:, 1, :], ALU.pow))
                gain, shift = pt[:, 4, :], pt[:, 5, :]
                o.then(pool.tensor_scalar(step, rstd, cst[:, 3:4], None, ALU.mult))
                o.mark(pool.tensor_scalar(gain, step, 1.0, None, ALU.add))
                o.then(pool.tensor_tensor(shift, step, mean_x, ALU.mult))
                o.then(pool.tensor_scalar(shift, shift, -1.0, None, ALU.mult))
                pool.sem_inc(base_ok, 1)

            def add_attention(b):
                for i in range(TPB):
                    after(pool, base_sb, b * TPB + i + 1)
                    after(pool, a_made, b * TPB + i + 1)
                    pool.tensor_tensor(xb[:, i, :], xb[:, i, :], att[:, i, :], ALU.add).then_inc(xa_made, 1)

            def row_scalars(b, more):
                after(pool, ln_stats, b + 1)
                after(pool, xn_sb, b * TPB)
                gain2, shift2 = pt[:, 6, :], pt[:, 7, :]
                mean_2, var_2 = mv[:, 2, :, 0], mv[:, 2, :, 1]
                o.then(pool.tensor_scalar(var_e, var_2, X_SCALE ** -2, LN_EPS * X_SCALE ** -2, ALU.mult, ALU.add))
                o.mark(pool.tensor_scalar(step, mean_2, -1.0, None, ALU.mult))
                o.then(pool.tensor_tensor(gain2, var_e, half_pow[:, 1, :], ALU.pow))
                o.then(pool.tensor_tensor(shift2, gain2, step, ALU.mult))
                pool.sem_inc(ln_ok, 1)
                if more:
                    guess(b + 1)
                o.clear()

            def low_piece(item, n):
                after(pool, w_hi, item * CHUNKS + n + 1)
                after(pool, w_scaled, item * CHUNKS + n + 1)
                pool.tensor_tensor(w[:, ds(item, 1), 1, n * CHUNK_W:(n + 1) * CHUNK_W], stage[:, n % RING:n % RING + 1, :],
                                   w[:, ds(item, 1), 0, n * CHUNK_W:(n + 1) * CHUNK_W], ALU.subtract).then_inc(w_lo, 1)

            guess(0)
            base_scalars(0)
            for item in range(BEFORE):
                for n in range(CHUNKS):
                    low_piece(item, n)
            add_attention(0)
            row_scalars(0, True)

            def together(b, more):
                base_scalars(b + 1)
                for n in range(CHUNKS):
                    low_piece(b + BEFORE, n)
                add_attention(b + 1)
                row_scalars(b + 1, more)

            with pool.Fori(0, BATCHES - 2) as b:
                together(b, True)
            together(BATCHES - 2, False)
            for item in range(EARLY - 1, ITEMS - 1):
                for n in range(CHUNKS):
                    low_piece(item, n)

            def gather(t, p):
                pool.sem_clear(idx_c)
                pool.tensor_copy(idx_g[:, p:p + 1], idx[:, ds(t, 1)]).then_inc(idx_c, 1)
                pool.wait_ge(idx_c, 1)
                pool.indirect_dma_start(out=xg[:, p, :], out_offset=None, in_=xn_rows,
                                        in_offset=bass.IndirectOffsetOnAxis(ap=idx_g[:, p:p + 1], axis=0)).then_inc(g_ld[p], 16)

            def add_rows(t, p):
                after(pool, y_sb, TILES + t + 1)
                pool.sem_clear(idx_c)
                pool.tensor_copy(idx_s[:, p:p + 1], idx[:, ds(t, 1)]).then_inc(idx_c, 1)
                pool.wait_ge(idx_c, 1)
                pool.indirect_dma_start(out=out, out_offset=bass.IndirectOffsetOnAxis(ap=idx_s[:, p:p + 1], axis=0),
                                        in_=rows[:, p, :], in_offset=None, compute_op=ALU.add).then_inc(y_add, 16)

            def rows_added(t):
                pool.wait_ge(y_add, (t + 1) * 16)
                pool.sem_inc(rows_free, 1)

            def pool_tile(t, p, before):
                after(pool, xt_mm, TILES + t + 2)
                gather(t + 3, 1 - p)
                if before is not None:
                    rows_added(before)
                add_rows(t, p)

            pool.wait_ge(table_ok, 1)
            pool.wait_ge(pad_st, 32)
            after(pool, xn_st, TILES * 16)
            gather(0, 0)
            gather(1, 1)
            for n in range(CHUNKS):
                low_piece(ITEMS - 1, n)
            after(pool, y_sb, TILES)
            pool.memset(hid[:, :, H:HP], 0.0).then_inc(hid_pad, 1)
            after(pool, sh_st, TILES * 16)
            after(pool, xt_mm, TILES + 1)
            gather(2, 0)
            pool_tile(0, 0, None)
            with pool.Fori(0, SLOT_TILES // 2 - 1) as i:
                pool_tile(i * 2 + 1, 1, i * 2)
                pool_tile(i * 2 + 2, 0, i * 2 + 1)
            t = SLOT_TILES - 2
            pool_tile(t, 1, t - 1)
            rows_added(t)
            add_rows(t + 1, 0)
            rows_added(t + 1)

        @block.scalar
        def _(act):
            act.wait_ge(ready, 1)
            act.wait_ge(const_ok, 1)
            act.activation(warm[:], rows[:, 0, 0:1], ACT.Silu).then_inc(warm_ok, 1)
            act.wait_ge(small_ld, 16 * SMALL)
            act.activation(cst[:, 0:2], gcol[:, 0:2], ACT.Tanh).then_inc(cst_act, 1)
            act.activation(cst[:, 2:3], gcol[:, 2:3], ACT.Tanh, scale=0.5).then_inc(cst_act, 1)
            act.activation(gw[:, :, 0, :], gw_f, ACT.Copy, scale=W_SCALE).then_inc(gw_hi, 1)

            def high_piece(item, n):
                after(act, w_ld[n % RING], (item * (CHUNKS // RING) + n // RING + 1) * 16)
                act.activation(w[:, ds(item, 1), 0, n * CHUNK_W:(n + 1) * CHUNK_W], stage[:, n % RING:n % RING + 1, :],
                               ACT.Copy, scale=W_SCALE).then_inc(w_hi, 1)
                after(act, w_hi, item * CHUNKS + n + 1)
                act.activation(stage[:, n % RING, :], stage[:, n % RING, :], ACT.Copy, scale=W_SCALE).then_inc(w_scaled, 1)

            def keep_qk(b):
                after(act, sim_mm, b * TPB)
                after(act, qk_mm, b * 2 + 2)
                for n, dst in enumerate((q_t, k_t)):
                    act.activation(dst, score_banks[n][:, :], ACT.Copy).then_inc(qk_sb, 1)

            def keep_scores(b, i):
                after(act, a_made, b * TPB)
                after(act, at_mm, b * TPB)
                after(act, xa_made, b * TPB)
                after(act, sim_mm, b * TPB + i + 1)
                act.activation(sim[:, i, :], score_banks[i][:, :], ACT.Copy).then_inc(sim_sb, 1)
                act.activation(att[:, i, :], score_banks[i][:, :], ACT.Tanh, scale=0.5 * SIM_SCALE).then_inc(tanh_sb, 1)

            def scaled_sigmoid(b, i):
                after(act, tanh_sb, b * TPB + i + 1)
                act.activation(att[:, i, :], att[:, i, :], ACT.Identity, bias=cst[:, 4:5], scale=cst[:, 4:5]).then_inc(sig_sb, 1)

            def base(b):
                after(act, base_ok, b + 1)
                for i in range(TPB):
                    act.activation(xb[:, i, :], xb[:, i, :], ACT.Identity, bias=pt[:, 5, i:i + 1],
                                   scale=pt[:, 4, i:i + 1]).then_inc(base_sb, 1)

            def count(b, n):
                act.wait_ge(cur_ok, b * ROUNDS + n + 1)
                for i in range(TPB // 2, TPB):
                    act.activation(junk[:, i, :], sim[:, i, :], ACT.Sign, bias=cur[:, 0, i:i + 1], scale=-1.0,
                                   accum_out=acc[:, i - TPB // 2:i - TPB // 2 + 1]).then_inc(cnt_sb, 1)

            def normalised(b, i):
                if i == 0:
                    after(act, ln_ok, b + 1)
                    after(act, xn_st, b * TPB * 16)
                    after(act, xt_mm, b * TPB)
                after(act, xn_lo, b * TPB + i - 1)
                act.activation(xn[:, i % 2, :], xb[:, i, :], ACT.Identity, bias=pt[:, 7, i:i + 1],
                               scale=pt[:, 6, i:i + 1]).then_inc(xn_sb, 1)
                after(act, xn_sb, b * TPB + i + 1)
                act.activation(xnr[:, i, 0:C], xn[:, i % 2, :], ACT.Copy).then_inc(xn_hi, 1)

            def keep_logits(b):
                after(act, xt_sb, (b + 1) * TPB)
                after(act, lg_mm, b + 1)
                act.activation(lg[:, ds(b * TPB, TPB), :, :],
                               pt_bank[:, 0:TPB * 2 * EXPERTS].rearrange("p (t a e) -> p t a e", t=TPB, a=2), ACT.Copy).then_inc(lg_sb, 1)

            def shared_silu(b, u):
                q, m = b * UPS + u, PIECES[u][2]
                after(act, up_mm, q + 1)
                after(act, hlo_sb, q - 1)
                act.activation(hb[0:m, u % 2, :], pg[u % 2][0:m, :], ACT.Silu, scale=UP_UNSCALE).then_inc(sil_sb, 1)

            def shared_high(b, u):
                q, m = b * UPS + u, PIECES[u][2]
                after(act, hid_sb, q + 1)
                after(act, down_mm, b * TPB)
                act.activation(hid_tb[0:m, u, 0, :], hb[0:m, u % 2, :], ACT.Copy).then_inc(hhi_sb, 1)

            def scores_and_rows(b, more):
                if more:
                    keep_qk(b + 1)
                    for i in range(TPB):
                        keep_scores(b + 1, i)
                for i in range(TPB):
                    normalised(b, i)

            keep_qk(0)
            for i in range(TPB):
                keep_scores(0, i)
            act.wait_ge(cst_ok, 1)
            for i in range(TPB):
                scaled_sigmoid(0, i)
            step = 3
            for n in range(ROUNDS):
                count(0, n)
                if n == 0:
                    base(0)
                for k in range(step * n, step * n + step):
                    high_piece(k // CHUNKS, k % CHUNKS)
            for k in range(step * ROUNDS, BEFORE * CHUNKS):
                high_piece(k // CHUNKS, k % CHUNKS)
            scores_and_rows(0, True)

            def together(b, more):
                count(b + 1, 0)
                keep_logits(b)
                count(b + 1, 1)
                for u in range(UPS):
                    shared_silu(b, u)
                    if u + 2 < ROUNDS:
                        count(b + 1, u + 2)
                    shared_high(b, u)
                    if u < TPB:
                        scaled_sigmoid(b + 1, u)
                        for n in range(u * CHUNKS // TPB, (u + 1) * CHUNKS // TPB):
                            high_piece(b + BEFORE, n)
                    if u == 2:
                        base(b + 1)
                scores_and_rows(b + 1, more)

            with act.Fori(0, BATCHES - 2) as b:
                together(b, True)
            together(BATCHES - 2, False)
            def router_exp():
                act.wait_ge(z_ok, 1)
                act.activation(r[1][:], r[0][:], ACT.Exp, scale=-UP_UNSCALE).then_inc(exp_ok, 1)

            keep_logits(BATCHES - 1)
            after(act, x1_st, TILES * 16)
            after(act, xn_st, TILES * 16)
            after(act, xt_mm, TILES)
            for u in range(UPS):
                if u == 0:
                    router_exp()
                shared_silu(BATCHES - 1, u)
                for n in range(u * PER_STEP, (u + 1) * PER_STEP):
                    if n - u * PER_STEP == PER_STEP // 2:
                        shared_high(BATCHES - 1, u)
                    if n < 3 * CHUNKS:
                        high_piece(EARLY - 1 + n // CHUNKS, n % CHUNKS)
            act.wait_ge(table_ok, 1)
            after(act, up_mm, BATCHES * UPS)
            for n in range(RING):
                high_piece(ITEMS - 1, n)
            for n in range(RING, CHUNKS):
                after(act, w_lo, (ITEMS - 1) * CHUNKS + n - RING + 1)
                act.dma_start(stage[:, n % RING, :], weights[ITEMS - 1, :, n * CHUNK_W:(n + 1) * CHUNK_W]).then_inc(w_ld[n % RING], 16)
            for n in range(RING, CHUNKS):
                high_piece(ITEMS - 1, n)

            def silu(t, p):
                after(act, up_mm, Q0 + t + 1)
                after(act, hid_sb, Q0 + t - 1)
                act.activation(sil[:, p, :], pg[p][:, 0:H], ACT.Silu, scale=UP_UNSCALE).then_inc(sil_sb, 1)

            def hidden_high(t, p):
                after(act, hid_mm, t + 1)
                after(act, down_mm, TILES + t - 1)
                act.activation(hid_t[:, p, 0, :], pt_bank[:, 0:HP], ACT.Copy).then_inc(hhi_sb, 1)

            def expert_rows(t, p):
                after(act, down_mm, TILES + t + 1)
                after(act, rows_free, t - 1)
                act.activation(rows[:, p, :], py[:, :], ACT.Copy, scale=w_slot[:, ds(t, 1)]).then_inc(y_sb, 1)

            silu(0, 0)
            with act.Fori(0, SLOT_TILES // 2) as i:
                for k in range(2):
                    t = i * 2 + k + 1
                    hidden_high(t - 1, k)
                    silu(t, 1 - k)
                    expert_rows(t - 1, k)
            hidden_high(SLOT_TILES - 1, 0)
            expert_rows(SLOT_TILES - 1, 0)

        @block.tensor
        def _(pe):
            pe.wait_ge(ready, 1)
            pe.wait_ge(wqk_ld, 32)

            def project(b, shared):
                after(pe, ctx_ld, (b + 1) * 16)
                after(pe, tanh_sb, b * TPB)
                if shared is not None:
                    after(pe, hid_sb, (shared + 1) * UPS)
                for n, m in enumerate((wq_s, wk_s)):
                    pe.matmul(score_banks[n][:, :], m, ctx_b, start=True, stop=True).then_inc(qk_mm, 1)

            def scores(b, i):
                after(pe, qk_sb, (b + 1) * 2)
                if i >= 2:
                    after(pe, x1_made, b * TPB - TPB + i - 1)
                pe.matmul(score_banks[i][:, :], q_t[:, i * P:(i + 1) * P], k_t, start=True, stop=True).then_inc(sim_mm, 1)

            def missed_rows(b):
                after(pe, miss_ok, b + 1)
                after(pe, tanh_sb, (b + 1) * TPB)
                pe.matmul(pa[0][0:1, 0:1], missed[:], one1[:], start=True, stop=True).then_inc(miss_mm, 1)

            def turn_attention(b):
                after(pe, lg_sb, b)
                after(pe, hid_sb, b * UPS)
                after(pe, a_made, (b + 1) * TPB)
                for i in range(TPB):
                    for j in range(TPB):
                        mm = pe.transpose(turn_banks[i][:, j * P:(j + 1) * P], att[:, j, i * P:(i + 1) * P], ident[:])
                    mm.then_inc(at_mm, 1)

            def turn_rows(src, bank_):
                for n in range(2 * KC):
                    mm = pe.transpose(bank_[:, n, :], src[:, n * P:(n + 1) * P], ident16[:])
                mm.then_inc(xt_mm, 1)

            def turn_batch(b):
                after(pe, lg_sb, b)
                after(pe, hid_sb, b * UPS)
                for i in range(TPB):
                    after(pe, xn_hi, b * TPB + i + 1)
                    after(pe, xn_lo, b * TPB + i + 1)
                    after(pe, xt_sb, b * TPB + i - 1)
                    turn_rows(xnr[:, i, :], xt_banks[i % 2])

            def logits(b):
                after(pe, xt_sb, (b + 1) * TPB)
                for i in range(TPB):
                    at = i * 2 * EXPERTS
                    for k in range(KC):
                        for part in range(2):
                            n = (2 - part) * EXPERTS
                            mm = pe.matmul(pt_bank[:, at:at + n], x_tb[:, part * KC + k, i * P:(i + 1) * P],
                                           gw[:, k, 0:2 - part, :].rearrange("p a e -> p (a e)"),
                                           start=(i, k, part) == (0, 0, 0), stop=(k, part) == (KC - 1, 1), skip_group_check=True)
                mm.then_inc(lg_mm, 1)

            def shared_up(b, u, beside=None):
                half, off, m = PIECES[u]
                if u == 1 and beside is not None:
                    after(pe, tanh_sb, (beside + 1) * TPB)
                if u == 0:
                    after(pe, y_sb, b * TPB)
                after(pe, hid_sb, b * UPS + u - 1)
                for k in range(KC):
                    for bank_, at in ((pg[u % 2], k * 2 * H + off), (pu[u % 2], k * 2 * H + H + off)):
                        for part, xpart in ((0, 0), (0, 1), (1, 0)):
                            mm = pe.matmul(bank_[0:m, :], w[:, half, part, at:at + m], x_tb[:, xpart * KC + k, :],
                                           start=(k, part, xpart) == (0, 0, 0), stop=(k, part) == (KC - 1, 1))
                mm.then_inc(up_mm, 1)

            def shared_down(b, i):
                if i >= 2:
                    after(pe, y_sb, b * TPB + i - 1)
                else:
                    after(pe, y_sb, b * TPB)
                for u, (half, off, m) in enumerate(PIECES):
                    after(pe, hhi_sb, b * UPS + u + 1)
                    after(pe, hlo_sb, b * UPS + u + 1)
                    at = UP_W + off // P * C
                    for part, wpart in ((0, 0), (0, 1), (1, 0)):
                        mm = pe.matmul(y_banks[i % 2][:, :], hid_tb[0:m, u, part, i * P:(i + 1) * P],
                                       w[0:m, half, wpart, at:at + C],
                                       start=(u, part, wpart) == (0, 0, 0), stop=(u, part) == (UPS - 1, 1))
                mm.then_inc(down_mm, 1)

            project(0, None)
            for i in range(TPB):
                scores(0, i)
            pe.wait_ge(const_ok, 2)
            missed_rows(0)
            project(1, None)
            turn_attention(0)
            for i in range(TPB):
                scores(1, i)
            turn_batch(0)
            after(pe, w_lo, HALVES * CHUNKS)
            after(pe, w_hi, HALVES * CHUNKS)
            pe.wait_ge(gw_ok, 1)

            def together(b, more):
                logits(b)
                for u in range(UPS):
                    shared_up(b, u, b + 1)
                for i in range(TPB):
                    if i == 2:
                        missed_rows(b + 1)
                    shared_down(b, i)
                if more:
                    project(b + 2, b)
                turn_attention(b + 1)
                if more:
                    for i in range(TPB):
                        scores(b + 2, i)
                turn_batch(b + 1)

            with pe.Fori(0, BATCHES - 2) as b:
                together(b, True)
            together(BATCHES - 2, False)

            def ranks():
                pe.wait_ge(route_ok, 1)
                sel = r[2][:].rearrange("p t e -> p (t e)")
                pe.matmul(pa[0][:, 0:P], tri[:], sel, start=True, stop=True).then_inc(route_mm, 1)
                pe.matmul(pa[1][:, 0:P], ones[:], sel, start=True, stop=True).then_inc(route_mm, 1)

            def slots(begin, end):
                pe.wait_ge(route_ok, 2)
                for n in range(begin, end):
                    pe.wait_ge(hot_ok, 3 * (n // SLOTS_STEP + 1))
                    pe.matmul(pa[0][:, 0:2 * SLOT_COLS], hot_col[:, n % SLOTS_STEP, :],
                              hot_val[:, n % SLOTS_STEP, :, :].rearrange("p v c -> p (v c)"),
                              start=(n == 0), stop=(n == TOPK * TILES - 1), skip_group_check=True).then_inc(hot_mm, 1)

            logits(BATCHES - 1)
            for u in range(UPS):
                shared_up(BATCHES - 1, u)
                if u == 0:
                    ranks()
                if u >= 3:
                    slots((u - 3) * SLOTS_STEP, (u - 2) * SLOTS_STEP)
            slots((UPS - 3) * SLOTS_STEP, (UPS - 2) * SLOTS_STEP)
            for i in range(TPB):
                shared_down(BATCHES - 1, i)

            pe.wait_ge(table_ok, 1)
            after(pe, w_lo, ITEMS * CHUNKS)
            after(pe, w_hi, ITEMS * CHUNKS)
            def up(t, p, item, ks):
                if 0 in ks:
                    after(pe, hid_sb, Q0 + t - 1)
                    after(pe, xt_sb, TILES + t + 1)
                for k in ks:
                    at = k * 2 * H
                    for part in range(2):
                        lhs = x_t[:, p, part * KC + k, :]
                        for half in range(2 - part):
                            begin, end = (k, part, half) == (0, 0, 0), (k, part) == (KC - 1, 1)
                            pe.matmul(pg[p][:, 0:H], lhs, w[:, item, half, at:at + H], start=begin, stop=end)
                            mm = pe.matmul(pu[p][:, 0:H], lhs, w[:, item, half, at + H:at + 2 * H], start=begin, stop=end)
                if KC - 1 in ks:
                    mm.then_inc(up_mm, 1)

            def turn_hidden(t, p):
                after(pe, hid_sb, Q0 + t + 1)
                after(pe, xt_sb, TILES + t + 3)
                for j in range(JC):
                    mm = pe.transpose(pt_bank[:, j * P:(j + 1) * P], hid[:, p, j * P:(j + 1) * P], ident[:])
                mm.then_inc(hid_mm, 1)

            def down(t, p, item):
                after(pe, hhi_sb, Q0 + t + 1)
                after(pe, hlo_sb, Q0 + t + 1)
                after(pe, y_sb, TILES + t)
                for j in range(JC):
                    at = UP_W + j * C
                    for part in range(2):
                        for half in range(2 - part):
                            mm = pe.matmul(py[:, :], hid_t[:, p, part, j * P:(j + 1) * P], w[:, item, half, at:at + C],
                                           start=(j, part, half) == (0, 0, 0), stop=(j, part) == (JC - 1, 1))
                mm.then_inc(down_mm, 1)

            def turn_gathered(t, p, n, q):
                pe.wait_ge(g_ld[p], (n + 1) * 16)
                after(pe, hhi_sb, q)
                after(pe, hlo_sb, q)
                turn_rows(xg[:, p, :], xt_ps)

            def item_of(t):
                return pe.value_load(tile_e[0:1, ds(t, 1)], min_val=HALVES, max_val=ITEMS - 1)

            after(pe, y_sb, TILES)
            after(pe, lg_sb, BATCHES)
            turn_gathered(0, 0, 0, Q0)
            after(pe, xt_sb, TILES + 1)
            turn_gathered(1, 1, 0, Q0)
            e = item_of(0)
            up(0, 0, ds(e, 1), range(KC))
            after(pe, xt_sb, TILES + 2)
            turn_gathered(2, 0, 1, Q0)
            pe.wait_ge(hid_pad, 1)
            def expert_step(t, k, n, before):
                now = item_of(t)
                up(t, k, ds(now, 1), range(0, KC // 2))
                turn_hidden(t - 1, 1 - k)
                up(t, k, ds(now, 1), range(KC // 2, KC))
                down(t - 1, 1 - k, ds(item_of(t - 1) if before is None else before, 1))
                turn_gathered(t + 2, k, n, Q0 + t)
                return now

            STEP = 4
            loops = (SLOT_TILES - 1) // STEP
            with pe.Fori(0, loops) as i:
                before = None
                for k in range(STEP):
                    before = expert_step(i * STEP + k + 1, (k + 1) % 2, i * (STEP // 2) + 1 + (k + 1) // 2, before)
            before = None
            for t in range(loops * STEP + 1, SLOT_TILES):
                before = expert_step(t, t % 2, (t + 2) // 2, before)
            t = SLOT_TILES - 1
            turn_hidden(t, t % 2)
            down(t, t % 2, ds(before, 1))

        @block.vector
        def _(dve):
            dve.wait_ge(ready, 1)
            o = Order(dve, dve_ch)

            dve.wait_ge(cst_act, 2)
            o.then(dve.tensor_scalar(cst[:, 5:6], cst[:, 2:3], 0.5, 0.5, ALU.mult, ALU.add))
            o.mark(dve.tensor_scalar(cst[:, 6:7], cst[:, 5:6], -1.0, 1.0, ALU.mult, ALU.add))
            o.then(dve.tensor_tensor(cst[:, 7:8], cst[:, 5:6], cst[:, 0:1], ALU.mult))
            o.mark(dve.tensor_tensor(cst[:, 3:4], cst[:, 6:7], cst[:, 0:1], ALU.mult))
            o.mark(dve.tensor_scalar(cst[:, 4:5], cst[:, 7:8], 0.25, None, ALU.mult))
            o.then(dve.tensor_scalar(cst[:, 8:9], cst[:, 1:2], DOWN_UNSCALE, None, ALU.mult))
            dve.wait_ge(gw_hi, 1)
            dve.scalar_tensor_tensor(out=gw[:, :, 1, :], in0=gw_f, scalar=W_SCALE, in1=gw[:, :, 0, :],
                                     op0=ALU.mult, op1=ALU.subtract).then_inc(gw_ok, 1)
            dve.sem_inc(cst_ok, 1)
            dve.wait_ge(const_ok, 2)
            unscaled_tanh_ffn = cst[:, 8:9]

            def statistics(s):
                o.wait()
                for i in range(TPB):
                    o.mark(dve.bn_aggr(mv[:, s, i, :], bn6[:, s, i, :]))
                o.wait()

            def x_stats(b):
                after(dve, x_ld, (b + 1) * 16)
                for i in range(TPB):
                    o.mark(dve.bn_stats(bn6[:, 1, i, :], xb[:, i, :]))
                statistics(1)
                dve.sem_inc(x_stats_ok, 1)

            def score_stats(b):
                for i in range(TPB):
                    after(dve, sim_sb, b * TPB + i + 1)
                    o.mark(dve.bn_stats(bn6[:, 0, i, :], sim[:, i, :]))
                statistics(0)
                dve.sem_inc(stats_ok, 1)

            def interpolate(b, n):
                half = TPB // 2
                if n == 0:
                    after(dve, guess_ok, b + 1)
                dve.sem_inc(cur_ok, 1)
                for i in range(half):
                    o.mark(dve.tensor_scalar(junk[:, i, :], sim[:, i, :], cur[:, 0, i:i + 1], 0.0, ALU.is_ge, ALU.add,
                                             accum_out=cur[:, 1, i:i + 1]))
                after(dve, cnt_sb, (b * ROUNDS + n + 1) * half)
                o.then(dve.tensor_scalar(cur[:, 1, half:], acc[:], -0.5, SEQ / 2.0, ALU.mult, ALU.add))
                o.mark(dve.tensor_scalar(above[:], cur[:, 1, :], float(KEEP), None, ALU.is_ge))
                o.then(dve.tensor_scalar(below[:], cur[:, 1, :], float(KEEP), None, ALU.is_lt))
                o.mark(dve.copy_predicated(lo, above[:].unsqueeze(1).to_broadcast([P, 2, TPB]), cur))
                o.then(dve.copy_predicated(hi, below[:].unsqueeze(1).to_broadcast([P, 2, TPB]), cur))
                if n < ROUNDS - 1:
                    gap, frac, width = tmp4[:, 0, :], tmp4[:, 1, :], tmp4[:, 2, :]
                    o.mark(dve.tensor_tensor(gap, lo[:, 1, :], hi[:, 1, :], ALU.subtract))
                    o.then(dve.tensor_tensor(width, hi[:, 0, :], lo[:, 0, :], ALU.subtract))
                    o.then(dve.reciprocal(gap, gap))
                    o.then(dve.scalar_tensor_tensor(out=frac, in0=lo[:, 1, :], scalar=KEEP - 4.0, in1=gap,
                                                    op0=ALU.subtract, op1=ALU.mult))
                    o.then(dve.scalar_tensor_tensor(out=frac, in0=frac, scalar=0.98, in1=width, op0=ALU.min, op1=ALU.mult))
                    o.then(dve.tensor_tensor(cur[:, 0, :], frac, lo[:, 0, :], ALU.add))

            rank, miss = tmp4[:, 3, :], tmp4[:, 4, :]

            def thresholds(two):
                o.wait()
                made = [o.mark(dve.tensor_scalar(masked[:, i % 2, :], sim[:, i, :], hi[:, 0, i:i + 1], 0.0, ALU.is_ge, ALU.add,
                                                 accum_out=hi[:, 1, i:i + 1])) for i in two]
                for n, i in enumerate(two):
                    o.wait(made[n])
                    made[n] = o.mark(dve.scalar_tensor_tensor(out=masked[:, i % 2, :], in0=masked[:, i % 2, :], scalar=-BIG,
                                                              in1=sim[:, i, :], op0=ALU.mult, op1=ALU.add))
                o.mark(dve.tensor_scalar(rank[:, two[0]:two[1] + 1], hi[:, 1, two[0]:two[1] + 1], -1.0, KEEP - 1.0, ALU.mult, ALU.add))
                for n, i in enumerate(two):
                    o.wait(made[n])
                    made[n] = o.mark(dve.max(top8[:, i, :], masked[:, i % 2, :]))
                for n, i in enumerate(two):
                    o.wait(made[n])
                    o.mark(dve.scalar_tensor_tensor(out=pick8[:, i, :], in0=iota_col[:, 0:8], scalar=rank[:, i:i + 1],
                                                    in1=top8[:, i, :], op0=ALU.is_equal, op1=ALU.mult,
                                                    accum_out=thr[:, i:i + 1]))

            def count_missed():
                o.wait()
                o.then(dve.tensor_scalar(miss, rank, 0.0, None, ALU.is_lt))
                o.then(dve.scalar_tensor_tensor(out=miss, in0=rank, scalar=7.5, in1=miss, op0=ALU.is_gt, op1=ALU.add,
                                                accum_out=missed[:]))
                dve.sem_inc(miss_ok, 1)

            def masks(b):
                after(dve, miss_mm, b + 1)
                o.then(dve.tensor_copy(missed_i[:], pa[0][0:1, 0:1]))
                any_missed = dve.value_load(missed_i[0:1, 0:1], min_val=0, max_val=2 * P * TPB)
                with dve.If(any_missed > 0):
                    f = Order(dve, fb_ch)
                    f.clear()
                    for i in range(TPB):
                        f.then(dve.tensor_copy(masked[:, 0, :], sim[:, i, :]))
                        with dve.Fori(0, (KEEP - 1) // 8):
                            dve.sem_clear(fb_ch)
                            dve.max(top8[:, i, :], masked[:, 0, :]).then_inc(fb_ch, 1)
                            dve.wait_ge(fb_ch, 1)
                            dve.match_replace(out=masked[:, 0, :], in_to_replace=top8[:, i, :], in_values=masked[:, 0, :],
                                              imm_value=-BIG).then_inc(fb_ch, 1)
                            dve.wait_ge(fb_ch, 2)
                        f.n = 0
                        dve.sem_clear(fb_ch)
                        f.then(dve.max(top8[:, i, :], masked[:, 0, :]))
                        f.then(dve.tensor_copy(thr[:, i:i + 1], top8[:, i, (KEEP - 1) % 8:(KEEP - 1) % 8 + 1]))
                after(dve, sig_sb, (b + 1) * TPB)
                for i in range(TPB):
                    dve.scalar_tensor_tensor(out=att[:, i, :], in0=sim[:, i, :], scalar=thr[:, i:i + 1], in1=att[:, i, :],
                                             op0=ALU.is_ge, op1=ALU.mult).then_inc(a_made, 1)

            def attended(b, more):
                for i in range(TPB):
                    after(dve, xa_made, b * TPB + i + 1)
                    after(dve, at_mm, b * TPB + i + 1)
                    dve.tensor_tensor(xb[:, i, :], turn_banks[i][:, :], xb[:, i, :], ALU.add).then_inc(x1_made, 1)
                for i in range(TPB):
                    after(dve, x1_made, b * TPB + i + 1)
                    o.mark(dve.bn_stats(bn6[:, 2, i, :], xb[:, i, :]))
                statistics(2)
                dve.sem_inc(ln_stats, 1)
                if more:
                    score_stats(b + 1)
                after(dve, up_mm, b * UPS)
                for i in range(TPB):
                    after(dve, xn_hi, b * TPB + i + 1)
                    dve.tensor_tensor(xnr[:, i, C:2 * C], xn[:, i % 2, :], xnr[:, i, 0:C], ALU.subtract).then_inc(xn_lo, 1)
                    if i:
                        rows_turned(b, i - 1)
                rows_turned(b, TPB - 1)
                o.clear()

            def rows_turned(b, i):
                after(dve, xt_mm, b * TPB + i + 1)
                dve.tensor_copy(x_tb[:, :, i * P:(i + 1) * P], xt_banks[i % 2]).then_inc(xt_sb, 1)

            def shared_hidden(b, u):
                q, m = b * UPS + u, PIECES[u][2]
                after(dve, sil_sb, q + 1)
                after(dve, up_mm, q + 1)
                dve.scalar_tensor_tensor(out=hb[0:m, u % 2, :], in0=pu[u % 2][0:m, :], scalar=UP_UNSCALE * H_SCALE,
                                         in1=hb[0:m, u % 2, :], op0=ALU.mult, op1=ALU.mult).then_inc(hid_sb, 1)

            def shared_low(b, u):
                q, m = b * UPS + u, PIECES[u][2]
                after(dve, hhi_sb, q + 1)
                dve.tensor_tensor(hid_tb[0:m, u, 1, :], hb[0:m, u % 2, :], hid_tb[0:m, u, 0, :], ALU.subtract).then_inc(hlo_sb, 1)

            def shared_rows(b, i):
                after(dve, down_mm, b * TPB + i + 1)
                after(dve, x1_ld[i % 2], (b * (TPB // 2) + i // 2 + 1) * 16)
                dve.scalar_tensor_tensor(out=rows[:, i % 2, :], in0=y_banks[i % 2][:, :], scalar=unscaled_tanh_ffn,
                                         in1=rows[:, i % 2, :], op0=ALU.mult, op1=ALU.add).then_inc(y_sb, 1)

            o.clear()
            score_stats(0)
            x_stats(0)
            for n in range(ROUNDS):
                interpolate(0, n)
            thresholds((0, 1))
            thresholds((2, 3))
            count_missed()
            masks(0)
            attended(0, True)

            def together(b, more):
                interpolate(b + 1, 0)
                x_stats(b + 1)
                interpolate(b + 1, 1)
                for u in range(UPS):
                    shared_hidden(b, u)
                    if u + 2 < ROUNDS:
                        interpolate(b + 1, u + 2)
                    if u + 2 == ROUNDS:
                        thresholds((0, 1))
                    shared_low(b, u)
                thresholds((2, 3))
                shared_rows(b, 0)
                count_missed()
                shared_rows(b, 1)
                masks(b + 1)
                shared_rows(b, 2)
                shared_rows(b, 3)
                attended(b + 1, more)

            with dve.Fori(0, BATCHES - 2) as b:
                together(b, True)
            together(BATCHES - 2, False)


            def bc(col):
                return col.unsqueeze(2).to_broadcast([P, TILES, EXPERTS])

            def over_tiles(row):
                return row.unsqueeze(1).to_broadcast([P, TILES, EXPERTS])

            score, cand, sel, hot1, hot2 = r[1][:], r[3][:], r[2][:], r[4][:], r[5][:]
            z, total, gate = r[0][:], r[1][:], slot_f[:, 0, :, :]

            def best(hot, col):
                o.then(dve.tensor_reduce(rc[:, col, :], cand, AX.X, ALU.max))
                o.then(dve.tensor_tensor(hot, cand, bc(rc[:, col, :]), ALU.is_equal))
                o.then(dve.tensor_tensor(hot, hot, over_tiles(first[:]), ALU.mult))
                o.then(dve.tensor_reduce(rc[:, col, :], hot, AX.X, ALU.max))
                o.then(dve.tensor_tensor(hot, over_tiles(first[:]), bc(rc[:, col, :]), ALU.is_equal))

            def sum_logits():
                after(dve, lg_sb, BATCHES)
                o.then(dve.tensor_tensor(r[0][:], lg[:, :, 0, :], lg[:, :, 1, :], ALU.add))
                dve.sem_inc(z_ok, 1)

            def choose():
                dve.wait_ge(exp_ok, 1)
                o.then(dve.tensor_scalar(score, score, 1.0, None, ALU.add))
                o.then(dve.reciprocal(score, score))
                o.then(dve.tensor_tensor(cand, score, over_tiles(bias_b[:]), ALU.add))

                best(hot1, 1)
                o.then(dve.scalar_tensor_tensor(out=cand, in0=hot1, scalar=-BIG, in1=cand, op0=ALU.mult, op1=ALU.add))
                best(hot2, 2)
                dve.tensor_tensor(sel, hot1, hot2, ALU.add).then_inc(route_ok, 1)
                for k, hot in enumerate((hot1, hot2)):
                    o.then(dve.tensor_tensor(z, score, hot, ALU.mult))
                    o.then(dve.tensor_reduce(rc[:, 3 + k, :], z, AX.X, ALU.add))
                o.then(dve.tensor_tensor(rc[:, 5, :], rc[:, 3, :], rc[:, 4, :], ALU.add))
                o.then(dve.reciprocal(rc[:, 5, :], rc[:, 5, :]))
                for k in range(TOPK):
                    o.then(dve.tensor_tensor(gate[:, k, :], rc[:, 3 + k, :], rc[:, 5, :], ALU.mult))

            def place():
                dve.wait_ge(route_mm, 2)
                o.then(dve.tensor_copy(total, pa[1][:, 0:P].rearrange("p (t e) -> p t e", t=TILES)))
                o.then(dve.tensor_copy(cand, total))
                a, c2 = cand, z
                step = 1
                while step < TILES:
                    o.mark(dve.tensor_copy(c2[:, 0:step, :], a[:, 0:step, :]))
                    o.then(dve.tensor_tensor(c2[:, step:, :], a[:, step:, :], a[:, :TILES - step, :], ALU.add))
                    a, c2 = c2, a
                    step *= 2
                o.then(dve.tensor_scalar(re8[:, 0, :], a[:, TILES - 1, :], float(P - 1), None, ALU.add))
                o.then(dve.tensor_copy(ri8[:], re8[:, 0, :]))
                o.then(dve.tensor_scalar(ri8[:], ri8[:], P.bit_length() - 1, None, ALU.logical_shift_right))
                o.then(dve.tensor_copy(re8[:, 0, :], ri8[:]))
                o.then(dve.tensor_copy(re8[:, 3, :], re8[:, 0, :]))
                ea, eb = re8[:, 3, :], re8[:, 1, :]
                step = 1
                while step < EXPERTS:
                    o.mark(dve.tensor_copy(eb[:, 0:step], ea[:, 0:step]))
                    o.then(dve.tensor_tensor(eb[:, step:], ea[:, step:], ea[:, :EXPERTS - step], ALU.add))
                    ea, eb = eb, ea
                    step *= 2
                ends = ea
                o.then(dve.tensor_tensor(re8[:, 2, :], ends, re8[:, 0, :], ALU.subtract))
                o.then(dve.tensor_scalar(re8[:, 2, :], re8[:, 2, :], float(P), None, ALU.mult))
                o.then(dve.tensor_tensor(a, a, total, ALU.subtract))
                o.then(dve.tensor_tensor(a, a, pa[0][:, 0:P].rearrange("p (t e) -> p t e", t=TILES), ALU.add))
                o.then(dve.tensor_tensor(a, a, over_tiles(re8[:, 2, :]), ALU.add))
                for k, hot in enumerate((hot1, hot2)):
                    o.then(dve.tensor_tensor(total, a, hot, ALU.mult))
                    o.then(dve.tensor_reduce(slot_f[:, 1, k, :], total, AX.X, ALU.add))
                o.then(dve.tensor_copy(slot_i[:, 0, :, :], slot_f[:, 1, :, :]))
                o.mark(dve.tensor_scalar(slot_i[:, 1, :, :], slot_i[:, 0, :, :], P.bit_length() - 1, None, ALU.logical_shift_right))
                o.then(dve.tensor_scalar(slot_i[:, 2, :, :], slot_i[:, 0, :, :], P - 1, None, ALU.bitwise_and))
                o.mark(dve.tensor_copy(slot_f[:, 1, :, :], slot_i[:, 1, :, :]))
                o.then(dve.tensor_copy(slot_f[:, 2, :, :], slot_i[:, 2, :, :]))
                o.then(dve.tensor_scalar(rc[:, 6, :], iota_tile[:, 0:TILES], float(P), iota_p[:, 0:1], ALU.mult, ALU.add))
                for k in range(TOPK):
                    o.then(dve.scalar_tensor_tensor(out=slot_f[:, 3, k, :], in0=rc[:, 6, :], scalar=-float(TOKENS),
                                                    in1=slot_f[:, 2, k, :], op0=ALU.add, op1=ALU.subtract))
                tcount = rc[0:1, 0:3, :].rearrange("p a b -> p (a b)")[:, 0:SLOT_COLS]
                o.then(dve.tensor_scalar(tcount, iota_col[0:1, 0:SLOT_COLS], 0.0, float(HALVES), ALU.mult, ALU.add))
                for n in range(EXPERTS - 1):
                    o.then(dve.scalar_tensor_tensor(out=tcount, in0=iota_col[0:1, 0:SLOT_COLS], scalar=ends[0:1, n:n + 1], in1=tcount,
                                                    op0=ALU.is_ge, op1=ALU.add))
                o.then(dve.tensor_copy(tile_e[:], tcount))
                dve.sem_inc(route_ok, 1)

            def hot_slots(begin, end):
                k, g, made = begin // TILES, begin % TILES, 3 * begin // SLOTS_STEP

                def per_slot(col, width):
                    return col[:, g:g + SLOTS_STEP].unsqueeze(2).to_broadcast([P, SLOTS_STEP, width])

                def over(row, width):
                    return row.unsqueeze(1).to_broadcast([P, SLOTS_STEP, width])

                if begin:
                    dve.wait_ge(hot_mm, begin)
                dve.tensor_tensor(hot_col, over(iota_col[:], P), per_slot(slot_f[:, 2, k, :], P), ALU.is_equal).then_inc(hot_ok, 1)
                o.then(dve.tensor_tensor(hot_val[:, :, 0, :], over(iota_tile, SLOT_COLS), per_slot(slot_f[:, 1, k, :], SLOT_COLS),
                                         ALU.is_equal))
                dve.tensor_tensor(hot_val[:, :, 1, :], hot_val[:, :, 0, :], per_slot(gate[:, k, :], SLOT_COLS),
                                  ALU.mult).then_inc(hot_ok, 1)
                dve.wait_ge(hot_ok, made + 2)
                dve.tensor_tensor(hot_val[:, :, 0, :], hot_val[:, :, 0, :], per_slot(slot_f[:, 3, k, :], SLOT_COLS),
                                  ALU.mult).then_inc(hot_ok, 1)

            def table():
                dve.wait_ge(hot_mm, TOPK * TILES)
                o.mark(dve.tensor_scalar(idx[:], pa[0][:, 0:SLOT_COLS], iota_p[:, 0:1], float(TOKENS), ALU.add, ALU.add))
                o.then(dve.tensor_scalar(w_slot[:], pa[0][:, SLOT_COLS:2 * SLOT_COLS], unscaled_tanh_ffn, None, ALU.mult))
                dve.sem_inc(table_ok, 1)

            sum_logits()
            for u in range(UPS):
                if u == 0:
                    choose()
                if u == 1:
                    place()
                if u >= 2:
                    hot_slots((u - 2) * SLOTS_STEP, (u - 1) * SLOTS_STEP)
                shared_hidden(BATCHES - 1, u)
                shared_low(BATCHES - 1, u)
            table()
            for i in range(TPB):
                shared_rows(BATCHES - 1, i)

            def hidden(t, p):
                after(dve, up_mm, Q0 + t + 1)
                after(dve, sil_sb, Q0 + t + 1)
                after(dve, hid_mm, t - 1)
                dve.scalar_tensor_tensor(out=hid[:, p, 0:H], in0=pu[p][:, 0:H], scalar=UP_UNSCALE * H_SCALE,
                                         in1=sil[:, p, :], op0=ALU.mult, op1=ALU.mult).then_inc(hid_sb, 1)

            def hidden_low(t, p):
                after(dve, hhi_sb, Q0 + t + 1)
                dve.tensor_tensor(hid_t[:, p, 1, :], pt_bank[:, 0:HP], hid_t[:, p, 0, :], ALU.subtract).then_inc(hlo_sb, 1)

            def gathered_turned(t, p, uses):
                after(dve, xt_mm, TILES + t + 1)
                after(dve, up_mm, Q0 + uses)
                dve.tensor_copy(x_t[:, p, :, :], xt_ps).then_inc(xt_sb, 1)

            gathered_turned(0, 0, 0)
            gathered_turned(1, 1, 0)
            hidden(0, 0)
            gathered_turned(2, 0, 1)
            with dve.Fori(0, SLOT_TILES // 2) as i:
                for k in range(2):
                    t = i * 2 + k + 1
                    hidden_low(t - 1, k)
                    hidden(t, 1 - k)
                    gathered_turned(t + 2, 1 - k, t + 1)
            hidden_low(SLOT_TILES - 1, 0)


def kernel(x, ctx_512, g_xattn, g_ffn, L0_xattn_Wq, L0_xattn_Wk, L0_xattn_gamma_raw, L0_ffn_gate_w, L0_ffn_gate_bias,
           L0_ffn_shared_gw, L0_ffn_shared_dw, L0_ffn_up_w, L0_ffn_down_w):
    import concourse.bacc as bacc
    from concourse import mybir
    from concourse.bass_utils import run_bass_kernel_spmd

    def chunks(m):
        m = np.asarray(m)
        return m.reshape(-1, P, m.shape[1]).transpose(1, 0, 2).reshape(P, -1)

    def item(gate, value, down):
        up = np.concatenate([np.asarray(gate).T, np.asarray(value).T], axis=1)
        dn = np.zeros((HP, C), np.float32)
        dn[:H] = np.asarray(down).T
        return np.concatenate([chunks(up), chunks(dn)], axis=1)

    gw, dw = np.asarray(L0_ffn_shared_gw), np.asarray(L0_ffn_shared_dw)
    up_w, down_w = np.asarray(L0_ffn_up_w), np.asarray(L0_ffn_down_w)
    S = HALVES * H
    items = [item(gw[S + h * H:S + (h + 1) * H], gw[h * H:(h + 1) * H], dw[:, h * H:(h + 1) * H]) for h in range(HALVES)]
    items += [item(up_w[e, :H], up_w[e, H:], down_w[e]) for e in range(EXPERTS)]
    arrays = {
        "x": np.asarray(x).reshape(TOKENS, C),
        "ctx_t": np.asarray(ctx_512).reshape(TOKENS, D).T,
        "wq_t": np.asarray(L0_xattn_Wq).T,
        "wk_t": np.asarray(L0_xattn_Wk).T,
        "gates": np.concatenate([np.asarray(g_xattn).reshape(1), np.asarray(g_ffn).reshape(1),
                                 np.asarray(L0_xattn_gamma_raw).reshape(1)]),
        "gate_wt": np.asarray(L0_ffn_gate_w).T.reshape(KC, P, EXPERTS).transpose(1, 0, 2),
        "gate_bias": np.asarray(L0_ffn_gate_bias),
        "weights": np.stack(items),
    }
    nc = bacc.Bacc("TRN2", target_bir_lowering=False, num_devices=1)
    named, args = {}, []
    for name, a in arrays.items():
        a = np.ascontiguousarray(a)
        named[f"in_{name}"] = a
        args.append(nc.dram_tensor(f"in_{name}", a.shape, mybir.dt.from_np(a.dtype), kind="ExternalInput").ap())
    out = nc.dram_tensor("out", (TOKENS + PAD_ROWS, C), mybir.dt.float32, kind="ExternalOutput").ap()
    xn_rows = nc.dram_tensor("xn_rows", (TOKENS + PAD_ROWS, 2 * C), mybir.dt.float16, kind="Internal").ap()
    build(nc, *args, out, xn_rows)
    res = run_bass_kernel_spmd(nc, [named], core_ids=[0])
    return res.results[0]["out"][:TOKENS].reshape(BATCHES, SEQ, C)
```

```python
import numpy as np

BATCHES, SEQ, C, D = 4, 512, 512, 128
P = 128
TOKENS = BATCHES * SEQ
TPB = SEQ // P
TILES = TOKENS // P
KC = C // P
EXPERTS, TOPK = 8, 2
H = 352
HALVES = 2
HP = 384
JC = HP // P
PIECES = [(h, j * P, min(P, H - j * P)) for h in range(HALVES) for j in range(JC)]
UPS = len(PIECES)
SLOTS_STEP = 4
SLOTS_STEPS = TOPK * TILES // SLOTS_STEP
BEFORE = 3
FIRST = 14
BY_DVE = 20
PER_STEP = 4
KEEP = int(SEQ * 0.3)
UP_W = KC * 2 * H
ITEM_W = UP_W + JC * C
ITEMS = HALVES + EXPERTS
EARLY = 7
CHUNKS = 8
RING = 4
CHUNK_W = ITEM_W // CHUNKS
SLOT_TILES = TOKENS * TOPK // P + EXPERTS - 1
SLOT_COLS = SLOT_TILES + 2
PAD_ROWS = P
SMALL = 3
ROUNDS = 5
X_SCALE, W_SCALE, H_SCALE = 16.0, 256.0, 16.0
UP_UNSCALE = 1.0 / (X_SCALE * W_SCALE)
DOWN_UNSCALE = 1.0 / (H_SCALE * W_SCALE)
SIM_SCALE = 1.0 / (float(np.sqrt(np.float32(D // 4))) * 4.0)
LN_EPS = 1e-5
BIG = 3.0e38
CREDIT = 32


def build(nc, x, ctx_t, wq_t, wk_t, gates, gate_wt, gate_bias, weights, out, xn_rows):
    import concourse.bass as bass
    from concourse import mybir
    from contextlib import ExitStack

    F32, F16, I32, U32 = mybir.dt.float32, mybir.dt.float16, mybir.dt.int32, mybir.dt.uint32
    ALU, ACT, AX = mybir.AluOpType, mybir.ActivationFunctionType, mybir.AxisListType
    ds = bass.ds

    x_tiles = x.rearrange("(g p) c -> p g c", p=P)
    out_tiles = out.rearrange("(g p) c -> p g c", p=P)
    xn_tiles = xn_rows.rearrange("(g p) c -> p g c", p=P)

    with ExitStack() as ctx:
        def sb(name, shape, dt=F32):
            return ctx.enter_context(nc.sbuf_tensor(name, shape, dt))

        def bank(name):
            return ctx.enter_context(nc.psum_tensor(name, [P, 512], F32))

        credited = []

        def sem(name, credit=True):
            s = ctx.enter_context(nc.semaphore(name))
            if credit:
                credited.append(s)
            return s

        w = sb("w", [P, ITEMS, 2, ITEM_W], F16)
        attn = w[:, EARLY:ITEMS, :, :].rearrange("p a b c -> p (a b c)").bitcast(F32)
        taken = [0]

        def attn_buf(words):
            taken[0] += words
            assert taken[0] <= (ITEMS - EARLY) * ITEM_W
            return attn[:, taken[0] - words:taken[0]]

        def attn_tiles():
            return attn_buf(TPB * SEQ).rearrange("p (i c) -> p i c", i=TPB)

        xb = attn_tiles()
        sim = attn_tiles()
        wq_s, wk_s = attn_buf(D), attn_buf(D)
        att = attn_tiles()
        xnr = attn_buf(TPB * C).bitcast(F16).rearrange("p (i c) -> p i c", i=TPB)
        taken[0] = (ITEMS - 1 - EARLY) * ITEM_W
        hot = attn_buf(2 * SEQ + TPB * SEQ // 2)
        q_t, k_t = hot[:, 0:SEQ], hot[:, SEQ:2 * SEQ]
        ctx_b = q_t
        junk = hot[:, 2 * SEQ:].bitcast(F16).rearrange("p (i c) -> p i c", i=TPB)
        masked = junk.rearrange("p i c -> p (i c)").bitcast(F32).rearrange("p (i c) -> p i c", i=2)
        xn = masked
        x_tb = attn_buf(KC * SEQ).bitcast(F16).rearrange("p (a c) -> p a c", a=2 * KC)

        stage = sb("stage", [P, RING, CHUNK_W])
        work = sb("work", [P, 2 * KC * P + 2 * HP + 2 * HP + 2 * C + 2 * H])
        used = [0]

        def work_buf(words):
            used[0] += words
            return work[:, used[0] - words:used[0]]

        hid_tb = work_buf(UPS * SEQ).bitcast(F16).rearrange("p (u a c) -> p u a c", u=UPS, a=2)
        hb = work_buf(2 * SEQ).rearrange("p (a c) -> p a c", a=2)
        used[0] = 0
        x_t = work_buf(2 * KC * P).bitcast(F16).rearrange("p (s a c) -> p s a c", s=2, a=2 * KC)
        hid16 = work_buf(2 * HP).bitcast(F16).rearrange("p (s a c) -> p s a c", s=2, a=2)
        hid_t = work_buf(2 * HP).bitcast(F16).rearrange("p (s a c) -> p s a c", s=2, a=2 * JC)
        hid = work_buf(2 * H).rearrange("p (a c) -> p a c", a=2)
        assert used[0] >= UPS * SEQ
        xg = work_buf(2 * C).bitcast(F16).rearrange("p (a c) -> p a c", a=2)
        rows = sb("rows", [P, 2, C])
        ident, ident16 = sb("ident", [P, P]), sb("ident16", [P, P], F16)
        ones, tri = sb("ones", [P, P], F16), sb("tri", [P, P], F16)
        one1 = sb("one1", [P, 1])
        iota_col = sb("iota_col", [P, P])
        iota_p = sb("iota_p", [P, 1])
        iota_tile = iota_col[:, 0:SLOT_COLS]
        first = sb("first", [P, EXPERTS])
        warm = sb("warm", [P, 1])
        gcol, cst = sb("gcol", [P, 3]), sb("cst", [P, 9])
        gw_f, gw = attn_buf(KC * EXPERTS).rearrange("p (k e) -> p k e", k=KC), sb("gw", [P, KC, 2, EXPERTS], F16)
        bias_b = sb("bias_b", [P, EXPERTS])
        half_pow = sb("half_pow", [P, 2, TPB])
        bn6 = attn_buf(3 * TPB * 6).rearrange("p (s i c) -> p s i c", s=3, i=TPB)
        mv = sb("mv", [P, 3, TPB, 2])
        pt = sb("pt", [P, 8, TPB])
        lo, hi, cur = (attn_buf(2 * TPB).rearrange("p (a i) -> p a i", a=2) for _ in range(3))
        steps = attn_buf(3 * TPB).rearrange("p (a i) -> p a i", a=3)
        below, above = sb("below", [P, TPB], U32), sb("above", [P, TPB], U32)
        tmp4 = sb("tmp4", [P, 6, TPB])
        top8, pick8 = (attn_buf(TPB * 8).rearrange("p (i c) -> p i c", i=TPB) for _ in range(2))
        thr = sb("thr", [P, TPB])
        acc = sb("acc", [P, TPB // 2])
        missed, missed_i = sb("missed", [P, 1]), sb("missed_i", [1, 1], I32)
        lg = sb("lg", [P, TILES, 2, EXPERTS])
        r = [sb(f"r{n}", [P, TILES, EXPERTS], F16 if n == 2 else F32) for n in range(6)]

        rc = sb("rc", [P, 7, TILES])
        re8 = sb("re8", [P, 6, EXPERTS])
        ri8 = sb("ri8", [P, EXPERTS], I32)
        slot_i = sb("slot_i", [P, 3, TOPK, TILES], I32)
        slot_f = sb("slot_f", [P, 4, TOPK, TILES])
        idx = sb("idx", [P, SLOT_COLS], I32)
        idx_g, idx_s = sb("idx_g", [P, 2], I32), sb("idx_s", [P, 2], I32)
        w_slot = sb("w_slot", [P, SLOT_COLS])
        tile_e = sb("tile_e", [1, SLOT_COLS], I32)
        hot_words = SLOTS_STEP * (P + 2 * SLOT_COLS)
        hot_cols = [hot[:, n * hot_words:n * hot_words + SLOTS_STEP * P].rearrange("p (a c) -> p a c", a=SLOTS_STEP) for n in range(2)]
        hot_vals = [hot[:, n * hot_words + SLOTS_STEP * P:(n + 1) * hot_words].rearrange("p (a v c) -> p a v c", a=SLOTS_STEP, v=2)
                    for n in range(2)]

        pa = [bank("pa0"), bank("pa1")]
        pg, pu = [bank("pg0"), bank("pg1")], [bank("pu0"), bank("pu1")]
        pt_bank = bank("pt_bank")
        py = bank("py")
        xt_banks = [b_[:, :].bitcast(F16).rearrange("p (a c) -> p a c", a=2 * KC) for b_ in (pt_bank, pg[0])]
        score_banks = [pu[1], pg[1], pa[0], pa[1]]
        turn_banks = [pa[0], pa[1], pt_bank, pg[0]]
        y_banks = [py, pu[0]]

        def down_bank(b, i):
            return y_banks[(i + 1) % 2 if isinstance(b, int) and b == BATCHES - 1 else i % 2]

        xt_ps = pt_bank[:, :].bitcast(F16).rearrange("p (a c) -> p a c", a=2 * KC)
        xt_second = pa[1][:, :].bitcast(F16).rearrange("p (a c) -> p a c", a=2 * KC)
        hid_banks = [b_[:, 0:HP].bitcast(F16).rearrange("p (a c) -> p a c", a=2 * JC) for b_ in pa]

        waits_apart = {}
        sp_tick, pool_tick = sem("sp_tick", False), sem("pool_tick", False)
        ready = sem("ready", False)
        const_ok = sem("const_ok", False)
        pool_c = sem("pool_c", False)
        small_ld = sem("small_ld", False)
        cst_act = sem("cst_act", False)
        cst_ok = sem("cst_ok", False)
        gw_ok = sem("gw_ok", False)
        gw_hi = sem("gw_hi", False)
        pad_st = sem("pad_st", False)
        w_ld = [sem(f"w_ld{n}") for n in range(RING)]
        w_hi = sem("w_hi")
        w_lo = [sem(f"w_lo{n}") for n in range(RING)]
        w_scaled = sem("w_scaled")
        x_ld, ctx_ld = sem("x_ld"), sem("ctx_ld")
        qk_mm, qk_sb = sem("qk_mm"), sem("qk_sb")
        lg_mm = sem("lg_mm")
        sim_mm, sim_sb, tanh_sb = sem("sim_mm"), sem("sim_sb"), sem("tanh_sb")
        sig_sb, xn_sb, xa_made = sem("sig_sb"), sem("xn_sb"), sem("xa_made")
        stats_ok, x_stats_ok, guess_ok, base_ok, base_sb = sem("stats_ok"), sem("x_stats_ok"), sem("guess_ok"), sem("base_ok"), sem("base_sb")
        cur_ok, cnt_sb = sem("cur_ok", False), sem("cnt_sb")
        miss_ok, miss_mm = sem("miss_ok"), sem("miss_mm")
        a_made, at_mm, x1_made = sem("a_made"), sem("at_mm"), sem("x1_made")
        x1_st, ln_stats, ln_ok = sem("x1_st"), sem("ln_stats"), sem("ln_ok")
        xn_hi, xn_lo, xn_st = sem("xn_hi"), sem("xn_lo"), sem("xn_st")
        xt_mm, xt_sb, xt_act = sem("xt_mm"), sem("xt_sb"), sem("xt_act")
        up_mm, sil_sb, hid_sb = sem("up_mm"), sem("sil_sb"), sem("hid_sb")
        hid_mm, hhi_sb, hlo_sb, ht_sb = sem("hid_mm"), sem("hhi_sb"), sem("hlo_sb"), sem("ht_sb")
        down_mm, y_sb = sem("down_mm"), sem("y_sb")
        lg_sb = sem("lg_sb")
        x1_ld, sh_st = [sem("x1_ld0"), sem("x1_ld1")], [sem("sh_st0"), sem("sh_st1")]
        pool_ch = sem("pool_ch", False)
        dve_ch = sem("dve_ch", False)
        fb_ch = sem("fb_ch", False)
        exp_ok, route_mm, route_ok = sem("exp_ok", False), sem("route_mm", False), sem("route_ok", False)
        z_ok = sem("z_ok", False)
        warm_ok = sem("warm_ok", False)
        wqk_ld = sem("wqk_ld", False)
        hid_pad = sem("hid_pad", False)
        hot_ok, hot_mm, table_ok = sem("hot_ok", False), sem("hot_mm", False), sem("table_ok", False)
        g_ld = [sem("g_ld0", False), sem("g_ld1", False)]
        idx_c = sem("idx_c", False)
        y_add = sem("y_add", False)
        rows_free = sem("rows_free")

        def after(eng, s, n):
            eng.wait_ge(s, n + CREDIT)
            if waits_apart.get(eng) is not None:
                eng.sem_inc(waits_apart[eng], 1)

        def by_dve(item, n):
            if not isinstance(item, int):
                return False
            if item == ITEMS - 1:
                return n % 2 == 1
            return n % RING == RING - 1 and (item >= EARLY - 1 or item * CHUNKS + n < BY_DVE)

        def scaled_pieces(item, n):
            first = [k for k in range(BEFORE * CHUNKS) if by_dve(k // CHUNKS, k % CHUNKS)]
            if isinstance(item, int):
                return item * CHUNKS + n + 1 - sum(by_dve(k // CHUNKS, k % CHUNKS) for k in range(item * CHUNKS + n + 1))
            return item * CHUNKS + n + 1 - len(first)

        ROWS_DVE = BATCHES * (TPB - 1)
        Q0 = BATCHES * UPS

        class Order:

            def __init__(self, eng, s):
                self.eng, self.s, self.n = eng, s, 0

            def mark(self, ins):
                self.n += 1
                ins.then_inc(self.s, 1)
                return self.n

            def wait(self, n=None):
                self.eng.wait_ge(self.s, self.n if n is None else n)

            def then(self, ins):
                self.mark(ins)
                self.wait()

            def clear(self):
                if self.n:
                    self.wait()
                self.eng.sem_clear(self.s)
                self.n = 0

        block = ctx.enter_context(nc.Block())

        @block.sync
        def _(sp):
            waits_apart[sp] = sp_tick
            sp.wait_ge(ready, 1)

            def load_piece(item, n):
                after(sp, w_lo[n % RING], item * (CHUNKS // RING) + n // RING)
                sp.dma_start(stage[:, n % RING, :], weights[ds(item, 1), :, n * CHUNK_W:(n + 1) * CHUNK_W]
                             .rearrange("a p c -> (a p) c")).then_inc(w_ld[n % RING], 16)

            def load_item(item):
                for n in range(CHUNKS):
                    load_piece(item, n)

            def load_context(b, tile0):
                after(sp, sim_mm, tile0)
                sp.dma_start(ctx_b, ctx_t[:, ds(b * SEQ, SEQ)]).then_inc(ctx_ld, 16)

            def load_x(tile0):
                after(sp, x1_st, tile0 * 16)
                after(sp, xn_sb, tile0)
                sp.dma_start(xb, x_tiles[:, ds(tile0, TPB), :]).then_inc(x_ld, 16)

            def store_attended(tile0):
                for i in range(TPB):
                    after(sp, x1_made, tile0 + i + 1)
                    sp.dma_start(out_tiles[:, ds(tile0 + i, 1), :], xb[:, i:i + 1, :]).then_inc(x1_st, 16)

            def store_rows(tile0):
                for i in range(TPB):
                    after(sp, xn_lo, tile0 + i + 1)
                    after(sp, xn_hi, tile0 + i + 1)
                    sp.dma_start(xn_tiles[:, ds(tile0 + i, 1), :], xnr[:, i:i + 1, :]).then_inc(xn_st, 16)

            def reload(b, tile0, i):
                after(sp, x1_st, (tile0 + TPB) * 16)
                after(sp, sh_st[i % 2], (b * (TPB // 2) + i // 2) * 16)
                sp.dma_start(rows[:, i % 2:i % 2 + 1, :], out_tiles[:, ds(tile0 + i, 1), :]).then_inc(x1_ld[i % 2], 16)

            def store_shared(tile0, i):
                after(sp, y_sb, tile0 + i + 1)
                sp.dma_start(out_tiles[:, ds(tile0 + i, 1), :], rows[:, i % 2:i % 2 + 1, :]).then_inc(sh_st[i % 2], 16)

            load_context(0, 0)
            sp.dma_start(wq_s, wq_t).then_inc(wqk_ld, 16)
            sp.dma_start(wk_s, wk_t).then_inc(wqk_ld, 16)
            load_x(0)
            sp.dma_start(gcol[:], gates.rearrange("(a n) -> a n", a=1).partition_broadcast(P)
                         .rearrange("p a n -> p (a n)")).then_inc(small_ld, 16)
            sp.dma_start(gw_f, gate_wt).then_inc(small_ld, 16)
            sp.dma_start(bias_b[:], gate_bias.rearrange("(a n) -> a n", a=1).partition_broadcast(P)
                         .rearrange("p a n -> p (a n)")).then_inc(small_ld, 16)
            for n in range(RING):
                load_piece(0, n)
            sp.wait_ge(const_ok, 1)
            sp.wait_ge(warm_ok, 1)
            sp.dma_start(out_tiles[:, TILES, :], rows[:, 0, :]).then_inc(pad_st, 16)
            sp.dma_start(xn_tiles[:, TILES, :], rows[:, 0, :].bitcast(F16)).then_inc(pad_st, 16)
            for k in range(RING, CHUNKS):
                load_piece(k // CHUNKS, k % CHUNKS)
            load_context(1, TPB)
            last = BEFORE * CHUNKS - 1
            for k in range(CHUNKS, last):
                load_piece(k // CHUNKS, k % CHUNKS)
            sp.wait_ge(pad_st, 32)
            store_attended(0)
            store_rows(0)
            load_x(TPB)
            load_piece(last // CHUNKS, last % CHUNKS)

            def together(b, more):
                tile0, tile1, tile2 = (sp.snap((b + n) * TPB) if more else (b + n) * TPB for n in range(3))
                later = sp.snap(b + 2) if more else None
                item = sp.snap(b + BEFORE) if more else b + BEFORE
                for n in range(RING):
                    load_piece(item, n)
                reload(b, tile0, 0)
                reload(b, tile0, 1)
                if more:
                    load_context(later, tile2)
                for n in range(RING, CHUNKS):
                    load_piece(item, n)
                store_shared(tile0, 0)
                reload(b, tile0, 2)
                store_attended(tile1)
                store_shared(tile0, 1)
                reload(b, tile0, 3)
                if more:
                    load_x(tile2)
                store_rows(tile1)
                store_shared(tile0, 2)
                store_shared(tile0, 3)

            with sp.Fori(0, BATCHES - 2) as b:
                together(b, True)
            together(BATCHES - 2, False)
            tile0 = TILES - TPB
            reload(BATCHES - 1, tile0, 0)
            reload(BATCHES - 1, tile0, 1)
            load_item(EARLY - 1)
            after(sp, x1_st, TILES * 16)
            after(sp, xn_st, TILES * 16)
            after(sp, xt_mm, TILES)
            load_item(EARLY)
            load_item(EARLY + 1)
            for n in range(RING):
                load_piece(ITEMS - 1, n)
            store_shared(tile0, 0)
            reload(BATCHES - 1, tile0, 2)
            store_shared(tile0, 1)
            reload(BATCHES - 1, tile0, 3)
            store_shared(tile0, 2)
            store_shared(tile0, 3)
            sp.wait_ge(pad_st, 32)
            after(sp, x1_st, TILES * 16)
            for s in sh_st:
                after(sp, s, TILES // 2 * 16)
            after(sp, rows_free, SLOT_TILES)

        @block.gpsimd
        def _(pool):
            waits_apart[pool] = pool_tick
            for s in credited:
                pool.sem_inc(s, CREDIT)
            pool.sem_inc(ready, 1)
            c = Order(pool, pool_c)
            pool.memset(rows[:, 0, :], 0.0).then_inc(const_ok, 1)
            c.mark(pool.memset(ident[:], 0.0))
            c.mark(pool.memset(ident16[:], 0.0))
            c.mark(pool.memset(ones[:], 1.0))
            c.mark(pool.memset(tri[:], 0.0))
            c.mark(pool.memset(half_pow[:, 0, :], 0.5))
            c.mark(pool.memset(half_pow[:, 1, :], -0.5))
            c.mark(pool.iota(iota_col[:], pattern=[[1, P]], base=0, channel_multiplier=0, allow_small_or_imprecise_dtypes=True))
            c.mark(pool.memset(one1[:], 1.0))
            c.mark(pool.iota(iota_p[:], pattern=[[1, 1]], base=0, channel_multiplier=1, allow_small_or_imprecise_dtypes=True))
            c.mark(pool.iota(first[:], pattern=[[-1, EXPERTS]], base=EXPERTS, channel_multiplier=0, allow_small_or_imprecise_dtypes=True))
            c.wait()
            for m in (ident, ident16):
                c.mark(pool.affine_select(out=m[:], in_=m[:], compare_op=ALU.not_equal, fill=1.0, base=0,
                                          pattern=[[-1, P]], channel_multiplier=1))
            c.mark(pool.affine_select(out=tri[:], in_=tri[:], compare_op=ALU.is_ge, fill=1.0, base=0,
                                      pattern=[[-1, P]], channel_multiplier=1))
            c.wait()
            pool.sem_inc(const_ok, 1)

            pool.wait_ge(cst_ok, 1)
            sd, var_e, rstd, step = pt[:, 0, :], pt[:, 1, :], pt[:, 2, :], pt[:, 3, :]
            o = Order(pool, pool_ch)

            def guess(b):
                after(pool, stats_ok, b + 1)
                after(pool, cnt_sb, b * ROUNDS * (TPB // 2))
                mean_s, var_s = mv[:, 0, :, 0], mv[:, 0, :, 1]
                o.mark(pool.memset(lo[:, 1, :], 290.0))
                o.mark(pool.memset(hi[:, 1, :], 60.0))
                o.then(pool.tensor_tensor(sd, var_s, half_pow[:, 0, :], ALU.pow))
                bracket = ((cur, 0.5077), (lo, -0.2), (hi, 1.2))
                for n, (_, z) in enumerate(bracket):
                    o.mark(pool.tensor_scalar(steps[:, n, :], sd, z, None, ALU.mult))
                o.wait()
                for n, (dst, _) in enumerate(bracket):
                    o.mark(pool.tensor_tensor(dst[:, 0, :], steps[:, n, :], mean_s, ALU.add))
                o.wait()
                pool.sem_inc(guess_ok, 1)

            def base_scalars(b):
                after(pool, x_stats_ok, b + 1)
                after(pool, base_sb, b * TPB)
                mean_x, var_x = mv[:, 1, :, 0], mv[:, 1, :, 1]
                o.then(pool.tensor_scalar(var_e, var_x, LN_EPS, None, ALU.add))
                o.then(pool.tensor_tensor(rstd, var_e, half_pow[:, 1, :], ALU.pow))
                gain, shift = pt[:, 4, :], pt[:, 5, :]
                o.then(pool.tensor_scalar(step, rstd, cst[:, 3:4], None, ALU.mult))
                o.mark(pool.tensor_scalar(gain, step, 1.0, None, ALU.add))
                o.then(pool.tensor_tensor(shift, step, mean_x, ALU.mult))
                o.then(pool.tensor_scalar(shift, shift, -1.0, None, ALU.mult))
                pool.sem_inc(base_ok, 1)

            def add_attention(b):
                for i in range(TPB):
                    after(pool, base_sb, b * TPB + i + 1)
                    after(pool, a_made, b * TPB + i + 1)
                    pool.tensor_tensor(xb[:, i, :], xb[:, i, :], att[:, i, :], ALU.add).then_inc(xa_made, 1)

            def row_scalars(b):
                after(pool, ln_stats, b + 1)
                after(pool, xn_sb, b * TPB)
                gain2, shift2 = pt[:, 6, :], pt[:, 7, :]
                mean_2, var_2 = mv[:, 2, :, 0], mv[:, 2, :, 1]
                o.then(pool.tensor_scalar(var_e, var_2, X_SCALE ** -2, LN_EPS * X_SCALE ** -2, ALU.mult, ALU.add))
                o.mark(pool.tensor_scalar(step, mean_2, -1.0, None, ALU.mult))
                o.then(pool.tensor_tensor(gain2, var_e, half_pow[:, 1, :], ALU.pow))
                o.then(pool.tensor_tensor(shift2, gain2, step, ALU.mult))
                pool.sem_inc(ln_ok, 1)

            def low_piece(item, n):
                if by_dve(item, n):
                    return
                after(pool, w_hi, item * CHUNKS + n + 1)
                after(pool, w_scaled, scaled_pieces(item, n))
                pool.tensor_tensor(w[:, ds(item, 1), 1, n * CHUNK_W:(n + 1) * CHUNK_W], stage[:, n % RING:n % RING + 1, :],
                                   w[:, ds(item, 1), 0, n * CHUNK_W:(n + 1) * CHUNK_W], ALU.subtract).then_inc(w_lo[n % RING], 1)

            def shared_low(b, u):
                q, m = b * UPS + u, PIECES[u][2]
                after(pool, hhi_sb, q + 1)
                pool.tensor_tensor(hid_tb[0:m, u, 1, :], hb[0:m, u % 2, :], hid_tb[0:m, u, 0, :], ALU.subtract).then_inc(hlo_sb, 1)

            guess(0)
            base_scalars(0)
            def first_pieces(begin, end):
                for k in range(begin, end):
                    low_piece(k // CHUNKS, k % CHUNKS)

            first_pieces(0, FIRST)
            add_attention(0)
            first_pieces(FIRST, FIRST + 3)
            row_scalars(0)
            first_pieces(FIRST + 3, FIRST + 6)
            guess(1)
            o.clear()
            first_pieces(FIRST + 6, BEFORE * CHUNKS)

            def together(b, more):
                base_scalars(b + 1)
                for u in range(UPS):
                    shared_low(b, u)
                    if u < TPB:
                        low_piece(b + BEFORE, u)
                add_attention(b + 1)
                for n in range(TPB, CHUNKS - 2):
                    low_piece(b + BEFORE, n)
                row_scalars(b + 1)
                for n in range(CHUNKS - 2, CHUNKS):
                    low_piece(b + BEFORE, n)
                if more:
                    guess(b + 2)
                o.clear()

            with pool.Fori(0, BATCHES - 2) as b:
                together(b, True)
            together(BATCHES - 2, False)
            for u in range(UPS):
                for n in range(u * PER_STEP, (u + 1) * PER_STEP):
                    if n % PER_STEP == PER_STEP // 2:
                        shared_low(BATCHES - 1, u)
                    low_piece(EARLY - 1 + n // CHUNKS, n % CHUNKS)

            def gather(t, p):
                pool.sem_clear(idx_c)
                pool.tensor_copy(idx_g[:, p:p + 1], idx[:, ds(t, 1)]).then_inc(idx_c, 1)
                pool.wait_ge(idx_c, 1)
                pool.indirect_dma_start(out=xg[:, p, :], out_offset=None, in_=xn_rows,
                                        in_offset=bass.IndirectOffsetOnAxis(ap=idx_g[:, p:p + 1], axis=0)).then_inc(g_ld[p], 16)

            def add_rows(t, p):
                pool.sem_clear(idx_c)
                pool.tensor_copy(idx_s[:, p:p + 1], idx[:, ds(t, 1)]).then_inc(idx_c, 1)
                pool.wait_ge(idx_c, 1)
                after(pool, y_sb, TILES + t + 1)
                pool.indirect_dma_start(out=out, out_offset=bass.IndirectOffsetOnAxis(ap=idx_s[:, p:p + 1], axis=0),
                                        in_=rows[:, p, :], in_offset=None, compute_op=ALU.add).then_inc(y_add, 16)

            def rows_added(t):
                pool.wait_ge(y_add, (t + 1) * 16)
                pool.sem_inc(rows_free, 1)

            def pool_tile(t, p, before):
                after(pool, xt_mm, TILES + t + 2)
                gather(t + 3, 1 - p)
                if before is not None:
                    rows_added(before)
                add_rows(t, p)

            pool.wait_ge(table_ok, 1)
            pool.wait_ge(pad_st, 32)
            after(pool, xn_st, TILES * 16)
            gather(0, 0)
            gather(1, 1)
            for n in range(CHUNKS):
                low_piece(ITEMS - 1, n)
            after(pool, down_mm, TILES)
            pool.memset(hid16[:, :, :, H:HP], 0.0).then_inc(hid_pad, 1)
            after(pool, xt_mm, TILES + 1)
            gather(2, 0)
            for s in sh_st:
                after(pool, s, TILES // 2 * 16)
            pool_tile(0, 0, None)
            with pool.Fori(0, SLOT_TILES // 2 - 1) as i:
                pool_tile(i * 2 + 1, 1, i * 2)
                pool_tile(i * 2 + 2, 0, i * 2 + 1)
            t = SLOT_TILES - 2
            pool_tile(t, 1, t - 1)
            rows_added(t)
            add_rows(t + 1, 0)
            rows_added(t + 1)

        @block.scalar
        def _(act):
            act.wait_ge(ready, 1)
            act.wait_ge(const_ok, 1)
            act.activation(warm[:], rows[:, 0, 0:1], ACT.Silu).then_inc(warm_ok, 1)
            act.wait_ge(small_ld, 16 * SMALL)
            act.activation(cst[:, 0:2], gcol[:, 0:2], ACT.Tanh).then_inc(cst_act, 1)
            act.activation(cst[:, 2:3], gcol[:, 2:3], ACT.Tanh, scale=0.5).then_inc(cst_act, 1)
            act.activation(gw[:, :, 0, :], gw_f, ACT.Copy, scale=W_SCALE).then_inc(gw_hi, 1)

            def high_piece(item, n):
                after(act, w_ld[n % RING], (item * (CHUNKS // RING) + n // RING + 1) * 16)
                act.activation(w[:, ds(item, 1), 0, n * CHUNK_W:(n + 1) * CHUNK_W], stage[:, n % RING:n % RING + 1, :],
                               ACT.Copy, scale=W_SCALE).then_inc(w_hi, 1)
                if not by_dve(item, n):
                    after(act, w_hi, item * CHUNKS + n + 1)
                    act.activation(stage[:, n % RING, :], stage[:, n % RING, :], ACT.Copy, scale=W_SCALE).then_inc(w_scaled, 1)

            def keep_qk(b):
                after(act, sim_mm, b * TPB)
                after(act, qk_mm, b * 2 + 2)
                for n, dst in enumerate((q_t, k_t)):
                    act.activation(dst, score_banks[n][:, :], ACT.Copy).then_inc(qk_sb, 1)

            def keep_scores(b):
                after(act, a_made, b * TPB)
                for i in range(TPB):
                    after(act, sim_mm, b * TPB + i + 1)
                    act.activation(sim[:, i, :], score_banks[i][:, :], ACT.Copy).then_inc(sim_sb, 1)

            def score_tanh(b):
                after(act, sim_mm, (b + 1) * TPB)
                after(act, at_mm, b * TPB)
                after(act, xa_made, b * TPB)
                for i in range(TPB):
                    act.activation(att[:, i, :], score_banks[i][:, :], ACT.Tanh, scale=0.5 * SIM_SCALE).then_inc(tanh_sb, 1)

            def scaled_sigmoid(b, i):
                after(act, tanh_sb, b * TPB + i + 1)
                act.activation(att[:, i, :], att[:, i, :], ACT.Identity, bias=cst[:, 4:5], scale=cst[:, 4:5]).then_inc(sig_sb, 1)

            def base(b, tiles=range(TPB)):
                after(act, base_ok, b + 1)
                for i in tiles:
                    act.activation(xb[:, i, :], xb[:, i, :], ACT.Identity, bias=pt[:, 5, i:i + 1],
                                   scale=pt[:, 4, i:i + 1]).then_inc(base_sb, 1)

            def count(b, n):
                act.wait_ge(cur_ok, b * ROUNDS + n + 1)
                for i in range(TPB // 2, TPB):
                    act.activation(junk[:, i, :], sim[:, i, :], ACT.Sign, bias=cur[:, 0, i:i + 1], scale=-1.0,
                                   accum_out=acc[:, i - TPB // 2:i - TPB // 2 + 1]).then_inc(cnt_sb, 1)

            def normalised(b, i):
                if i == 0:
                    after(act, ln_ok, b + 1)
                    after(act, xn_st, b * TPB * 16)
                    after(act, xt_mm, b * TPB)
                after(act, xn_lo, b * TPB + i - 1)
                act.activation(xn[:, i % 2, :], xb[:, i, :], ACT.Identity, bias=pt[:, 7, i:i + 1],
                               scale=pt[:, 6, i:i + 1]).then_inc(xn_sb, 1)
                after(act, xn_sb, b * TPB + i + 1)
                act.activation(xnr[:, i, 0:C], xn[:, i % 2, :], ACT.Copy).then_inc(xn_hi, 1)

            def keep_logits(b):
                after(act, lg_mm, b + 1)
                act.activation(lg[:, ds(b * TPB, TPB), :, :],
                               pt_bank[:, 0:TPB * 2 * EXPERTS].rearrange("p (t a e) -> p t a e", t=TPB, a=2), ACT.Copy).then_inc(lg_sb, 1)

            def shared_silu(b, u):
                q, m = b * UPS + u, PIECES[u][2]
                after(act, up_mm, q + 1)
                after(act, hlo_sb, q - 1)
                act.activation(hb[0:m, u % 2, :], pg[u % 2][0:m, :], ACT.Silu, scale=UP_UNSCALE).then_inc(sil_sb, 1)

            def shared_high(b, u):
                q, m = b * UPS + u, PIECES[u][2]
                after(act, hid_sb, q + 1)
                after(act, down_mm, b * TPB)
                act.activation(hid_tb[0:m, u, 0, :], hb[0:m, u % 2, :], ACT.Copy).then_inc(hhi_sb, 1)

            def scores_and_rows(b, more, pieces=()):
                if more:
                    keep_qk(b + 1)
                for k in pieces:
                    high_piece(k // CHUNKS, k % CHUNKS)
                for i in range(TPB):
                    normalised(b, i)
                if more:
                    keep_scores(b + 1)
                after(act, up_mm, b * UPS)
                after(act, xt_mm, (b + 1) * TPB)
                act.activation(x_tb[:, :, (TPB - 1) * P:], xt_banks[(TPB - 1) % 2], ACT.Copy).then_inc(xt_act, 1)
                if more:
                    score_tanh(b + 1)

            keep_qk(0)
            keep_scores(0)
            score_tanh(0)
            act.wait_ge(cst_ok, 1)
            for i in range(TPB):
                scaled_sigmoid(0, i)
            for n in range(ROUNDS):
                count(0, n)
                if n:
                    base(0, (n - 1,))
                high_piece(n // CHUNKS, n % CHUNKS)
            for k in range(ROUNDS, FIRST + RING):
                high_piece(k // CHUNKS, k % CHUNKS)
            scores_and_rows(0, True, range(FIRST + RING, FIRST + RING + 2))
            for k in range(FIRST + RING + 2, BEFORE * CHUNKS):
                high_piece(k // CHUNKS, k % CHUNKS)

            def together(b, more):
                count(b + 1, 0)
                keep_logits(b)
                for u in range(UPS):
                    shared_silu(b, u)
                    if u + 1 < ROUNDS:
                        count(b + 1, u + 1)
                    if u == UPS - 1:
                        shared_high(b, u - 1)
                    if u != UPS - 2:
                        shared_high(b, u)
                    if u < TPB:
                        scaled_sigmoid(b + 1, u)
                        high_piece(b + BEFORE, u)
                    if u == ROUNDS - 2:
                        base(b + 1)
                for n in range(TPB, CHUNKS):
                    high_piece(b + BEFORE, n)
                scores_and_rows(b + 1, more)

            with act.Fori(0, BATCHES - 2) as b:
                together(b, True)
            together(BATCHES - 2, False)
            def router_exp():
                act.wait_ge(z_ok, 1)
                act.activation(r[1][:], r[0][:], ACT.Exp, scale=-UP_UNSCALE).then_inc(exp_ok, 1)

            after(act, xt_act, BATCHES)
            act.activation(warm[:], warm[:], ACT.Exp)
            keep_logits(BATCHES - 1)
            after(act, x1_st, TILES * 16)
            after(act, xn_st, TILES * 16)
            after(act, xt_mm, TILES)
            for u in range(UPS):
                if u == 0:
                    router_exp()
                shared_silu(BATCHES - 1, u)
                for n in range(u * PER_STEP, (u + 1) * PER_STEP):
                    if n - u * PER_STEP == PER_STEP // 2:
                        shared_high(BATCHES - 1, u)
                    if n < 3 * CHUNKS:
                        high_piece(EARLY - 1 + n // CHUNKS, n % CHUNKS)
            act.wait_ge(table_ok, 1)
            after(act, up_mm, BATCHES * UPS)
            for n in range(RING):
                high_piece(ITEMS - 1, n)
            for n in range(RING, CHUNKS):
                after(act, w_lo[n % RING], (ITEMS - 1) * (CHUNKS // RING) + n // RING)
                act.dma_start(stage[:, n % RING, :], weights[ITEMS - 1, :, n * CHUNK_W:(n + 1) * CHUNK_W]).then_inc(w_ld[n % RING], 16)
            for n in range(RING, CHUNKS):
                high_piece(ITEMS - 1, n)

            def silu(t, p):
                after(act, up_mm, Q0 + t + 1)
                after(act, hlo_sb, Q0 + t - 1)
                act.activation(hid[:, p, :], pg[p][:, 0:H], ACT.Silu, scale=UP_UNSCALE).then_inc(sil_sb, 1)

            def hidden_high(t, p):
                after(act, hid_sb, Q0 + t + 1)
                after(act, hid_mm, t - 1)
                act.activation(hid16[:, p, 0, 0:H], hid[:, p, :], ACT.Copy).then_inc(hhi_sb, 1)

            def expert_rows(t, p):
                after(act, down_mm, TILES + t + 1)
                after(act, rows_free, t - 1)
                act.activation(rows[:, p, :], py[:, :], ACT.Copy, scale=w_slot[:, ds(t, 1)]).then_inc(y_sb, 1)

            silu(0, 0)
            hidden_high(0, 0)
            for s in sh_st:
                after(act, s, TILES // 2 * 16)
            with act.Fori(0, SLOT_TILES // 2) as i:
                for k in range(2):
                    t = i * 2 + k + 1
                    silu(t, 1 - k)
                    hidden_high(t, 1 - k)
                    expert_rows(t - 1, k)
            expert_rows(SLOT_TILES - 1, 0)

        @block.tensor
        def _(pe):
            pe.wait_ge(ready, 1)
            pe.wait_ge(wqk_ld, 32)

            def project(b, shared):
                after(pe, ctx_ld, (b + 1) * 16)
                after(pe, tanh_sb, b * TPB)
                if shared is not None:
                    after(pe, hid_sb, (shared + 1) * UPS)
                for n, m in enumerate((wq_s, wk_s)):
                    pe.matmul(score_banks[n][:, :], m, ctx_b, start=True, stop=True).then_inc(qk_mm, 1)

            def scores(b, i):
                after(pe, qk_sb, (b + 1) * 2)
                if i >= 2:
                    after(pe, x1_made, b * TPB - TPB + i - 1)
                pe.matmul(score_banks[i][:, :], q_t[:, i * P:(i + 1) * P], k_t, start=True, stop=True).then_inc(sim_mm, 1)

            def missed_rows(b):
                after(pe, miss_ok, b + 1)
                after(pe, tanh_sb, (b + 1) * TPB)
                pe.matmul(pa[0][0:1, 0:1], missed[:], one1[:], start=True, stop=True).then_inc(miss_mm, 1)

            def turn_attention(b):
                after(pe, lg_sb, b)
                after(pe, hid_sb, b * UPS)
                after(pe, a_made, (b + 1) * TPB)
                for i in range(TPB):
                    for j in range(TPB):
                        mm = pe.transpose(turn_banks[i][:, j * P:(j + 1) * P], att[:, j, i * P:(i + 1) * P], ident[:])
                    mm.then_inc(at_mm, 1)

            def turn_rows(src, bank_):
                for n in range(2 * KC):
                    mm = pe.transpose(bank_[:, n, :], src[:, n * P:(n + 1) * P], ident16[:])
                mm.then_inc(xt_mm, 1)

            def turn_batch(b, i):
                if i == 0:
                    after(pe, lg_sb, b)
                    after(pe, hid_sb, b * UPS)
                    after(pe, xt_act, b)
                after(pe, xn_hi, b * TPB + i + 1)
                after(pe, xn_lo, b * TPB + i + 1)
                if i >= 2:
                    after(pe, xt_sb, b * (TPB - 1) + i - 1)
                turn_rows(xnr[:, i, :], xt_banks[i % 2])

            def logits(b):
                after(pe, xt_sb, (b + 1) * (TPB - 1))
                for i in range(TPB):
                    if i == TPB - 1:
                        after(pe, xt_act, b + 1)
                    at = i * 2 * EXPERTS
                    for k in range(KC):
                        for part in range(2):
                            n = (2 - part) * EXPERTS
                            mm = pe.matmul(pt_bank[:, at:at + n], x_tb[:, part * KC + k, i * P:(i + 1) * P],
                                           gw[:, k, 0:2 - part, :].rearrange("p a e -> p (a e)"),
                                           start=(i, k, part) == (0, 0, 0), stop=(k, part) == (KC - 1, 1), skip_group_check=True)
                mm.then_inc(lg_mm, 1)

            def shared_up(b, u, beside=None, ks=range(KC)):
                half, off, m = PIECES[u]
                if u == 1 and beside is not None:
                    after(pe, tanh_sb, (beside + 1) * TPB)
                if u == 0 and 0 in ks:
                    after(pe, y_sb, b * TPB)
                if 0 in ks:
                    after(pe, hid_sb, b * UPS + u - 1)
                for k in ks:
                    for bank_, at in ((pg[u % 2], k * 2 * H + off), (pu[u % 2], k * 2 * H + H + off)):
                        for part, xpart in ((0, 0), (0, 1), (1, 0)):
                            mm = pe.matmul(bank_[0:m, :], w[:, half, part, at:at + m], x_tb[:, xpart * KC + k, :],
                                           start=(k, part, xpart) == (0, 0, 0), stop=(k, part) == (KC - 1, 1))
                if KC - 1 in ks:
                    mm.then_inc(up_mm, 1)

            def shared_down(b, i, pieces=range(UPS)):
                bank_ = down_bank(b, i)
                if 0 in pieces:
                    after(pe, y_sb, b * TPB + max(0, i - 1))
                    if bank_ is pu[0]:
                        after(pe, hid_sb, b * UPS + UPS - 1)
                for u in pieces:
                    half, off, m = PIECES[u]
                    after(pe, hhi_sb, b * UPS + u + 1)
                    after(pe, hlo_sb, b * UPS + u + 1)
                    at = UP_W + off // P * C
                    for part, wpart in ((0, 0), (0, 1), (1, 0)):
                        mm = pe.matmul(bank_[:, :], hid_tb[0:m, u, part, i * P:(i + 1) * P],
                                       w[0:m, half, wpart, at:at + C],
                                       start=(u, part, wpart) == (0, 0, 0), stop=(u, part) == (UPS - 1, 1))
                if UPS - 1 in pieces:
                    mm.then_inc(down_mm, 1)

            project(0, None)
            for i in range(TPB):
                scores(0, i)
            pe.wait_ge(const_ok, 2)
            missed_rows(0)
            project(1, None)
            turn_attention(0)
            for i in range(TPB):
                scores(1, i)
            for i in range(TPB):
                turn_batch(0, i)
            for s in w_lo:
                after(pe, s, HALVES * (CHUNKS // RING))
            after(pe, w_hi, HALVES * CHUNKS)
            pe.wait_ge(gw_ok, 1)

            def together(b, more):
                logits(b)
                for u in range(UPS):
                    shared_up(b, u, b + 1)
                shared_down(b, 0, range(0, 4))
                missed_rows(b + 1)
                shared_down(b, 1, range(0, 4))
                shared_down(b, 0, range(4, UPS))
                shared_down(b, 1, range(4, UPS))
                turn_attention(b + 1)
                if more:
                    project(b + 2, b)
                shared_down(b, 2)
                if more:
                    for i in range(TPB):
                        scores(b + 2, i)
                    turn_batch(b + 1, 0)
                    shared_down(b, 3, range(0, 3))
                    turn_batch(b + 1, 1)
                    shared_down(b, 3, range(3, UPS))
                else:
                    shared_down(b, 3)
                    turn_batch(b + 1, 0)
                    turn_batch(b + 1, 1)
                turn_batch(b + 1, 2)
                turn_batch(b + 1, 3)

            with pe.Fori(0, BATCHES - 2) as b:
                together(b, True)
            together(BATCHES - 2, False)

            def ranks():
                pe.wait_ge(route_ok, 1)
                sel = r[2][:].rearrange("p t e -> p (t e)")
                pe.matmul(pa[0][:, 0:P], tri[:], sel, start=True, stop=True).then_inc(route_mm, 1)
                pe.matmul(pa[1][:, 0:P], ones[:], sel, start=True, stop=True).then_inc(route_mm, 1)

            def slots(step):
                pe.wait_ge(hot_ok, 3 * (step + 1))
                for n in range(SLOTS_STEP):
                    pe.matmul(pa[0][:, 0:2 * SLOT_COLS], hot_cols[step % 2][:, n, :],
                              hot_vals[step % 2][:, n, :, :].rearrange("p v c -> p (v c)"),
                              start=(step, n) == (0, 0), stop=(step, n) == (SLOTS_STEPS - 1, SLOTS_STEP - 1),
                              skip_group_check=True).then_inc(hot_mm, 1)

            def turn_gathered(t, p, n, bank_=xt_ps):
                pe.wait_ge(g_ld[p], (n + 1) * 16)
                if bank_ is xt_ps:
                    after(pe, xt_sb, ROWS_DVE + t)
                turn_rows(xg[:, p, :], bank_)

            logits(BATCHES - 1)
            for u in range(UPS):
                if u == 1:
                    shared_up(BATCHES - 1, u, ks=range(0, KC // 2))
                    ranks()
                    shared_up(BATCHES - 1, u, ks=range(KC // 2, KC))
                elif u == UPS - 2:
                    shared_up(BATCHES - 1, u, ks=range(0, KC // 2))
                    slots(0)
                    shared_up(BATCHES - 1, u, ks=range(KC // 2, KC))
                else:
                    shared_up(BATCHES - 1, u)
                if u > UPS - 3:
                    slots(2 * (u - UPS + 2) + 1)
                    slots(2 * (u - UPS + 2) + 2)
            shared_down(BATCHES - 1, 0, range(0, UPS // 2))
            slots(SLOTS_STEPS - 3)
            shared_down(BATCHES - 1, 0, range(UPS // 2, UPS))
            slots(SLOTS_STEPS - 2)
            slots(SLOTS_STEPS - 1)
            for i in range(1, TPB - 1):
                shared_down(BATCHES - 1, i)
            after(pe, lg_sb, BATCHES)
            turn_gathered(0, 0, 0)
            turn_gathered(1, 1, 0, xt_second)
            shared_down(BATCHES - 1, TPB - 1)

            for s in w_lo:
                after(pe, s, ITEMS * (CHUNKS // RING))
            after(pe, w_hi, ITEMS * CHUNKS)
            def up(t, p, item, ks):
                if 0 in ks:
                    after(pe, hid_sb, Q0 + t - 1)
                    after(pe, xt_sb, ROWS_DVE + t + 1)
                for k in ks:
                    at = k * 2 * H
                    for part in range(2):
                        lhs = x_t[:, p, part * KC + k, :]
                        for half in range(2 - part):
                            begin, end = (k, part, half) == (0, 0, 0), (k, part) == (KC - 1, 1)
                            pe.matmul(pg[p][:, 0:H], lhs, w[:, item, half, at:at + H], start=begin, stop=end)
                            mm = pe.matmul(pu[p][:, 0:H], lhs, w[:, item, half, at + H:at + 2 * H], start=begin, stop=end)
                if KC - 1 in ks:
                    mm.then_inc(up_mm, 1)

            def turn_hidden(t, p):
                after(pe, hhi_sb, Q0 + t + 1)
                after(pe, hlo_sb, Q0 + t + 1)
                after(pe, ht_sb, t - 1)
                for n in range(2 * JC):
                    mm = pe.transpose(hid_banks[p][:, n, :], hid16[:, p, n // JC, n % JC * P:(n % JC + 1) * P], ident16[:])
                mm.then_inc(hid_mm, 1)

            def down(t, p, item):
                after(pe, ht_sb, t + 1)
                after(pe, y_sb, TILES + t)
                for j in range(JC):
                    at = UP_W + j * C
                    for part in range(2):
                        for half in range(2 - part):
                            mm = pe.matmul(py[:, :], hid_t[:, p, part * JC + j, :], w[:, item, half, at:at + C],
                                           start=(j, part, half) == (0, 0, 0), stop=(j, part) == (JC - 1, 1))
                mm.then_inc(down_mm, 1)

            def item_of(t):
                return pe.value_load(tile_e[0:1, ds(t, 1)], min_val=HALVES, max_val=ITEMS - 1)

            def turn_and_up(t, p, item):
                up(t, p, ds(item, 1), range(0, KC // 2))
                turn_hidden(t - 1, 1 - p)
                up(t, p, ds(item, 1), range(KC // 2, KC))

            pe.wait_ge(table_ok, 1)
            after(pe, y_sb, TILES - 1)
            up(0, 0, ds(item_of(0), 1), range(KC))
            pe.wait_ge(hid_pad, 1)
            turn_gathered(2, 0, 1)
            turn_and_up(1, 1, item_of(1))

            def expert_steps(t0, n0, steps):
                down_item = item_of(t0)
                for k in range(steps):
                    if k:
                        up_item = item_of(t0 + k + 2)
                    down(t0 + k, k % 2, ds(down_item, 1))
                    if k == 0:
                        next_item, up_item = item_of(t0 + 1), item_of(t0 + 2)
                    turn_gathered(t0 + k + 3, 1 - k % 2, n0 + (k + 3) // 2)
                    turn_and_up(t0 + k + 2, k % 2, up_item)
                    down_item, next_item = next_item, up_item

            STEP = 6
            loops = (SLOT_TILES - 2) // STEP
            with pe.Fori(0, loops) as i:
                expert_steps(i * STEP, i * (STEP // 2), STEP)
            t = loops * STEP
            expert_steps(t, t // 2, SLOT_TILES - 2 - t)
            t = SLOT_TILES - 2
            down(t, t % 2, ds(item_of(t), 1))
            turn_gathered(t + 3, (t + 3) % 2, (t + 3) // 2)
            turn_hidden(t + 1, (t + 1) % 2)
            down(t + 1, (t + 1) % 2, ds(item_of(t + 1), 1))

        @block.vector
        def _(dve):
            dve.wait_ge(ready, 1)
            o = Order(dve, dve_ch)

            dve.wait_ge(cst_act, 2)
            o.then(dve.tensor_scalar(cst[:, 5:6], cst[:, 2:3], 0.5, 0.5, ALU.mult, ALU.add))
            o.mark(dve.tensor_scalar(cst[:, 6:7], cst[:, 5:6], -1.0, 1.0, ALU.mult, ALU.add))
            o.then(dve.tensor_tensor(cst[:, 7:8], cst[:, 5:6], cst[:, 0:1], ALU.mult))
            o.mark(dve.tensor_tensor(cst[:, 3:4], cst[:, 6:7], cst[:, 0:1], ALU.mult))
            o.mark(dve.tensor_scalar(cst[:, 4:5], cst[:, 7:8], 0.25, None, ALU.mult))
            o.then(dve.tensor_scalar(cst[:, 8:9], cst[:, 1:2], DOWN_UNSCALE, None, ALU.mult))
            dve.wait_ge(gw_hi, 1)
            dve.scalar_tensor_tensor(out=gw[:, :, 1, :], in0=gw_f, scalar=W_SCALE, in1=gw[:, :, 0, :],
                                     op0=ALU.mult, op1=ALU.subtract).then_inc(gw_ok, 1)
            dve.sem_inc(cst_ok, 1)
            dve.wait_ge(const_ok, 2)
            unscaled_tanh_ffn = cst[:, 8:9]

            def low_piece(item, n):
                after(dve, w_hi, item * CHUNKS + n + 1)
                dve.scalar_tensor_tensor(out=w[:, item, 1, n * CHUNK_W:(n + 1) * CHUNK_W], in0=stage[:, n % RING, :],
                                         scalar=W_SCALE, in1=w[:, item, 0, n * CHUNK_W:(n + 1) * CHUNK_W],
                                         op0=ALU.mult, op1=ALU.subtract).then_inc(w_lo[n % RING], 1)

            def statistics(s):
                o.wait()
                for i in range(TPB):
                    o.mark(dve.bn_aggr(mv[:, s, i, :], bn6[:, s, i, :]))
                o.wait()

            def x_stats(b):
                after(dve, x_ld, (b + 1) * 16)
                for i in range(TPB):
                    o.mark(dve.bn_stats(bn6[:, 1, i, :], xb[:, i, :]))
                statistics(1)
                dve.sem_inc(x_stats_ok, 1)

            def score_stats(b, tiles):
                for i in tiles:
                    after(dve, sim_sb, b * TPB + i + 1)
                    o.mark(dve.bn_stats(bn6[:, 0, i, :], sim[:, i, :]))
                if TPB - 1 in tiles:
                    statistics(0)
                    dve.sem_inc(stats_ok, 1)

            def interpolate(b, n):
                half = TPB // 2
                if n == 0:
                    after(dve, guess_ok, b + 1)
                dve.sem_inc(cur_ok, 1)
                for i in range(half):
                    o.mark(dve.tensor_scalar(junk[:, i, :], sim[:, i, :], cur[:, 0, i:i + 1], 0.0, ALU.is_ge, ALU.add,
                                             accum_out=cur[:, 1, i:i + 1]))
                after(dve, cnt_sb, (b * ROUNDS + n + 1) * half)
                o.then(dve.tensor_scalar(cur[:, 1, half:], acc[:], -0.5, SEQ / 2.0, ALU.mult, ALU.add))
                o.mark(dve.tensor_scalar(above[:], cur[:, 1, :], float(KEEP), None, ALU.is_ge))
                o.then(dve.tensor_scalar(below[:], cur[:, 1, :], float(KEEP), None, ALU.is_lt))
                o.mark(dve.copy_predicated(lo, above[:].unsqueeze(1).to_broadcast([P, 2, TPB]), cur))
                o.then(dve.copy_predicated(hi, below[:].unsqueeze(1).to_broadcast([P, 2, TPB]), cur))
                if n < ROUNDS - 1:
                    gap, frac, width = tmp4[:, 0, :], tmp4[:, 1, :], tmp4[:, 2, :]
                    o.mark(dve.tensor_tensor(gap, lo[:, 1, :], hi[:, 1, :], ALU.subtract))
                    o.then(dve.tensor_tensor(width, hi[:, 0, :], lo[:, 0, :], ALU.subtract))
                    o.then(dve.reciprocal(gap, gap))
                    o.then(dve.scalar_tensor_tensor(out=frac, in0=lo[:, 1, :], scalar=KEEP - 4.0, in1=gap,
                                                    op0=ALU.subtract, op1=ALU.mult))
                    o.then(dve.scalar_tensor_tensor(out=frac, in0=frac, scalar=0.98, in1=width, op0=ALU.min, op1=ALU.mult))
                    o.then(dve.tensor_tensor(cur[:, 0, :], frac, lo[:, 0, :], ALU.add))

            rank, miss = tmp4[:, 3, :], tmp4[:, 4, :]

            def thresholds(two):
                o.wait()
                made = [o.mark(dve.tensor_scalar(masked[:, i % 2, :], sim[:, i, :], hi[:, 0, i:i + 1], 0.0, ALU.is_ge, ALU.add,
                                                 accum_out=hi[:, 1, i:i + 1])) for i in two]
                for n, i in enumerate(two):
                    o.wait(made[n])
                    made[n] = o.mark(dve.scalar_tensor_tensor(out=masked[:, i % 2, :], in0=masked[:, i % 2, :], scalar=-BIG,
                                                              in1=sim[:, i, :], op0=ALU.mult, op1=ALU.add))
                o.mark(dve.tensor_scalar(rank[:, two[0]:two[1] + 1], hi[:, 1, two[0]:two[1] + 1], -1.0, KEEP - 1.0, ALU.mult, ALU.add))
                for n, i in enumerate(two):
                    o.wait(made[n])
                    made[n] = o.mark(dve.max(top8[:, i, :], masked[:, i % 2, :]))
                for n, i in enumerate(two):
                    o.wait(made[n])
                    o.mark(dve.scalar_tensor_tensor(out=pick8[:, i, :], in0=iota_col[:, 0:8], scalar=rank[:, i:i + 1],
                                                    in1=top8[:, i, :], op0=ALU.is_equal, op1=ALU.mult,
                                                    accum_out=thr[:, i:i + 1]))

            def count_missed():
                o.wait()
                o.then(dve.tensor_scalar(miss, rank, 0.0, None, ALU.is_lt))
                o.then(dve.scalar_tensor_tensor(out=miss, in0=rank, scalar=7.5, in1=miss, op0=ALU.is_gt, op1=ALU.add,
                                                accum_out=missed[:]))
                dve.sem_inc(miss_ok, 1)

            def masks(b, piece=None):
                after(dve, miss_mm, b + 1)
                o.then(dve.tensor_copy(missed_i[:], pa[0][0:1, 0:1]))
                if piece is not None:
                    low_piece(*piece)
                any_missed = dve.value_load(missed_i[0:1, 0:1], min_val=0, max_val=2 * P * TPB)
                with dve.If(any_missed > 0):
                    f = Order(dve, fb_ch)
                    f.clear()
                    for i in range(TPB):
                        f.then(dve.tensor_copy(masked[:, 0, :], sim[:, i, :]))
                        with dve.Fori(0, (KEEP - 1) // 8):
                            dve.sem_clear(fb_ch)
                            dve.max(top8[:, i, :], masked[:, 0, :]).then_inc(fb_ch, 1)
                            dve.wait_ge(fb_ch, 1)
                            dve.match_replace(out=masked[:, 0, :], in_to_replace=top8[:, i, :], in_values=masked[:, 0, :],
                                              imm_value=-BIG).then_inc(fb_ch, 1)
                            dve.wait_ge(fb_ch, 2)
                        f.n = 0
                        dve.sem_clear(fb_ch)
                        f.then(dve.max(top8[:, i, :], masked[:, 0, :]))
                        f.then(dve.tensor_copy(thr[:, i:i + 1], top8[:, i, (KEEP - 1) % 8:(KEEP - 1) % 8 + 1]))
                after(dve, sig_sb, (b + 1) * TPB)
                for i in range(TPB):
                    dve.scalar_tensor_tensor(out=att[:, i, :], in0=sim[:, i, :], scalar=thr[:, i:i + 1], in1=att[:, i, :],
                                             op0=ALU.is_ge, op1=ALU.mult).then_inc(a_made, 1)

            def attended(b, more, shared):
                def x1_stats(i):
                    after(dve, x1_made, b * TPB + i + 1)
                    o.mark(dve.bn_stats(bn6[:, 2, i, :], xb[:, i, :]))

                if shared is not None:
                    shared_rows(shared, 0)
                for i in range(TPB):
                    after(dve, xa_made, b * TPB + i + 1)
                    after(dve, at_mm, b * TPB + i + 1)
                    dve.tensor_tensor(xb[:, i, :], turn_banks[i][:, :], xb[:, i, :], ALU.add).then_inc(x1_made, 1)
                    if i > 0:
                        x1_stats(i - 1)
                    if i == 1 and shared is not None and not more:
                        shared_rows(shared, 1)
                x1_stats(TPB - 1)
                statistics(2)
                dve.sem_inc(ln_stats, 1)
                if shared is None:
                    low_piece(HALVES, 3)
                if shared is not None:
                    if more:
                        shared_rows(shared, 1)
                    shared_rows(shared, 2)
                after(dve, up_mm, b * UPS)
                for i in range(TPB):
                    after(dve, xn_hi, b * TPB + i + 1)
                    dve.tensor_tensor(xnr[:, i, C:2 * C], xn[:, i % 2, :], xnr[:, i, 0:C], ALU.subtract).then_inc(xn_lo, 1)
                    if 0 < i < TPB - 1:
                        rows_turned(b, i - 1)
                if more:
                    score_stats(b + 1, (0, 1))
                rows_turned(b, TPB - 2)
                if shared is not None:
                    shared_rows(shared, 3)
                if more:
                    score_stats(b + 1, (2, 3))
                o.clear()

            def rows_turned(b, i):
                after(dve, xt_mm, b * TPB + i + 1)
                dve.tensor_copy(x_tb[:, :, i * P:(i + 1) * P], xt_banks[i % 2]).then_inc(xt_sb, 1)

            def shared_hidden(b, u):
                q, m = b * UPS + u, PIECES[u][2]
                after(dve, sil_sb, q + 1)
                after(dve, up_mm, q + 1)
                dve.scalar_tensor_tensor(out=hb[0:m, u % 2, :], in0=pu[u % 2][0:m, :], scalar=UP_UNSCALE * H_SCALE,
                                         in1=hb[0:m, u % 2, :], op0=ALU.mult, op1=ALU.mult).then_inc(hid_sb, 1)

            def shared_rows(b, i):
                after(dve, down_mm, b * TPB + i + 1)
                after(dve, x1_ld[i % 2], (b * (TPB // 2) + i // 2 + 1) * 16)
                dve.scalar_tensor_tensor(out=rows[:, i % 2, :], in0=down_bank(b, i)[:, :], scalar=unscaled_tanh_ffn,
                                         in1=rows[:, i % 2, :], op0=ALU.mult, op1=ALU.add).then_inc(y_sb, 1)

            o.clear()
            score_stats(0, range(TPB))
            x_stats(0)
            for n in range(ROUNDS):
                interpolate(0, n)
            low_piece(0, 3)
            thresholds((0, 1))
            low_piece(0, 7)
            thresholds((2, 3))
            count_missed()
            masks(0, (1, 3))
            low_piece(1, 7)
            attended(0, True, None)

            def together(b, more):
                x_stats(b + 1)
                interpolate(b + 1, 0)
                for u in range(UPS):
                    shared_hidden(b, u)
                    if u + 1 < ROUNDS:
                        interpolate(b + 1, u + 1)
                    if u + 2 == ROUNDS:
                        thresholds((0, 1))
                        thresholds((2, 3))
                    if u + 1 == ROUNDS:
                        count_missed()
                masks(b + 1)
                attended(b + 1, more, b)

            with dve.Fori(0, BATCHES - 2) as b:
                together(b, True)
            together(BATCHES - 2, False)


            def bc(col):
                return col.unsqueeze(2).to_broadcast([P, TILES, EXPERTS])

            def over_tiles(row):
                return row.unsqueeze(1).to_broadcast([P, TILES, EXPERTS])

            score, cand, sel, hot1, hot2 = r[1][:], r[3][:], r[2][:], r[4][:], r[5][:]
            z, total, gate = r[0][:], r[1][:], slot_f[:, 0, :, :]

            def best(hot, col):
                o.then(dve.tensor_reduce(rc[:, col, :], cand, AX.X, ALU.max))
                o.then(dve.tensor_tensor(hot, cand, bc(rc[:, col, :]), ALU.is_equal))
                o.then(dve.tensor_tensor(hot, hot, over_tiles(first[:]), ALU.mult))
                o.then(dve.tensor_reduce(rc[:, col, :], hot, AX.X, ALU.max))
                o.then(dve.tensor_tensor(hot, over_tiles(first[:]), bc(rc[:, col, :]), ALU.is_equal))

            def sum_logits():
                after(dve, lg_sb, BATCHES)
                o.then(dve.tensor_tensor(r[0][:], lg[:, :, 0, :], lg[:, :, 1, :], ALU.add))
                dve.sem_inc(z_ok, 1)

            def choose():
                dve.wait_ge(exp_ok, 1)
                o.then(dve.tensor_scalar(score, score, 1.0, None, ALU.add))
                o.then(dve.reciprocal(score, score))
                o.then(dve.tensor_tensor(cand, score, over_tiles(bias_b[:]), ALU.add))

                best(hot1, 1)
                o.then(dve.scalar_tensor_tensor(out=cand, in0=hot1, scalar=-BIG, in1=cand, op0=ALU.mult, op1=ALU.add))
                best(hot2, 2)
                dve.tensor_tensor(sel, hot1, hot2, ALU.add).then_inc(route_ok, 1)
                for k, hot in enumerate((hot1, hot2)):
                    o.then(dve.tensor_tensor(z, score, hot, ALU.mult))
                    o.then(dve.tensor_reduce(rc[:, 3 + k, :], z, AX.X, ALU.add))
                o.then(dve.tensor_tensor(rc[:, 5, :], rc[:, 3, :], rc[:, 4, :], ALU.add))
                o.then(dve.reciprocal(rc[:, 5, :], rc[:, 5, :]))
                for k in range(TOPK):
                    o.then(dve.tensor_tensor(gate[:, k, :], rc[:, 3 + k, :], rc[:, 5, :], ALU.mult))

            def count_tokens():
                dve.wait_ge(route_mm, 2)
                o.then(dve.tensor_copy(total, pa[1][:, 0:P].rearrange("p (t e) -> p t e", t=TILES)))
                o.then(dve.tensor_copy(cand, total))
                a, c2 = cand, z
                step = 1
                while step < TILES:
                    o.mark(dve.tensor_copy(c2[:, 0:step, :], a[:, 0:step, :]))
                    o.then(dve.tensor_tensor(c2[:, step:, :], a[:, step:, :], a[:, :TILES - step, :], ALU.add))
                    a, c2 = c2, a
                    step *= 2
                o.then(dve.tensor_scalar(re8[:, 0, :], a[:, TILES - 1, :], float(P - 1), None, ALU.add))
                o.then(dve.tensor_copy(ri8[:], re8[:, 0, :]))
                o.then(dve.tensor_scalar(ri8[:], ri8[:], P.bit_length() - 1, None, ALU.logical_shift_right))
                o.then(dve.tensor_copy(re8[:, 0, :], ri8[:]))
                o.then(dve.tensor_copy(re8[:, 3, :], re8[:, 0, :]))
                ea, eb = re8[:, 3, :], re8[:, 1, :]
                step = 1
                while step < EXPERTS:
                    o.mark(dve.tensor_copy(eb[:, 0:step], ea[:, 0:step]))
                    o.then(dve.tensor_tensor(eb[:, step:], ea[:, step:], ea[:, :EXPERTS - step], ALU.add))
                    ea, eb = eb, ea
                    step *= 2
                ends = ea
                o.then(dve.tensor_tensor(re8[:, 2, :], ends, re8[:, 0, :], ALU.subtract))
                o.then(dve.tensor_scalar(re8[:, 2, :], re8[:, 2, :], float(P), None, ALU.mult))
                return a, ends

            def place(a):
                o.then(dve.tensor_tensor(a, a, total, ALU.subtract))
                o.then(dve.tensor_tensor(a, a, pa[0][:, 0:P].rearrange("p (t e) -> p t e", t=TILES), ALU.add))
                o.then(dve.tensor_tensor(a, a, over_tiles(re8[:, 2, :]), ALU.add))
                for k, hot in enumerate((hot1, hot2)):
                    o.then(dve.tensor_tensor(total, a, hot, ALU.mult))
                    o.then(dve.tensor_reduce(slot_f[:, 1, k, :], total, AX.X, ALU.add))
                o.then(dve.tensor_copy(slot_i[:, 0, :, :], slot_f[:, 1, :, :]))
                o.mark(dve.tensor_scalar(slot_i[:, 1, :, :], slot_i[:, 0, :, :], P.bit_length() - 1, None, ALU.logical_shift_right))
                o.then(dve.tensor_scalar(slot_i[:, 2, :, :], slot_i[:, 0, :, :], P - 1, None, ALU.bitwise_and))
                o.mark(dve.tensor_copy(slot_f[:, 1, :, :], slot_i[:, 1, :, :]))
                o.then(dve.tensor_copy(slot_f[:, 2, :, :], slot_i[:, 2, :, :]))
                o.then(dve.tensor_scalar(rc[:, 6, :], iota_tile[:, 0:TILES], float(P), iota_p[:, 0:1], ALU.mult, ALU.add))
                for k in range(TOPK):
                    o.then(dve.scalar_tensor_tensor(out=slot_f[:, 3, k, :], in0=rc[:, 6, :], scalar=-float(TOKENS),
                                                    in1=slot_f[:, 2, k, :], op0=ALU.add, op1=ALU.subtract))

            def tile_experts(ends):
                tcount = rc[0:1, 0:3, :].rearrange("p a b -> p (a b)")[:, 0:SLOT_COLS]
                o.then(dve.tensor_scalar(tcount, iota_col[0:1, 0:SLOT_COLS], 0.0, float(HALVES), ALU.mult, ALU.add))
                for n in range(EXPERTS - 1):
                    o.then(dve.scalar_tensor_tensor(out=tcount, in0=iota_col[0:1, 0:SLOT_COLS], scalar=ends[0:1, n:n + 1], in1=tcount,
                                                    op0=ALU.is_ge, op1=ALU.add))
                o.then(dve.tensor_copy(tile_e[:], tcount))
                dve.sem_inc(route_ok, 1)

            def hot_slots(step):
                k, g, made = step * SLOTS_STEP // TILES, step * SLOTS_STEP % TILES, 3 * step
                hot_col, hot_val = hot_cols[step % 2], hot_vals[step % 2]

                def per_slot(col, width):
                    return col[:, g:g + SLOTS_STEP].unsqueeze(2).to_broadcast([P, SLOTS_STEP, width])

                def over(row, width):
                    return row.unsqueeze(1).to_broadcast([P, SLOTS_STEP, width])

                if step >= 2:
                    dve.wait_ge(hot_mm, (step - 1) * SLOTS_STEP)
                dve.tensor_tensor(hot_val[:, :, 0, :], over(iota_tile, SLOT_COLS), per_slot(slot_f[:, 1, k, :], SLOT_COLS),
                                  ALU.is_equal).then_inc(hot_ok, 1)
                dve.tensor_tensor(hot_col, over(iota_col[:], P), per_slot(slot_f[:, 2, k, :], P), ALU.is_equal).then_inc(hot_ok, 1)
                dve.wait_ge(hot_ok, made + 1)
                o.then(dve.tensor_tensor(hot_val[:, :, 1, :], hot_val[:, :, 0, :], per_slot(gate[:, k, :], SLOT_COLS), ALU.mult))
                dve.tensor_tensor(hot_val[:, :, 0, :], hot_val[:, :, 0, :], per_slot(slot_f[:, 3, k, :], SLOT_COLS),
                                  ALU.mult).then_inc(hot_ok, 1)

            def table():
                dve.wait_ge(hot_mm, TOPK * TILES)
                o.mark(dve.tensor_scalar(idx[:], pa[0][:, 0:SLOT_COLS], iota_p[:, 0:1], float(TOKENS), ALU.add, ALU.add))
                o.then(dve.tensor_scalar(w_slot[:], pa[0][:, SLOT_COLS:2 * SLOT_COLS], unscaled_tanh_ffn, None, ALU.mult))
                dve.sem_inc(table_ok, 1)

            def low_pieces(u):
                for n in range(u * PER_STEP, (u + 1) * PER_STEP):
                    if by_dve(EARLY - 1 + n // CHUNKS, n % CHUNKS):
                        low_piece(EARLY - 1 + n // CHUNKS, n % CHUNKS)

            sum_logits()
            for u in range(UPS):
                if u == 0:
                    choose()
                if u == 1:
                    counted, ends = count_tokens()
                if u == 2:
                    place(counted)
                if u == 3:
                    hot_slots(0)
                    hot_slots(1)
                if u == 4:
                    hot_slots(2)
                    tile_experts(ends)
                if u == 5:
                    hot_slots(3)
                    hot_slots(4)
                if u:
                    low_pieces(u - 1)
                shared_hidden(BATCHES - 1, u)
            for step in range(5, SLOTS_STEPS):
                hot_slots(step)
            low_pieces(UPS - 1)
            table()
            for i in range(TPB - 1):
                shared_rows(BATCHES - 1, i)
                for n in ((1, 3), (5,), (7,))[i]:
                    low_piece(ITEMS - 1, n)

            def hidden(t, p):
                after(dve, up_mm, Q0 + t + 1)
                after(dve, sil_sb, Q0 + t + 1)
                dve.scalar_tensor_tensor(out=hid[:, p, :], in0=pu[p][:, 0:H], scalar=UP_UNSCALE * H_SCALE,
                                         in1=hid[:, p, :], op0=ALU.mult, op1=ALU.mult).then_inc(hid_sb, 1)

            def hidden_low(t, p):
                after(dve, hhi_sb, Q0 + t + 1)
                after(dve, hid_mm, t - 1)
                dve.tensor_tensor(hid16[:, p, 1, 0:H], hid[:, p, :], hid16[:, p, 0, 0:H], ALU.subtract).then_inc(hlo_sb, 1)

            def hidden_turned(t, p):
                after(dve, hid_mm, t + 1)
                after(dve, down_mm, TILES + t - 1)
                dve.tensor_copy(hid_t[:, p, :, :], hid_banks[p]).then_inc(ht_sb, 1)

            def gathered_turned(t, p, uses, bank_=xt_ps):
                after(dve, xt_mm, TILES + t + 1)
                after(dve, up_mm, Q0 + uses)
                dve.tensor_copy(x_t[:, p, :, :], bank_).then_inc(xt_sb, 1)

            after(dve, down_mm, TILES)
            gathered_turned(0, 0, 0)
            gathered_turned(1, 1, 0, xt_second)
            shared_rows(BATCHES - 1, TPB - 1)

            def hidden_rows(t, p):
                hidden(t, p)
                hidden_low(t, p)
                gathered_turned(t + 2, p, t + 1)
                hidden_turned(t, p)

            hidden_rows(0, 0)
            with dve.Fori(0, SLOT_TILES // 2) as i:
                for k in range(2):
                    hidden_rows(i * 2 + k + 1, 1 - k)


def kernel(x, ctx_512, g_xattn, g_ffn, L0_xattn_Wq, L0_xattn_Wk, L0_xattn_gamma_raw, L0_ffn_gate_w, L0_ffn_gate_bias,
           L0_ffn_shared_gw, L0_ffn_shared_dw, L0_ffn_up_w, L0_ffn_down_w):
    import concourse.bacc as bacc
    from concourse import mybir
    from concourse.bass_utils import run_bass_kernel_spmd

    def chunks(m):
        m = np.asarray(m)
        return m.reshape(-1, P, m.shape[1]).transpose(1, 0, 2).reshape(P, -1)

    def item(gate, value, down):
        up = np.concatenate([np.asarray(gate).T, np.asarray(value).T], axis=1)
        dn = np.zeros((HP, C), np.float32)
        dn[:H] = np.asarray(down).T
        return np.concatenate([chunks(up), chunks(dn)], axis=1)

    gw, dw = np.asarray(L0_ffn_shared_gw), np.asarray(L0_ffn_shared_dw)
    up_w, down_w = np.asarray(L0_ffn_up_w), np.asarray(L0_ffn_down_w)
    S = HALVES * H
    items = [item(gw[S + h * H:S + (h + 1) * H], gw[h * H:(h + 1) * H], dw[:, h * H:(h + 1) * H]) for h in range(HALVES)]
    items += [item(up_w[e, :H], up_w[e, H:], down_w[e]) for e in range(EXPERTS)]
    arrays = {
        "x": np.asarray(x).reshape(TOKENS, C),
        "ctx_t": np.asarray(ctx_512).reshape(TOKENS, D).T,
        "wq_t": np.asarray(L0_xattn_Wq).T,
        "wk_t": np.asarray(L0_xattn_Wk).T,
        "gates": np.concatenate([np.asarray(g_xattn).reshape(1), np.asarray(g_ffn).reshape(1),
                                 np.asarray(L0_xattn_gamma_raw).reshape(1)]),
        "gate_wt": np.asarray(L0_ffn_gate_w).T.reshape(KC, P, EXPERTS).transpose(1, 0, 2),
        "gate_bias": np.asarray(L0_ffn_gate_bias),
        "weights": np.stack(items),
    }
    nc = bacc.Bacc("TRN2", target_bir_lowering=False, num_devices=1)
    named, args = {}, []
    for name, a in arrays.items():
        a = np.ascontiguousarray(a)
        named[f"in_{name}"] = a
        args.append(nc.dram_tensor(f"in_{name}", a.shape, mybir.dt.from_np(a.dtype), kind="ExternalInput").ap())
    out = nc.dram_tensor("out", (TOKENS + PAD_ROWS, C), mybir.dt.float32, kind="ExternalOutput").ap()
    xn_rows = nc.dram_tensor("xn_rows", (TOKENS + PAD_ROWS, 2 * C), mybir.dt.float16, kind="Internal").ap()
    build(nc, *args, out, xn_rows)
    res = run_bass_kernel_spmd(nc, [named], core_ids=[0])
    return res.results[0]["out"][:TOKENS].reshape(BATCHES, SEQ, C)
```
